# Optimizing a Trainium2 kernel written in Bass

```python
import numpy as np
import jax
import jax.numpy as jnp

def _softmax(x, axis=-1):
    return jax.nn.softmax(x, axis=axis)

def _gelu(x):
    return jax.nn.gelu(x, approximate=True)

def _silu(x):
    return jax.nn.silu(x)

def _sigmoid(x):
    return jax.nn.sigmoid(x)

def _layernorm(x, axis=-1, eps=1e-05):
    m = jnp.mean(x, axis=axis, keepdims=True)
    v = jnp.var(x, axis=axis, keepdims=True)
    return (x - m) / jnp.sqrt(v + eps)

def _scatter_add(tgt, idx, src, axis=0):
    return tgt.at[idx].add(src)

def _segment_sum(src, seg, n):
    return jax.ops.segment_sum(src, seg, n)
kernel_name = 'mk_seq_postln_d2_jaxref_r8_07a1cf'

def setup_inputs(seed: int=0):
    np.random.seed(seed)
    _w = jnp.asarray

    def _L0_attn_setup():
        import jax, jax.numpy as jnp
        import numpy as np
        B, S, D, H = (4, 256, 128, 16)
        DH = D // H
        key = jax.random.key(seed)
        ks = jax.random.split(key, 5)
        std = 1.0 / np.sqrt(D)
        return {'x': jax.random.normal(ks[0], (B, S, D), dtype=jnp.float32), 'mask': jnp.ones((S, S), dtype=bool), 'Wq': jax.random.normal(ks[1], (D, D), dtype=jnp.float32) * std, 'Wk': jax.random.normal(ks[2], (D, D), dtype=jnp.float32) * std, 'Wv': jax.random.normal(ks[3], (D, D), dtype=jnp.float32) * std, 'Wout': jax.random.normal(ks[4], (D, D), dtype=jnp.float32) * std}
    _L0_attn_in = _L0_attn_setup()

    def _L0_ffn_setup():
        import jax, jax.numpy as jnp
        import numpy as np
        DIM = 128
        DEPTH = 2
        HEADS = 8
        DIM_HEAD = 64
        WINDOW = 64
        INNER = HEADS * DIM_HEAD
        HID = int(DIM * 4 * 2 / 3)
        B, N = (2, 1024)
        QK_SCALE = 8.0

        def shift_token(t):
            t1, t2 = jnp.split(t, 2, axis=-1)
            t2 = jnp.pad(t2, ((0, 0), (1, 0), (0, 0)))[:, :-1]
            return jnp.concatenate([t1, t2], axis=-1)

        def l2norm(t):
            return t / jnp.clip(jnp.linalg.norm(t, axis=-1, keepdims=True), 1e-12)

        def rotate_half(x):
            x1, x2 = jnp.split(x, 2, axis=-1)
            return jnp.concatenate([-x2, x1], axis=-1)

        def rotary_xpos(q, k):
            n = q.shape[-2]
            half_idx = jnp.arange(0, DIM_HEAD, 2, dtype=jnp.float32)
            inv_freq = 1.0 / 10000.0 ** (half_idx / DIM_HEAD)
            t = jnp.arange(n, dtype=jnp.float32)
            freqs = t[:, None] * inv_freq[None, :]
            freqs = jnp.concatenate([freqs, freqs], axis=-1)
            base = (half_idx + 0.4 * DIM_HEAD) / (1.4 * DIM_HEAD)
            power = (t - n // 2) / float(WINDOW // 2)
            scale = base[None, :] ** power[:, None]
            scale = jnp.concatenate([scale, scale], axis=-1)
            cos, sin = (jnp.cos(freqs), jnp.sin(freqs))
            q = q * cos * scale + rotate_half(q) * sin * scale
            k = k * cos / scale + rotate_half(k) * sin / scale
            return (q, k)

        def local_attention(q, k, v):
            b, h, n, d = q.shape
            w = n // WINDOW
            bq = q.reshape(b, h, w, WINDOW, d) * QK_SCALE
            bk = k.reshape(b, h, w, WINDOW, d)
            bv = v.reshape(b, h, w, WINDOW, d)

            def look_around(t):
                p = jnp.pad(t, ((0, 0), (0, 0), (1, 0), (0, 0), (0, 0)))
                return jnp.concatenate([p[:, :, :w], p[:, :, 1:]], axis=3)
            bk, bv = (look_around(bk), look_around(bv))
            bt = jnp.arange(n).reshape(w, WINDOW)
            btp = jnp.pad(bt, ((1, 0), (0, 0)), constant_values=-1)
            btk = jnp.concatenate([btp[:w], btp[1:]], axis=1)
            sim = jnp.einsum('bhwid,bhwjd->bhwij', bq, bk)
            i = bt[:, :, None]
            j = btk[:, None, :]
            mask = (i < j) | (i > j + WINDOW) | (j == -1)
            sim = jnp.where(mask, -jnp.finfo(sim.dtype).max, sim)
            attn = jax.nn.softmax(sim, axis=-1)
            out = jnp.einsum('bhwij,bhwjd->bhwid', attn, bv)
            return out.reshape(b, h, n, d)

        def _layer(x, wqkv, qs, ksc, wo, lg, lb, w1, b1, w2, b2):
            b, n, _ = x.shape
            h = shift_token(x)
            qkv = h @ wqkv
            q, k, v = jnp.split(qkv, 3, axis=-1)
            to_heads = lambda t: t.reshape(b, n, HEADS, DIM_HEAD).transpose(0, 2, 1, 3)
            q, k, v = (to_heads(q), to_heads(k), to_heads(v))
            q = l2norm(q) * qs
            k = l2norm(k) * ksc
            q, k = rotary_xpos(q, k)
            o = local_attention(q, k, v)
            o = o.transpose(0, 2, 1, 3).reshape(b, n, INNER)
            x = x + o @ wo
            h = shift_token(x)
            mu = h.mean(-1, keepdims=True)
            var = h.var(-1, keepdims=True)
            h = (h - mu) / jnp.sqrt(var + 1e-05) * lg + lb
            h = h @ w1 + b1
            a, g = jnp.split(h, 2, axis=-1)
            h = a * jax.nn.gelu(g, approximate=False)
            x = x + h @ w2 + b2
            return x
        key = jax.random.key(seed)
        ks = jax.random.split(key, 6)
        return {'x': jax.random.normal(ks[0], (B, N, DIM), jnp.float32), 'wqkv': jax.random.normal(ks[1], (DEPTH, DIM, 3 * INNER), jnp.float32) * 0.02, 'q_scale': jnp.ones((DEPTH, DIM_HEAD), jnp.float32), 'k_scale': jnp.ones((DEPTH, DIM_HEAD), jnp.float32), 'wo': jax.random.normal(ks[2], (DEPTH, INNER, DIM), jnp.float32) * 0.02, 'ln_g': jnp.ones((DEPTH, DIM), jnp.float32), 'ln_b': jnp.zeros((DEPTH, DIM), jnp.float32), 'w1': jax.random.normal(ks[3], (DEPTH, DIM, 2 * HID), jnp.float32) * 0.02, 'b1': jnp.zeros((DEPTH, 2 * HID), jnp.float32), 'w2': jax.random.normal(ks[4], (DEPTH, HID, DIM), jnp.float32) * 0.02, 'b2': jnp.zeros((DEPTH, DIM), jnp.float32)}
    _L0_ffn_in = _L0_ffn_setup()

    def _L1_attn_setup():
        import jax, jax.numpy as jnp
        import numpy as np
        D = 128
        HS = 128
        NKV = 2

        def apply_rope(x):
            d = x.shape[-1]
            T = x.shape[-2]
            positions = jnp.arange(0, d, 2, dtype=jnp.float32)
            theta = 10000.0 ** (-2.0 * positions / d)
            angles = jnp.arange(T, dtype=jnp.float32)[:, None] * theta[None, :]
            cos, sin = (jnp.cos(angles), jnp.sin(angles))
            xr = x.reshape(x.shape[:-1] + (d // 2, 2))
            out = jnp.stack([xr[..., 0] * cos - xr[..., 1] * sin, xr[..., 1] * cos + xr[..., 0] * sin], axis=-1)
            return out.reshape(x.shape)
        key = jax.random.key(seed)
        k1, k2, k3, k4, k5 = jax.random.split(key, 5)
        B, T = (4, 256)
        x = jax.random.normal(k1, (B, T, D), dtype=jnp.float32)
        s = 1.0 / np.sqrt(D)
        Wq = jax.random.normal(k2, (NKV, HS, D), dtype=jnp.float32) * s
        Wk = jax.random.normal(k3, (HS, D), dtype=jnp.float32) * s
        Wv = jax.random.normal(k4, (HS, D), dtype=jnp.float32) * s
        Wo = jax.random.normal(k5, (D, NKV * HS), dtype=jnp.float32) * (1.0 / np.sqrt(NKV * HS))
        return {'x': x, 'Wq': Wq, 'Wk': Wk, 'Wv': Wv, 'Wo': Wo}
    _L1_attn_in = _L1_attn_setup()

    def _L1_ffn_setup():
        import jax, jax.numpy as jnp
        import numpy as np
        E = 8
        K = 2
        D = 128
        key = jax.random.key(seed)
        k0, k1, k2, k3 = jax.random.split(key, 4)
        x = jax.random.normal(k0, (2, 256, D), dtype=jnp.float32)
        gate_w = jax.random.normal(k1, (D, E), dtype=jnp.float32) * 0.02
        fc_w = jax.random.normal(k2, (E, D, 4 * D), dtype=jnp.float32) * 0.02
        proj_w = jax.random.normal(k3, (E, 4 * D, D), dtype=jnp.float32) * 0.02
        return {'x': x, 'gate_w': gate_w, 'fc_w': fc_w, 'proj_w': proj_w}
    _L1_ffn_in = _L1_ffn_setup()
    _d = {'L0_attn_x': _L0_attn_in['x'], 'L0_attn_mask': _L0_attn_in['mask'], 'L0_attn_Wq': _L0_attn_in['Wq'], 'L0_attn_Wk': _L0_attn_in['Wk'], 'L0_attn_Wv': _L0_attn_in['Wv'], 'L0_attn_Wout': _L0_attn_in['Wout'], 'L0_ffn_wqkv': _L0_ffn_in['wqkv'], 'L0_ffn_q_scale': _L0_ffn_in['q_scale'], 'L0_ffn_k_scale': _L0_ffn_in['k_scale'], 'L0_ffn_wo': _L0_ffn_in['wo'], 'L0_ffn_ln_g': _L0_ffn_in['ln_g'], 'L0_ffn_ln_b': _L0_ffn_in['ln_b'], 'L0_ffn_w1': _L0_ffn_in['w1'], 'L0_ffn_b1': _L0_ffn_in['b1'], 'L0_ffn_w2': _L0_ffn_in['w2'], 'L0_ffn_b2': _L0_ffn_in['b2'], 'L1_attn_Wq': _L1_attn_in['Wq'], 'L1_attn_Wk': _L1_attn_in['Wk'], 'L1_attn_Wv': _L1_attn_in['Wv'], 'L1_attn_Wo': _L1_attn_in['Wo'], 'L1_ffn_gate_w': _L1_ffn_in['gate_w'], 'L1_ffn_fc_w': _L1_ffn_in['fc_w'], 'L1_ffn_proj_w': _L1_ffn_in['proj_w']}
    _x0 = _d['L0_attn_x']
    _d['L0_attn_x'] = jax.random.normal(jax.random.fold_in(jax.random.key(seed), 1), (2, 1024, 128), dtype=_x0.dtype)
    del _x0
    return _d

def reference(L0_attn_x, L0_attn_mask, L0_attn_Wq, L0_attn_Wk, L0_attn_Wv, L0_attn_Wout, L0_ffn_wqkv, L0_ffn_q_scale, L0_ffn_k_scale, L0_ffn_wo, L0_ffn_ln_g, L0_ffn_ln_b, L0_ffn_w1, L0_ffn_b1, L0_ffn_w2, L0_ffn_b2, L1_attn_Wq, L1_attn_Wk, L1_attn_Wv, L1_attn_Wo, L1_ffn_gate_w, L1_ffn_fc_w, L1_ffn_proj_w):

    def _L0_attn_ref(x, mask, Wq, Wk, Wv, Wout):
        import jax, jax.numpy as jnp
        import numpy as np
        B, S, D, H = (4, 256, 128, 16)
        DH = D // H
        n, s, d = x.shape
        scale = 1.0 / np.sqrt(DH).astype(np.float32)
        q = (x @ Wq).reshape(n, s, H, DH)
        k = (x @ Wk).reshape(n, s, H, DH)
        v = (x @ Wv).reshape(n, s, H, DH)
        attn = jnp.einsum('nqhd,nkhd->nqkh', q, k) * scale
        attn = jax.nn.softmax(attn, axis=-2)
        z = jnp.einsum('nqkh,nkhd->nqhd', attn, v).reshape(n, s, d)
        z = jnp.einsum('nqd,de->nqe', z, Wout)
        return x + z

    def _L0_ffn_ref(x, wqkv, q_scale, k_scale, wo, ln_g, ln_b, w1, b1, w2, b2):
        import jax, jax.numpy as jnp
        import numpy as np
        DIM = 128
        DEPTH = 2
        HEADS = 8
        DIM_HEAD = 64
        WINDOW = 64
        INNER = HEADS * DIM_HEAD
        HID = int(DIM * 4 * 2 / 3)
        B, N = (2, 1024)
        QK_SCALE = 8.0

        def shift_token(t):
            t1, t2 = jnp.split(t, 2, axis=-1)
            t2 = jnp.pad(t2, ((0, 0), (1, 0), (0, 0)))[:, :-1]
            return jnp.concatenate([t1, t2], axis=-1)

        def l2norm(t):
            return t / jnp.clip(jnp.linalg.norm(t, axis=-1, keepdims=True), 1e-12)

        def rotate_half(x):
            x1, x2 = jnp.split(x, 2, axis=-1)
            return jnp.concatenate([-x2, x1], axis=-1)

        def rotary_xpos(q, k):
            n = q.shape[-2]
            half_idx = jnp.arange(0, DIM_HEAD, 2, dtype=jnp.float32)
            inv_freq = 1.0 / 10000.0 ** (half_idx / DIM_HEAD)
            t = jnp.arange(n, dtype=jnp.float32)
            freqs = t[:, None] * inv_freq[None, :]
            freqs = jnp.concatenate([freqs, freqs], axis=-1)
            base = (half_idx + 0.4 * DIM_HEAD) / (1.4 * DIM_HEAD)
            power = (t - n // 2) / float(WINDOW // 2)
            scale = base[None, :] ** power[:, None]
            scale = jnp.concatenate([scale, scale], axis=-1)
            cos, sin = (jnp.cos(freqs), jnp.sin(freqs))
            q = q * cos * scale + rotate_half(q) * sin * scale
            k = k * cos / scale + rotate_half(k) * sin / scale
            return (q, k)

        def local_attention(q, k, v):
            b, h, n, d = q.shape
            w = n // WINDOW
            bq = q.reshape(b, h, w, WINDOW, d) * QK_SCALE
            bk = k.reshape(b, h, w, WINDOW, d)
            bv = v.reshape(b, h, w, WINDOW, d)

            def look_around(t):
                p = jnp.pad(t, ((0, 0), (0, 0), (1, 0), (0, 0), (0, 0)))
                return jnp.concatenate([p[:, :, :w], p[:, :, 1:]], axis=3)
            bk, bv = (look_around(bk), look_around(bv))
            bt = jnp.arange(n).reshape(w, WINDOW)
            btp = jnp.pad(bt, ((1, 0), (0, 0)), constant_values=-1)
            btk = jnp.concatenate([btp[:w], btp[1:]], axis=1)
            sim = jnp.einsum('bhwid,bhwjd->bhwij', bq, bk)
            i = bt[:, :, None]
            j = btk[:, None, :]
            mask = (i < j) | (i > j + WINDOW) | (j == -1)
            sim = jnp.where(mask, -jnp.finfo(sim.dtype).max, sim)
            attn = jax.nn.softmax(sim, axis=-1)
            out = jnp.einsum('bhwij,bhwjd->bhwid', attn, bv)
            return out.reshape(b, h, n, d)

        def _layer(x, wqkv, qs, ksc, wo, lg, lb, w1, b1, w2, b2):
            b, n, _ = x.shape
            h = shift_token(x)
            qkv = h @ wqkv
            q, k, v = jnp.split(qkv, 3, axis=-1)
            to_heads = lambda t: t.reshape(b, n, HEADS, DIM_HEAD).transpose(0, 2, 1, 3)
            q, k, v = (to_heads(q), to_heads(k), to_heads(v))
            q = l2norm(q) * qs
            k = l2norm(k) * ksc
            q, k = rotary_xpos(q, k)
            o = local_attention(q, k, v)
            o = o.transpose(0, 2, 1, 3).reshape(b, n, INNER)
            x = x + o @ wo
            h = shift_token(x)
            mu = h.mean(-1, keepdims=True)
            var = h.var(-1, keepdims=True)
            h = (h - mu) / jnp.sqrt(var + 1e-05) * lg + lb
            h = h @ w1 + b1
            a, g = jnp.split(h, 2, axis=-1)
            h = a * jax.nn.gelu(g, approximate=False)
            x = x + h @ w2 + b2
            return x
        for l in range(DEPTH):
            x = _layer(x, wqkv[l], q_scale[l], k_scale[l], wo[l], ln_g[l], ln_b[l], w1[l], b1[l], w2[l], b2[l])
        return x

    def _L1_attn_ref(x, Wq, Wk, Wv, Wo):
        import jax, jax.numpy as jnp
        import numpy as np
        D = 128
        HS = 128
        NKV = 2

        def apply_rope(x):
            d = x.shape[-1]
            T = x.shape[-2]
            positions = jnp.arange(0, d, 2, dtype=jnp.float32)
            theta = 10000.0 ** (-2.0 * positions / d)
            angles = jnp.arange(T, dtype=jnp.float32)[:, None] * theta[None, :]
            cos, sin = (jnp.cos(angles), jnp.sin(angles))
            xr = x.reshape(x.shape[:-1] + (d // 2, 2))
            out = jnp.stack([xr[..., 0] * cos - xr[..., 1] * sin, xr[..., 1] * cos + xr[..., 0] * sin], axis=-1)
            return out.reshape(x.shape)
        B, T, _ = x.shape
        k = apply_rope(x @ Wk.T)
        v = x @ Wv.T
        q = jnp.einsum('btd,hkd->bhtk', x, Wq)
        q = apply_rope(q)
        scale = HS ** (-0.5)
        scores = jnp.einsum('bhtk,bsk->bhts', q, k) * scale
        causal = jnp.tril(jnp.ones((T, T), dtype=bool))
        scores = jnp.where(causal, scores, -jnp.inf)
        w = jax.nn.softmax(scores, axis=-1)
        out = jnp.einsum('bhts,bsk->bhtk', w, v)
        out = out.transpose(0, 2, 1, 3).reshape(B, T, NKV * HS)
        return out @ Wo.T

    def _L1_ffn_ref(x, gate_w, fc_w, proj_w):
        import jax, jax.numpy as jnp
        import numpy as np
        E = 8
        K = 2
        D = 128
        orig_shape = x.shape
        d = orig_shape[-1]
        xt = x.reshape(-1, d)
        gates = jax.nn.softmax(xt @ gate_w, axis=-1)
        top_v, top_i = jax.lax.top_k(gates, K)
        top_v = top_v / jnp.sum(top_v, axis=-1, keepdims=True)
        h = jnp.einsum('nd,edf->enf', xt, fc_w)
        h = jax.nn.gelu(h, approximate=False)
        eo = jnp.einsum('enf,efd->end', h, proj_w)
        eo_nt = jnp.swapaxes(eo, 0, 1)
        sel = jnp.take_along_axis(eo_nt, top_i[:, :, None], axis=1)
        out = jnp.sum(sel * top_v[:, :, None], axis=1)
        return out.reshape(orig_shape)
    x = L0_attn_x
    x = _layernorm(x + _L0_attn_ref(x, L0_attn_mask, L0_attn_Wq, L0_attn_Wk, L0_attn_Wv, L0_attn_Wout), axis=-1)
    x = _layernorm(x + _L0_ffn_ref(x, L0_ffn_wqkv, L0_ffn_q_scale, L0_ffn_k_scale, L0_ffn_wo, L0_ffn_ln_g, L0_ffn_ln_b, L0_ffn_w1, L0_ffn_b1, L0_ffn_w2, L0_ffn_b2), axis=-1)
    x = _layernorm(x + _L1_attn_ref(x, L1_attn_Wq, L1_attn_Wk, L1_attn_Wv, L1_attn_Wo), axis=-1)
    x = _layernorm(x + _L1_ffn_ref(x, L1_ffn_gate_w, L1_ffn_fc_w, L1_ffn_proj_w), axis=-1)
    return x

_drawn_inputs = setup_inputs


def setup_inputs(seed=0):
    import zlib

    import numpy as np

    out = dict(_drawn_inputs(seed))
    spreads = {'L0_ffn_q_scale': (1.0, 0.6),
     'L0_ffn_k_scale': (1.0, 0.6),
     'L0_ffn_ln_g': (1.0, 0.6),
     'L0_ffn_ln_b': (0.0, 0.8),
     'L0_ffn_b1': (0.0, 0.8),
     'L0_ffn_b2': (0.0, 0.272)}
    factors = {'L0_ffn_wqkv': 3.438, 'L0_ffn_wo': 3.414, 'L0_ffn_w1': 5.79, 'L0_ffn_w2': 5.653}
    for name, (base, spread) in spreads.items():
        noise = np.random.default_rng([zlib.crc32(name.encode()), seed]).standard_normal(out[name].shape)
        drawn = base * np.exp(spread * noise) if base else spread * noise
        out[name] = jnp.asarray(drawn.astype(out[name].dtype))
    for name, factor in factors.items():
        out[name] = (out[name] * factor).astype(out[name].dtype)
    return out
```

```python
import concourse.bass as bass
from concourse import mybir
from contextlib import ExitStack

F32 = mybir.dt.float32
BF16 = mybir.dt.bfloat16
ALU = mybir.AluOpType
ACTF = mybir.ActivationFunctionType
AXX = mybir.AxisListType.X

P = 128
D = 128
NB = 2
SEQ = 1024
TPB = SEQ // P
NT = NB * TPB
BANK = 512
NEG = -3.3895313892515355e38
LOCAL_NEG = -3e37
EPS = 1e-5

H0, DH0 = 16, 8
GH = 4
NG = H0 // GH
STRIP = 32
SPLIT = 3
QK_ROWS = SPLIT * SPLIT * DH0
AUG = QK_ROWS + SPLIT

DEPTH = 2
H1, DH1 = 8, 64
INNER = H1 * DH1
WIN = 64
HID = int(D * 4 * 2 / 3)
HCH = -(-HID // 3)
HIDC = [min(HCH, HID - c * HCH) for c in range(3)]
KEYS = WIN + P
QK_SCALE = 8.0

NKV, HS = 2, 128
NE, FF, TOPK = 8, 4 * D, 2
FCH = FF // P
CHUNK = 512


class Sem:

    def __init__(self, handle):
        self.handle, self.count = handle, 0


class Queue:

    def __init__(self, sems):
        self.items, self.reached, self.sems = [], {}, sems

    def __call__(self, method, *args, after=(), sem=None, by=1, **kw):
        for s, value in after:
            if value > self.reached.get(s, 0):
                self.reached[s] = value
                self.items.append((None, s, value, None))
        self.items.append((method, args, kw, (sem, by)))
        if sem is None:
            return None
        self.sems[sem].count += by
        return sem, self.sems[sem].count

    def wait(self, *after):
        for s, value in after:
            if value > self.reached.get(s, 0):
                self.reached[s] = value
                self.items.append((None, s, value, None))

    def play(self, eng):
        for method, a, kw, last in self.items:
            if method is None:
                eng.wait_ge(self.sems[a].handle, kw)
            else:
                ins = method(*a, **kw)
                if last[0] is not None:
                    ins.then_inc(self.sems[last[0]].handle, last[1])


class Ring:

    def __init__(self, bufs):
        self.bufs = bufs
        self.free = [[] for _ in bufs]
        self.order = list(range(len(bufs)))

    def take(self):
        i = self.order.pop(0)
        return i, self.bufs[i], self.free[i]

    def give(self, i, *after):
        self.free[i] = list(after)
        self.order.append(i)


def weave(gens, width, skew=1):
    gens = list(gens)
    live, turn, nxt = [], 0, 0
    while gens or live:
        if gens and len(live) < width and turn >= nxt:
            live.append(gens.pop(0))
            nxt = turn + skew
        for g in list(live):
            try:
                next(g)
            except StopIteration:
                live.remove(g)
        turn += 1


def program(nc, T):
    ctx = ExitStack()
    with ctx:
        names = {}

        def sb(name, shape, dt=F32):
            return ctx.enter_context(nc.sbuf_tensor(name, shape, dt))

        class Sems(dict):
            def __missing__(self, name):
                self[name] = Sem(ctx.enter_context(nc.semaphore(name)))
                return self[name]

        sems = Sems()
        PE, DV, AC, GP, SP = (Queue(sems) for _ in range(5))
        mm, tr = nc.tensor.matmul, nc.tensor.transpose
        vec, act, gps, sync = nc.vector, nc.scalar, nc.gpsimd, nc.sync
        banks = Ring([ctx.enter_context(nc.psum_tensor(f"bank{i}", [P, BANK], F32)) for i in range(8)])

        ident = sb("ident", [P, P])
        identb = sb("identb", [P, P], BF16)
        ones_row = sb("ones_row", [1, P])
        local_mask = sb("local_mask", [P, 2, 2, KEYS], BF16)
        causal_mask = sb("causal_mask", [P, P], BF16)
        lower = sb("lower", [P, NE, NE])

        x = sb("x", [P, NT, D])
        xin = sb("xin", [P, NT, D])

        def load(dst, src, sem):
            return SP(sync.dma_start, dst, src, sem=sem, by=16)

        ld_x = load(x[:, :, :], T["x"].rearrange("b (t p) d -> p (b t) d", p=P), "ld_x")
        ld_id = load(ident[:, :], T["c_ident"], "ld_ident")
        wqkv0 = sb("wqkv0", [P, 3, D])
        for j, n in enumerate(("Wq", "Wk", "Wv")):
            ld_w0 = load(wqkv0[:, j, :], T[n], "ld_w0")
        wout0 = sb("wout0", [P, D])
        ld_w0 = load(wout0[:, :], T["Wout"], "ld_w0")
        load(identb[:, :], T["c_identb"], "ld_const")
        load(ones_row[:, :], T["c_ones"], "ld_const")
        load(local_mask[:, :, :, :], T["c_local"], "ld_const")
        load(causal_mask[:, :], T["c_causal"], "ld_const")
        ld_const = load(lower[:, :, :], T["c_lower"], "ld_const")

        stat = Ring([sb(f"stat{i}", [P, TPB, 6]) for i in range(2)])
        mean_var = [sb(f"mean_var{i}", [P, TPB, 2]) for i in range(2)]
        rstd = [sb(f"rstd{i}", [P, TPB]) for i in range(2)]

        x_ready = {t: ld_x for t in range(NT)}

        def transposed(t, dst, after, sem):
            i, bank, free = banks.take()
            done = PE(tr, bank[:, 0:P], x[:, t, :], ident[:, :], after=[x_ready[t], ld_id, *free], sem="pe_xT")
            done = AC(act.copy, dst, bank[:, 0:P], after=[done, *after], sem=sem)
            banks.give(i, done)
            return done

        def layer_norm(b, src_ready):
            ts = range(b * TPB, (b + 1) * TPB)
            si, st, free = stat.take()
            for j, t in enumerate(ts):
                done = DV(vec.bn_stats, st[:, j, :], x[:, t, :], after=[src_ready[t], *free], sem="ln_stat")
            for j, t in enumerate(ts):
                done = DV(vec.bn_aggr, mean_var[si][:, j, :], st[:, j, :], after=[done], sem="ln_aggr")
            yield
            v = DV(vec.tensor_scalar, rstd[si][:, :], mean_var[si][:, :, 1], EPS, None, ALU.add, after=[done],
                   sem="ln_eps")
            v = AC(act.activation, rstd[si][:, :], rstd[si][:, :], ACTF.Sqrt, after=[v], sem="ln_sqrt")
            v = DV(vec.reciprocal, rstd[si][:, :], rstd[si][:, :], after=[v], sem="ln_recip")
            yield
            for j, t in enumerate(ts):
                x_ready[t] = DV(vec.tensor_scalar, x[:, t, :], x[:, t, :], mean_var[si][:, j, 0:1],
                                rstd[si][:, j:j + 1], ALU.subtract, ALU.mult, after=[v], sem="ln_out")
            stat.give(si, x_ready[ts[-1]])
            yield

        def stage_out():
            for b in range(NB):
                ts = slice(b * TPB, (b + 1) * TPB)
                o = SP(sync.dma_start, T["out"][b].rearrange("(t p) d -> p t d", p=P), x[:, ts, :],
                       after=[x_ready[t] for t in range(b * TPB, (b + 1) * TPB)], sem="store", by=16)
            SP.wait(o)

        def done_all():
            return [(name, s.count) for name, s in sems.items() if s.count]

        def fence(tokens):
            for q in (SP, GP, PE, DV, AC):
                q.wait(*tokens)

        region = ExitStack()
        with region:
            def rb(name, shape, dt=F32):
                return region.enter_context(nc.sbuf_tensor(name, shape, dt))

            xT = rb("a_xT", [P, SEQ])
            parts = [rb(f"a_parts{j}", [P, SPLIT, SEQ], BF16) for j in range(2)]
            rest = rb("a_rest", [P, 2, BANK])
            UH = H0 // 2
            aug = [[rb(f"a_aug{u}{j}", [AUG, UH, SEQ], BF16) for j in range(2)] for u in range(2)]
            vaug = [rb(f"a_v{b}", [P, TPB, H0, STRIP]) for b in range(NB)]
            probs = Ring([rb(f"a_p{i}", [P, BANK]) for i in range(9)])
            oT = rb("a_oT", [P, BANK])
            z = rb("a_z", [P, TPB, D])
            zT = rb("a_zT", [P, P])
            mx = [rb(f"a_mx{i}", [P, 2, GH * TPB]) for i in range(2)]
            nmax = rb("a_nmax", [P, GH * TPB])
            mrest = rb("a_mrest", [GH * TPB, P])
            mpart = rb("a_mpart", [GH * TPB, SPLIT, P], BF16)
            rden = rb("a_rden", [P, TPB // 2, GH])
            scratch = [nc.dram_tensor(f"a_scratch{j}", [NB, SPLIT, P, SEQ], BF16).ap() for j in range(2)]

            vz = [GP(gps.memset, vaug[b][:, :, :, :], 0.0, sem="vaug_zero") for b in range(NB)]
            vz = [GP(gps.memset, vaug[b][:, :, :, DH0:DH0 + 1], 1.0, after=[vz[b]], sem="vaug_one")
                  for b in range(NB)]
            for u in range(2):
                ld_ones = load(aug[u][1][QK_ROWS:AUG, :, :], T["c_augones"], "ld_augones")
            v_ready, sc_ready = {}, {}
            scratch_free = {}
            parts_free = []
            xT_free = []

            def project(b):
                nonlocal parts_free, xT_free
                ts = range(b * TPB, (b + 1) * TPB)
                for j, t in enumerate(ts):
                    xt = transposed(t, xT[:, j * P:(j + 1) * P], xT_free, "a_xT")
                    yield
                last_mm = []
                for j in range(2):
                    for half in range(SEQ // BANK):
                        i, bank, free = banks.take()
                        cols = slice(half * BANK, (half + 1) * BANK)
                        m = PE(mm, bank[:, :], wqkv0[:, j, :], xT[:, cols], start=True, stop=True,
                               after=[xt, ld_w0, *free], sem="a_qk")
                        d = DV(vec.tensor_copy, parts[j][:, 0, cols], bank[:, :], after=[m, *parts_free], sem="a_split")
                        d = DV(vec.tensor_tensor, rest[:, half, :], bank[:, :], parts[j][:, 0, cols], ALU.subtract,
                               after=[d], sem="a_split")
                        banks.give(i, d)
                        d = DV(vec.tensor_copy, parts[j][:, 1, cols], rest[:, half, :], after=[d], sem="a_split")
                        d = DV(vec.tensor_tensor, parts[j][:, 2, cols], rest[:, half, :], parts[j][:, 1, cols],
                               ALU.subtract, after=[d], sem="a_split")
                        yield
                    sc_ready[b, j] = SP(sync.dma_start, scratch[j][b].rearrange("s p t -> p s t"), parts[j][:, :, :],
                                        after=[d], sem=f"scratch{b}{j}", by=16)
                parts_free = [sc_ready[b, 0], sc_ready[b, 1]]
                for j, t in enumerate(ts):
                    i, bank, free = banks.take()
                    m = PE(mm, bank[:, 0:D], xT[:, j * P:(j + 1) * P], wqkv0[:, 2, :], start=True, stop=True,
                           after=[xt, ld_w0, *free], sem="a_v")
                    v_ready[t] = AC(act.copy, vaug[b][:, j, :, 0:DH0],
                                    bank[:, 0:D].rearrange("p (h d) -> p h d", h=H0), after=[m, vz[b]], sem="a_vcopy")
                    banks.give(i, v_ready[t])
                    yield
                xT_free = [m]

            aug_ready = {}
            aug_free = {0: [], 1: []}

            def gather(b, u):
                for j in range(2):
                    for a in range(SPLIT):
                        for c in range(SPLIT):
                            row = (a * SPLIT + c) * DH0
                            src = scratch[j][b, (a, c)[j], u * UH * DH0:(u + 1) * UH * DH0, :]
                            aug_ready[b, u] = SP(sync.dma_start, aug[u][j][row:row + DH0, :, :],
                                                 src.rearrange("(h d) t -> d h t", d=DH0),
                                                 after=[sc_ready[b, j], *aug_free[u]], sem=f"gather{b}{u}", by=16)
                yield

            nmax_ready = {}
            mrow_free = []
            m_free = []

            def maxima(b, g):
                nonlocal mrow_free, m_free
                u = g // (NG // 2)
                mxb = mx[(b * NG + g) % 2]
                for hh in range(GH):
                    hu = (g * GH + hh) % UH
                    for qt in range(TPB):
                        for half in range(2):
                            i, bank, free = banks.take()
                            m = PE(mm, bank[:, :], aug[u][0][0:QK_ROWS, hu, qt * P:(qt + 1) * P],
                                   aug[u][1][0:QK_ROWS, hu, half * BANK:(half + 1) * BANK], start=True, stop=True,
                                   after=[aug_ready[b, u], *free], sem="a_smax")
                            c = hh * TPB + qt
                            d = DV(vec.reduce_max, mxb[:, half, c:c + 1], bank[:, :], AXX, after=[m], sem="a_max")
                            banks.give(i, d)
                            yield
                n = DV(vec.tensor_tensor, nmax[:, :], mxb[:, 0, :], mxb[:, 1, :], ALU.max, after=[d, *mrow_free],
                       sem="a_max2")
                i, bank, free = banks.take()
                m = PE(tr, bank[0:GH * TPB, 0:P], nmax[:, :], ident[:, :], after=[n, *free], sem="a_maxT")
                mrow_free = [m]
                d = DV(vec.tensor_scalar, mrest[:, :], bank[0:GH * TPB, 0:P], -1.0, None, ALU.mult, after=[m],
                       sem="a_mneg")
                banks.give(i, d)
                d = DV(vec.tensor_copy, mpart[:, 0, :], mrest[:, :], after=[d, *m_free], sem="a_msplit")
                d = DV(vec.tensor_tensor, mrest[:, :], mrest[:, :], mpart[:, 0, :], ALU.subtract, after=[d],
                       sem="a_msplit")
                d = DV(vec.tensor_copy, mpart[:, 1, :], mrest[:, :], after=[d], sem="a_msplit")
                d = DV(vec.tensor_tensor, mpart[:, 2, :], mrest[:, :], mpart[:, 1, :], ALU.subtract, after=[d],
                       sem="a_msplit")
                hu = (g * GH) % UH
                sem = f"mrows{b}{g}"
                for s in range(SPLIT):
                    dst = aug[u][0][QK_ROWS + s:QK_ROWS + s + 1, hu:hu + GH, :]
                    r = SP(sync.dma_start, dst.rearrange("a h (t q) -> a (h t) q", q=P), mpart[:, s, :],
                           after=[d], sem=sem, by=16)
                nmax_ready[b, g] = r
                m_free = [r]
                yield

            z_ready = {}
            oT_free, z_free, zT_free = [], [], []
            HEAD_TILES = TPB // 2

            def attend(b, g):
                nonlocal oT_free
                u = g // (NG // 2)
                scale = 1.0 / float(DH0) ** 0.5
                for half in range(2):
                    oi, obank, ofree = banks.take()
                    pend = []

                    def values(kt, tiles):
                        nonlocal ofree
                        for hh, (pi, pbuf, e) in enumerate(tiles):
                            h = g * GH + hh
                            m = PE(mm, obank[hh * STRIP:(hh + 1) * STRIP, :], vaug[b][:, kt, h, :], pbuf[:, :],
                                   start=(kt == 0), stop=(kt == TPB - 1), after=[e, v_ready[b * TPB + kt], *ofree],
                                   sem="a_pv")
                            probs.give(pi, m)
                        ofree = []
                        return m

                    for kt in range(TPB):
                        tiles = []
                        for hh in range(GH):
                            hu = (g * GH + hh) % UH
                            i, bank, free = banks.take()
                            m = PE(mm, bank[:, :], aug[u][1][:, hu, kt * P:(kt + 1) * P],
                                   aug[u][0][:, hu, half * BANK:(half + 1) * BANK], start=True, stop=True,
                                   after=[nmax_ready[b, g], ld_ones, *free], sem="a_sT")
                            pi, pbuf, pfree = probs.take()
                            e = AC(act.activation, pbuf[:, :], bank[:, :], ACTF.Exp, scale=scale, after=[m, *pfree],
                                   sem="a_exp")
                            banks.give(i, e)
                            tiles.append((pi, pbuf, e))
                            yield
                        if pend:
                            values(*pend)
                        pend = (kt, tiles)
                    m = values(*pend)
                    yield
                    e = AC(act.copy, oT[:, :], obank[:, :], after=[m, *oT_free], sem="a_oT")
                    banks.give(oi, e)
                    yield
                    i, bank, free = banks.take()
                    for q in range(HEAD_TILES):
                        m = PE(tr, bank[:, q * P:(q + 1) * P], oT[:, q * P:(q + 1) * P], ident[:, :], after=[e, *free],
                               sem="a_oTT")
                    oT_free = [m]
                    yield
                    o = bank[:, :].rearrange("p (q h c) -> p q h c", q=HEAD_TILES, h=GH)
                    d = DV(vec.reciprocal, rden[:, :, :], o[:, :, :, DH0], after=[m], sem="a_rden")
                    zz = z[:, half * HEAD_TILES:(half + 1) * HEAD_TILES, g * STRIP:(g + 1) * STRIP]
                    zz = zz.rearrange("p q (h c) -> p q h c", h=GH)
                    for q in range(HEAD_TILES):
                        d = DV(vec.tensor_tensor, zz[:, q], o[:, q, :, 0:DH0],
                               rden[:, q, :].unsqueeze(2).to_broadcast([P, GH, DH0]), ALU.mult,
                               after=[d, *z_free], sem="a_z")
                    banks.give(i, d)
                    z_ready[b] = d
                aug_free[u] = [("a_sT", sems["a_sT"].count), ("a_smax", sems["a_smax"].count)]

            def output(b):
                nonlocal z_free, zT_free
                out = {}
                for j in range(TPB):
                    t = b * TPB + j
                    i, bank, free = banks.take()
                    m = PE(tr, bank[:, 0:P], z[:, j, :], ident[:, :], after=[z_ready[b], *free], sem="a_zTT")
                    z_free = [m]
                    e = AC(act.copy, zT[:, :], bank[:, 0:P], after=[m, *zT_free], sem="a_zT")
                    m = PE(mm, bank[:, P:2 * P], zT[:, :], wout0[:, :], start=True, stop=True, after=[e], sem="a_out")
                    zT_free = [m]
                    out[t] = DV(vec.scalar_tensor_tensor, x[:, t, :], x[:, t, :], 2.0, bank[:, P:2 * P], ALU.mult,
                                ALU.add, after=[m], sem="a_res")
                    banks.give(i, out[t])
                    yield
                yield from layer_norm(b, out)

            weave([project(0)], 1)
            weave([gather(0, 0)], 1)
            weave([gather(0, 1)], 1)
            groups = [(b, g) for b in range(NB) for g in range(NG)]
            weave([maxima(0, 0)], 1)
            extra = []
            for n, (b, g) in enumerate(groups):
                work = [attend(b, g)]
                if b == 0 and g == 0:
                    work.append(project(1))
                if n + 1 < len(groups):
                    nb, ng = groups[n + 1]
                    work.insert(0, maxima(nb, ng))
                weave(work, len(work), 0)
                if b + 1 < NB and g % 2 == 1:
                    weave([gather(b + 1, g // 2)], 1)
                if g == NG - 1:
                    weave([output(b)], 1)


        region = ExitStack()
        with region:
            fence(done_all())
            wqkv = [rb(f"b_wqkv{l}", [P, 3 * INNER]) for l in range(DEPTH)]
            wo = [rb(f"b_wo{l}", [P, INNER // P, D]) for l in range(DEPTH)]
            w1 = [rb(f"b_w1{l}", [P, 2 * HID]) for l in range(DEPTH)]
            w2 = [rb(f"b_w2{l}", [HCH, 3, D]) for l in range(DEPTH)]
            b1 = [rb(f"b_b1{l}", [HCH, 6]) for l in range(DEPTH)]
            b2 = [rb(f"b_b2{l}", [1, D]) for l in range(DEPTH)]
            ln = [rb(f"b_ln{l}", [P, 2]) for l in range(DEPTH)]
            scales = [rb(f"b_scales{l}", [P, 2, DH1]) for l in range(DEPTH)]
            ld_w = []
            for l in range(DEPTH):
                s = f"ld_layer{l}"
                load(wqkv[l][:, :], T["wqkv"][l], s)
                for j, n in enumerate(("q_scale", "k_scale")):
                    load(scales[l][:, j, :], T[n][l:l + 1, :].to_broadcast([P, DH1]), s)
                load(wo[l][:, :, :], T["wo"][l].rearrange("(c p) d -> p c d", p=P), s)
                load(w1[l][:, :], T["w1"][l], s)
                for c in range(3):
                    n = HIDC[c]
                    load(w2[l][0:n, c, :], T["w2"][l][c * HCH:c * HCH + n, :], s)
                    for j in range(2):
                        lo = j * HID + c * HCH
                        load(b1[l][0:n, 3 * j + c:3 * j + c + 1],
                             T["b1"][l:l + 1, lo:lo + n].rearrange("a n -> n a"), s)
                load(b2[l][:, :], T["b2"][l:l + 1, :], s)
                load(ln[l][:, 0:1], T["ln_g"][l:l + 1, :].rearrange("a n -> n a"), s)
                ld_w.append(load(ln[l][:, 1:2], T["ln_b"][l:l + 1, :].rearrange("a n -> n a"), s))

            rot_q = rb("b_rot", [P, 4, TPB, DH1])
            hT = rb("b_hT", [P, SEQ + 1])
            sq = Ring([rb(f"b_sq{i}", [P, INNER]) for i in range(1)])
            t1 = Ring([rb(f"b_t1{i}", [P, INNER]) for i in range(2)])
            t2 = Ring([rb(f"b_t2{i}", [P, INNER]) for i in range(2)])
            ss = rb("b_ss", [P, TPB, 2, H1])
            qk = rb("b_qk", [P, TPB, 2, INNER])
            kT = rb("b_kT", [P, H1 // 2, WIN + SEQ])
            qT = rb("b_qT", [P, H1 // 2, SEQ])
            vv = [rb(f"b_vv{b}", [P, TPB, H1, DH1 + 1]) for b in range(NB)]
            pp = Ring([rb(f"b_p{i}", [P, H1, 2 * P]) for i in range(2)])
            pT = Ring([rb(f"b_pT{i}", [P, H1, 2, P]) for i in range(2)])
            mxl = Ring([rb(f"b_mx{i}", [P, H1]) for i in range(2)])
            rdl = Ring([rb(f"b_rd{i}", [P, H1]) for i in range(2)])
            oo = Ring([rb(f"b_o{i}", [P, INNER]) for i in range(2)])
            ooT = Ring([rb(f"b_oT{i}", [P, INNER // P, P]) for i in range(1)])
            zero = [GP(gps.memset, hT[:, 0:1], 0.0, sem="b_zero"),
                    GP(gps.memset, kT[:, :, 0:WIN], 0.0, sem="b_zero")]
            zero += [GP(gps.memset, p[:, :, 0:WIN], 0.0, sem="b_zero") for p in pp.bufs]
            zero += [GP(gps.memset, v[:, :, :, DH1:DH1 + 1], 1.0, sem="b_zero") for v in vv]
            b_zero = zero[-1]
            flat = qk[:, :, :, :].rearrange("p t a c -> p (t a c)")
            hh = flat[:, 0:SEQ].rearrange("p (t d) -> p t d", t=TPB)
            nT = flat[:, SEQ:2 * SEQ]
            gl = Ring([flat[0:HCH, (4 + i) * CHUNK:(5 + i) * CHUNK] for i in range(2)])
            uT = Ring([flat[0:HCH, (6 + 3 * i) * CHUNK:(9 + 3 * i) * CHUNK].rearrange("p (c t) -> p c t", c=3)
                       for i in range(2)])

            for t in range(NT):
                done = GP(gps.tensor_copy, xin[:, t, :], x[:, t, :], after=[x_ready[t]], sem="b_keep")
            kept = done

            hT_free = []
            qk_free, ss_free, kT_free = [], [], []
            vv_free = {0: [], 1: []}
            rn_ready, v_done, qT_done, kT_done, r_done = {}, {}, {}, {}, {}
            x_free = {t: kept for t in range(NT)}

            def shifted(t, after):
                j = t % TPB
                i, bank, free = banks.take()
                m = PE(tr, bank[:, 0:P], x[:, t, :], ident[:, :], after=[x_ready[t], *free], sem="pe_xT")
                half = D // 2
                AC(act.copy, hT[0:half, j * P:(j + 1) * P], bank[0:half, 0:P], after=[m, b_zero, *after], sem="b_hT")
                h = AC(act.copy, hT[half:P, j * P + 1:(j + 1) * P + 1], bank[half:P, 0:P], sem="b_hT")
                banks.give(i, h)
                return m, h

            def fold(l):
                tab_in = SP(sync.dma_start, rot_q[:, :, :, :], T["c_rot"], after=rot_free, sem="ld_rot", by=16)
                for j in range(2):
                    c, s, g = 2 * j, 2 * j + 1, scales[l][:, j, :]
                    half = DH1 // 2
                    for tab, lo, src in ((c, 0, g[:, 0:half]), (c, half, g[:, half:]), (s, 0, g[:, half:]),
                                         (s, half, g[:, 0:half])):
                        d = DV(vec.tensor_tensor, rot_q[:, tab, :, lo:lo + half], rot_q[:, tab, :, lo:lo + half],
                               src.unsqueeze(1).to_broadcast([P, TPB, half]), ALU.mult,
                               after=[tab_in, ld_w[l]], sem="b_fold")
                return d

            def qkv(b, l, j, tables):
                nonlocal hT_free
                t = b * TPB + j
                m, h = shifted(t, hT_free if j == 0 else [])
                yield
                for part in range(3):
                    i, bank, free = banks.take()
                    m = PE(mm, bank[:, :], hT[:, j * P:(j + 1) * P], wqkv[l][:, part * INNER:(part + 1) * INNER],
                           start=True, stop=True, after=[h, ld_w[l], *free], sem="b_qkv")
                    if part == 2:
                        v_done[t] = AC(act.copy, vv[b][:, j, :, 0:DH1], bank[:, :].rearrange("p (h d) -> p h d", h=H1),
                                       after=[m, b_zero, *vv_free[b]], sem="b_v")
                        banks.give(i, v_done[t])
                        if j == TPB - 1:
                            hT_free = [m]
                        yield
                        continue
                    si, s, sfree = sq.take()
                    a = AC(act.square, s[:, :], bank[:, :], after=[m, *sfree], sem="b_sq")
                    d = DV(vec.reduce_sum, ss[:, j, part, :], s[:, :].rearrange("p (h d) -> p h d", h=H1), AXX,
                           after=[a, *ss_free], sem="b_ss")
                    sq.give(si, d)
                    v = bank[:, :].rearrange("p (h d) -> p h d", h=H1)
                    half = DH1 // 2

                    def table(k, lo, n):
                        return rot_q[:, 2 * part + k, j, lo:lo + n].unsqueeze(1).to_broadcast([P, H1, n])
                    i1, a1, free1 = t1.take()
                    i2, a2, free2 = t2.take()
                    r1 = DV(vec.tensor_tensor, a1[:, :].rearrange("p (h d) -> p h d", h=H1), v, table(0, 0, DH1),
                            ALU.mult, after=[m, tables, *free1], sem="b_rot")
                    a2v = a2[:, :].rearrange("p (h d) -> p h d", h=H1)
                    DV(vec.tensor_tensor, a2v[:, :, 0:half], v[:, :, half:], table(1, 0, half), ALU.mult,
                       after=free2, sem="b_rot")
                    r2 = DV(vec.tensor_tensor, a2v[:, :, half:], v[:, :, 0:half], table(1, half, half), ALU.mult,
                            sem="b_rot")
                    banks.give(i, a, r2)
                    g = GP(gps.tensor_tensor, qk[:, j, part, :], a1[:, :], a2[:, :], ALU.add, after=[r2, *qk_free],
                           sem="b_rotsum")
                    t1.give(i1, g)
                    t2.give(i2, g)
                    r_done[t] = g
                    rn_ready[b] = d
                    yield

            def norms(b):
                a = AC(act.activation, ss[:, :, :, :], ss[:, :, :, :], ACTF.Sqrt, after=[rn_ready[b]], sem="b_norm")
                d = DV(vec.tensor_scalar, ss[:, :, :, :], ss[:, :, :, :], 1e-12, None, ALU.max, after=[a], sem="b_clip")
                rn_ready[b] = DV(vec.reciprocal, ss[:, :, :, :], ss[:, :, :, :], after=[d], sem="b_rn")

            def turn(b, j):
                nonlocal qk_free, ss_free
                t = b * TPB + j
                v = qk[:, j, :, :].rearrange("p a (h d) -> p (a h) d", h=H1)
                d = DV(vec.tensor_tensor, v, v,
                       ss[:, j, :, :].rearrange("p a h -> p (a h)").unsqueeze(2).to_broadcast([P, 2 * H1, DH1]),
                       ALU.mult, after=[rn_ready[b], r_done[t]], sem="b_scale")
                ss_free = [d]
                yield
                for part in range(2):
                    i, bank, free = banks.take()
                    for c in range(INNER // P):
                        m = PE(tr, bank[:, c * P:(c + 1) * P], qk[:, j, part, c * P:(c + 1) * P], ident[:, :],
                               after=[d, *free], sem="b_qkT")
                    src = bank[:, :].rearrange("p (c t) -> p c t", t=P)
                    if part == 0:
                        e = AC(act.copy, qT[:, :, j * P:(j + 1) * P], src, after=[m, *kT_free], sem="b_qT")
                        qT_done[t] = e
                    else:
                        e = AC(act.copy, kT[:, :, WIN + j * P:WIN + (j + 1) * P], src, after=[m, *kT_free], sem="b_kT")
                        kT_done[t] = e
                    banks.give(i, e)
                    yield
                qk_free = [m]

            def local(b, l, j):
                nonlocal kT_free
                t = b * TPB + j
                xi, mxb, mfree = mxl.take()
                held = []
                for k in range(H1 // 2):
                    i, bank, free = banks.take()
                    PE(mm, bank[:, 0:2 * KEYS], identb[:, :],
                       local_mask[:, 0 if j else 1, :, :].rearrange("p a k -> p (a k)"), start=True, stop=False,
                       after=[ld_const, *free])
                    held.append((i, bank))
                for p in range(H1 // 2):
                    for hp in range(2):
                        rows = slice(hp * DH1, (hp + 1) * DH1)
                        m = PE(mm, held[p // 2 * 2 + hp][1][:, p % 2 * KEYS:(p % 2 + 1) * KEYS],
                               qT[rows, p, j * P:(j + 1) * P], kT[rows, p, j * P:j * P + KEYS], start=False,
                               stop=(p % 2 == 1), after=[qT_done[t], kT_done[t], b_zero], sem="b_s")
                        if p % 2:
                            k = p // 2 * 2 + hp
                            d = DV(vec.reduce_max, mxb[:, 2 * k:2 * k + 2],
                                   held[k][1][:, 0:2 * KEYS].rearrange("p (a k) -> p a k", a=2), AXX,
                                   after=[m, *mfree], sem="b_max")
                d = DV(vec.tensor_scalar, mxb[:, :], mxb[:, :], -QK_SCALE, None, ALU.mult, after=[d], sem="b_nmax")
                yield
                pi, pb, pfree = pp.take()
                ti, pt, tfree = pT.take()
                for p in range(H1 // 2):
                    for hp in range(2):
                        h = 2 * p + hp
                        k = p // 2 * 2 + hp
                        i, bank = held[k]
                        e = AC(act.activation, pb[:, h, WIN:], bank[:, p % 2 * KEYS:(p % 2 + 1) * KEYS], ACTF.Exp,
                               bias=mxb[:, 2 * k + p % 2:2 * k + p % 2 + 1], scale=QK_SCALE,
                               after=[d, b_zero, *pfree], sem="b_exp")
                        if p % 2:
                            banks.give(i, e)
                    if p == H1 // 2 - 1:
                        mxl.give(xi, e)
                    yield
                    i, bank, free = banks.take()
                    for k in range(4):
                        m = PE(tr, bank[:, k * P:(k + 1) * P], pb[:, 2 * p + k // 2, (k % 2) * P:(k % 2 + 1) * P],
                               ident[:, :], after=[e, *free], sem="b_pT")
                    dst = pt[:, 2 * p:2 * p + 2, :, :].rearrange("p a c q -> p (a c q)")
                    if p % 2:
                        c = AC(act.copy, dst, bank[:, :], after=[m, *tfree], sem="b_pTa")
                        ca = c
                    else:
                        c = DV(vec.tensor_copy, dst, bank[:, :], after=[m, *tfree], sem="b_pTd")
                        cd = c
                    banks.give(i, c)
                    yield
                pp.give(pi, m)
                ri, rd, rfree = rdl.take()
                oi, o, ofree = oo.take()
                for q in range(2):
                    i, bank, free = banks.take()
                    for h4 in range(4):
                        h = 4 * q + h4
                        out = bank[:, h4 * (DH1 + 1):(h4 + 1) * (DH1 + 1)]
                        if j:
                            PE(mm, out, pt[P - WIN:, h, 0, :], vv[b][P - WIN:, j - 1, h, :], start=True, stop=False,
                               after=[ca, cd, v_done[t - 1], *free])
                        m = PE(mm, out, pt[:, h, 1, :], vv[b][:, j, h, :], start=(j == 0), stop=True,
                               after=[ca, cd, v_done[t], *free], sem="b_o")
                    bv = bank[:, 0:4 * (DH1 + 1)].rearrange("p (h d) -> p h d", h=4)
                    d = DV(vec.reciprocal, rd[:, 4 * q:4 * q + 4], bv[:, :, DH1], after=[m, *rfree], sem="b_rden")
                    d = DV(vec.tensor_tensor, o[:, 4 * q * DH1:4 * (q + 1) * DH1].rearrange("p (h d) -> p h d", h=4),
                           bv[:, :, 0:DH1], rd[:, 4 * q:4 * q + 4].unsqueeze(2).to_broadcast([P, 4, DH1]), ALU.mult,
                           after=[d, *ofree], sem="b_on")
                    banks.give(i, d)
                pT.give(ti, m)
                rdl.give(ri, d)
                if j == TPB - 1:
                    vv_free[b] = [m]
                    kT_free = [("b_s", sems["b_s"].count)]
                yield
                i, bank, free = banks.take()
                for c in range(INNER // P):
                    m = PE(tr, bank[:, c * P:(c + 1) * P], o[:, c * P:(c + 1) * P], ident[:, :], after=[d, *free],
                           sem="b_oTT")
                oo.give(oi, m)
                ci, ot, cfree = ooT.take()
                e = AC(act.copy, ot[:, :, :].rearrange("p c t -> p (c t)"), bank[:, :], after=[m, *cfree], sem="b_oT")
                banks.give(i, e)
                yield
                i, bank, free = banks.take()
                for c in range(INNER // P):
                    m = PE(mm, bank[:, 0:D], ot[:, c, :], wo[l][:, c, :], start=(c == 0), stop=(c == INNER // P - 1),
                           after=[e, *free], sem="b_wo" if c == INNER // P - 1 else None)
                ooT.give(ci, m)
                x_ready[t] = DV(vec.tensor_tensor, x[:, t, :], bank[:, 0:D], x[:, t, :], ALU.add,
                                after=[m, x_free[t]], sem="b_res")
                banks.give(i, x_ready[t])
                yield

            hh_free, nT_free = [], []
            stats_done, h_done, nT_done = {}, {}, {}

            def ffn_head(b, j, si, st):
                nonlocal hT_free
                t = b * TPB + j
                m, h = shifted(t, hT_free if j == 0 else [])
                yield
                i, bank, free = banks.take()
                m = PE(tr, bank[:, 0:P], hT[:, j * P:(j + 1) * P], ident[:, :], after=[h, *free], sem="f_hh")
                if j == TPB - 1:
                    hT_free = [m]
                h_done[t] = AC(act.copy, hh[:, j, :], bank[:, 0:P], after=[m, *hh_free], sem="f_h")
                banks.give(i, h_done[t])
                yield
                d = DV(vec.bn_stats, st[:, j, :], hh[:, j, :], after=[h_done[t]], sem="f_stat")
                stats_done[b] = DV(vec.bn_aggr, mean_var[si][:, j, :], st[:, j, :], after=[d], sem="f_aggr")
                yield

            def ffn_norm(b, l, j, si, v):
                nonlocal hh_free
                t = b * TPB + j
                d = DV(vec.tensor_scalar, hh[:, j, :], hh[:, j, :], mean_var[si][:, j, 0:1], rstd[si][:, j:j + 1],
                       ALU.subtract, ALU.mult, after=[v], sem="f_n")
                yield
                i, bank, free = banks.take()
                m = PE(tr, bank[:, 0:P], hh[:, j, :], ident[:, :], after=[d, *free], sem="f_nTT")
                hh_free = [m]
                nT_done[t] = DV(vec.tensor_scalar, nT[:, j * P:(j + 1) * P], bank[:, 0:P], ln[l][:, 0:1],
                                ln[l][:, 1:2], ALU.mult, ALU.add, after=[m, ld_w[l], *nT_free], sem="f_nT")
                banks.give(i, nT_done[t])
                yield

            def ffn_mix(b, l, half):
                nonlocal nT_free
                tpc = CHUNK // P
                t0 = b * TPB + half * tpc
                cols = slice(half * CHUNK, (half + 1) * CHUNK)
                ui, u, ufree = uT.take()
                for c in range(3):
                    n = HIDC[c]
                    i, gbank, free = banks.take()
                    lo = HID + c * HCH
                    m = PE(mm, gbank[0:n, :], w1[l][:, lo:lo + n], nT[:, cols], start=True, stop=True,
                           after=[nT_done[t0 + tpc - 1], *free], sem="f_w1")
                    gi, gb, gfree = gl.take()
                    a = AC(act.activation, gb[0:n, :], gbank[0:n, :], ACTF.Gelu, bias=b1[l][0:n, 3 + c:4 + c],
                           scale=1.0, after=[m, *gfree], sem="f_gelu")
                    banks.give(i, a)
                    i, abank, free = banks.take()
                    lo = c * HCH
                    m = PE(mm, abank[0:n, :], w1[l][:, lo:lo + n], nT[:, cols], start=True, stop=True,
                           after=free, sem="f_w1")
                    d = DV(vec.scalar_tensor_tensor, u[0:n, c, :], abank[0:n, :], b1[l][0:n, c:c + 1], gb[0:n, :],
                           ALU.add, ALU.mult, after=[m, a, *ufree], sem="f_u")
                    banks.give(i, d)
                    gl.give(gi, d)
                    yield
                nT_free = [m]
                for q in range(tpc):
                    t = t0 + q
                    i, bank, free = banks.take()
                    for c in range(3):
                        n = HIDC[c]
                        PE(mm, bank[:, 0:D], u[0:n, c, q * P:(q + 1) * P], w2[l][0:n, c, :], start=(c == 0), stop=False,
                           after=[d, *free])
                    m = PE(mm, bank[:, 0:D], ones_row[:, :], b2[l][:, :], start=False, stop=True, sem="f_w2")
                    x_ready[t] = DV(vec.tensor_tensor, x[:, t, :], bank[:, 0:D], x[:, t, :], ALU.add,
                                    after=[m, x_ready[t]], sem="f_res")
                    banks.give(i, x_ready[t])
                    yield
                uT.give(ui, m)

            def finish_rstd(si, done):
                v = DV(vec.tensor_scalar, rstd[si][:, :], mean_var[si][:, :, 1], EPS, None, ALU.add, after=[done],
                       sem="ln_eps")
                v = AC(act.activation, rstd[si][:, :], rstd[si][:, :], ACTF.Sqrt, after=[v], sem="ln_sqrt")
                return DV(vec.reciprocal, rstd[si][:, :], rstd[si][:, :], after=[v], sem="ln_recip")

            rot_free = []
            for l in range(DEPTH):
                tables = fold(l)
                for b in range(NB):
                    weave([qkv(b, l, j, tables) for j in range(TPB)], 2, 2)
                    norms(b)
                    weave([turn(b, j) for j in range(TPB)], 2, 1)
                    weave([local(b, l, j) for j in range(TPB)], 2, 5)
                rot_free = [("b_rot", sems["b_rot"].count)]
                hh_free = list(qk_free)
                for b in range(NB):
                    si, st, free = stat.take()
                    weave([ffn_head(b, j, si, st) for j in range(TPB)], 2, 1)
                    v = finish_rstd(si, stats_done[b])
                    weave([ffn_norm(b, l, j, si, v) for j in range(TPB)], 2, 1)
                    stat.give(si, v)
                    weave([ffn_mix(b, l, half) for half in range(SEQ // CHUNK)], 2, 3)
                qk_free = [("f_w2", sems["f_w2"].count), ("f_w1", sems["f_w1"].count)]
            for b in range(NB):
                ready = {}
                for t in range(b * TPB, (b + 1) * TPB):
                    ready[t] = DV(vec.tensor_tensor, x[:, t, :], x[:, t, :], xin[:, t, :], ALU.add,
                                  after=[x_ready[t], kept], sem="b_add")
                weave([layer_norm(b, ready)], 1)

        region = ExitStack()
        with region:
            fence(done_all())
            wq1 = rb("c_wqkv", [P, 4, HS])
            wo1 = rb("c_wo", [P, NKV, D])
            for j in range(NKV):
                load(wq1[:, j, :], T["Wq1T"][j], "ld_c")
                load(wo1[:, j, :], T["Wo1T"][j * P:(j + 1) * P, :], "ld_c")
            load(wq1[:, 2, :], T["Wk1T"], "ld_c")
            ld_c = load(wq1[:, 3, :], T["Wv1T"], "ld_c")
            rope_tab = rb("c_rope", [P, 2, TPB, HS])
            ld_rope = load(rope_tab[:, :, :, :], T["c_rope"], "ld_rope")
            xTc = Ring([rb(f"c_xT{i}", [P, P]) for i in range(2)])
            r1 = Ring([rb(f"c_r1{i}", [P, 3, HS]) for i in range(2)])
            r2 = Ring([rb(f"c_r2{i}", [P, 3, HS]) for i in range(2)])
            qkT = [rb(f"c_qkT{b}", [P, 3, SEQ]) for b in range(NB)]
            vc = [rb(f"c_v{b}", [P, TPB, HS + 1]) for b in range(NB)]
            pc = Ring([rb(f"c_p{i}", [P, SEQ]) for i in range(3)])
            pcT = Ring([rb(f"c_pT{i}", [P, SEQ]) for i in range(3)])
            mc = Ring([rb(f"c_m{i}", [P, 4]) for i in range(4)])
            oc = Ring([rb(f"c_o{i}", [P, NKV, HS]) for i in range(2)])
            ocT = Ring([rb(f"c_oT{i}", [P, NKV, P]) for i in range(2)])
            for b in range(NB):
                c_one = GP(gps.memset, vc[b][:, :, HS:HS + 1], 1.0, sem="c_one")
            qk_done, vc_done, res = {}, {}, {}

            def rope(b, j):
                t = b * TPB + j
                xi, xt, xfree = xTc.take()
                e = transposed(t, xt[:, :], xfree, "c_xT")
                yield
                i, bank, free = banks.take()
                m = PE(mm, bank[:, :], xt[:, :], wq1[:, :, :].rearrange("p a k -> p (a k)"), start=True, stop=True,
                       after=[e, ld_c, *free], sem="c_qkv")
                xTc.give(xi, m)
                v = bank[:, 0:3 * HS].rearrange("p (a k) -> p a k", a=3)
                vc_done[t] = AC(act.copy, vc[b][:, j, 0:HS], bank[:, 3 * HS:], after=[m, c_one], sem="c_v")
                i1, a1, f1 = r1.take()
                i2, a2, f2 = r2.take()
                d = DV(vec.tensor_tensor, a1[:, :, :], v, rope_tab[:, 0, j, :].unsqueeze(1).to_broadcast([P, 3, HS]),
                       ALU.mult, after=[m, vc_done[t], ld_rope, *f1], sem="c_rot")
                for k in range(2):
                    d = DV(vec.tensor_tensor, a2[:, :, k::2], v[:, :, 1 - k::2],
                           rope_tab[:, 1, j, k::2].unsqueeze(1).to_broadcast([P, 3, HS // 2]), ALU.mult,
                           after=f2, sem="c_rot")
                banks.give(i, vc_done[t], d)
                g = GP(gps.tensor_tensor, a1[:, :, :], a1[:, :, :], a2[:, :, :], ALU.add, after=[d], sem="c_rotsum")
                r2.give(i2, g)
                yield
                i, bank, free = banks.take()
                for a in range(3):
                    m = PE(tr, bank[:, a * P:(a + 1) * P], a1[:, a, :], ident[:, :], after=[g, *free], sem="c_rT")
                r1.give(i1, m)
                qk_done[t] = AC(act.copy, qkT[b][:, :, j * P:(j + 1) * P],
                                bank[:, 0:3 * P].rearrange("p (a t) -> p a t", a=3), after=[m], sem="c_qkT")
                banks.give(i, qk_done[t])
                yield

            def causal(b, j):
                t = b * TPB + j
                oi, o, ofree = oc.take()
                nk = j + 1
                halves = [(lo, min(lo + 4, nk)) for lo in range(0, nk, 4)]
                for h in range(NKV):
                    mi, mb, mfree = mc.take()
                    sbk = []
                    for n, (lo, hi) in enumerate(halves):
                        i, bank, free = banks.take()
                        last = hi == nk
                        w = (hi - lo) * P
                        m = PE(mm, bank[:, 0:w], qkT[b][:, h, j * P:(j + 1) * P], qkT[b][:, 2, lo * P:hi * P],
                               start=True, stop=not last, after=[qk_done[t], *free], sem="c_s")
                        if last:
                            m = PE(mm, bank[:, w - P:w], identb[:, :], causal_mask[:, :], start=False, stop=True,
                                   after=[ld_const], sem="c_s")
                        d = DV(vec.reduce_max, mb[:, n:n + 1], bank[:, 0:w], AXX, after=[m, *mfree], sem="c_max")
                        sbk.append((i, bank, lo, w))
                    if len(halves) == 2:
                        d = DV(vec.tensor_tensor, mb[:, 0:1], mb[:, 0:1], mb[:, 1:2], ALU.max, after=[d], sem="c_max2")
                    d = DV(vec.tensor_scalar, mb[:, 2:3], mb[:, 0:1], -float(HS) ** -0.5, None, ALU.mult, after=[d],
                           sem="c_nmax")
                    pi, pb, pfree = pc.take()
                    for i, bank, lo, w in sbk:
                        e = AC(act.activation, pb[:, lo * P:lo * P + w], bank[:, 0:w], ACTF.Exp, bias=mb[:, 2:3],
                               scale=float(HS) ** -0.5, after=[d, *pfree], sem="c_exp")
                        banks.give(i, e)
                    mc.give(mi, e)
                    yield
                    ti, pt, tfree = pcT.take()
                    for n, (lo, hi) in enumerate(halves):
                        i, bank, free = banks.take()
                        for k in range(lo, hi):
                            m = PE(tr, bank[:, (k - lo) * P:(k - lo + 1) * P], pb[:, k * P:(k + 1) * P], ident[:, :],
                                   after=[e, *free], sem="c_pTT")
                        c = DV(vec.tensor_copy, pt[:, lo * P:hi * P], bank[:, 0:(hi - lo) * P], after=[m, *tfree],
                               sem="c_pT")
                        banks.give(i, c)
                    pc.give(pi, m)
                    yield
                    i, bank, free = banks.take()
                    for k in range(nk):
                        m = PE(mm, bank[:, 0:HS + 1], pt[:, k * P:(k + 1) * P], vc[b][:, k, :], start=(k == 0),
                               stop=(k == nk - 1), after=[c, vc_done[b * TPB + k], *free], sem="c_o")
                    pcT.give(ti, m)
                    mi, mb, mfree = mc.take()
                    d = DV(vec.reciprocal, mb[:, 3:4], bank[:, HS:HS + 1], after=[m, *mfree], sem="c_rden")
                    d = DV(vec.tensor_scalar, o[:, h, :], bank[:, 0:HS], mb[:, 3:4], None, ALU.mult,
                           after=[d, *ofree], sem="c_on")
                    mc.give(mi, d)
                    banks.give(i, d)
                    yield
                i, bank, free = banks.take()
                for h in range(NKV):
                    m = PE(tr, bank[:, h * P:(h + 1) * P], o[:, h, :], ident[:, :], after=[d, *free], sem="c_oTT")
                oc.give(oi, m)
                ci, ot, cfree = ocT.take()
                e = AC(act.copy, ot[:, :, :], bank[:, 0:NKV * P].rearrange("p (a t) -> p a t", a=NKV),
                       after=[m, *cfree], sem="c_oT")
                for h in range(NKV):
                    m = PE(mm, bank[:, 3 * P:4 * P], ot[:, h, :], wo1[:, h, :], start=(h == 0), stop=(h == NKV - 1),
                           after=[e], sem="c_wo")
                ocT.give(ci, m)
                res[t] = DV(vec.tensor_tensor, x[:, t, :], bank[:, 3 * P:4 * P], x[:, t, :], ALU.add,
                            after=[m, x_ready[t]], sem="c_res")
                banks.give(i, res[t])
                yield

            for b in range(NB):
                weave([rope(b, j) for j in range(TPB)], 2, 2)
                weave([causal(b, j) for j in range(TPB)], 2, 3)
                weave([layer_norm(b, res)], 1)

        region = ExitStack()
        with region:
            fence(done_all())
            fc = Ring([rb(f"d_fc{i}", [P, FF]) for i in range(3)])
            pj = Ring([rb(f"d_pj{i}", [P, FCH, D]) for i in range(3)])
            gate_w = rb("d_gate", [P, NE])
            ld_g = load(gate_w[:, :], T["gate_w"], "ld_gate")
            xTd = rb("d_xT", [P, NT, P])
            y = xin
            gate = rb("d_gates", [P, NT, NE])
            g1 = rb("d_g1", [P, NT, 1])
            cmp = rb("d_cmp", [P, NT, NE, NE])
            cmp2 = rb("d_cmp2", [P, NT, NE, NE])
            wsel = rb("d_w", [P, NT, NE])
            hid = Ring([rb(f"d_h{i}", [P, FCH, CHUNK]) for i in range(2)])

            xT_done = {}

            def logits(t):
                xT_done[t] = transposed(t, xTd[:, t, :], [], "d_xT")
                yield
                PE(mm, gbank[:, t * NE:(t + 1) * NE], xTd[:, t, :], gate_w[:, :], start=True, stop=True,
                   after=[xT_done[t], ld_g, *gfree], sem="d_logit")
                yield

            gi, gbank, gfree = banks.take()
            weave([logits(t) for t in range(NT)], 2, 1)
            lg = gbank[:, 0:NT * NE].rearrange("p (t e) -> p t e", e=NE)
            m = ("d_logit", sems["d_logit"].count)
            d = DV(vec.reduce_max, g1[:, :, 0], lg, AXX, after=[m], sem="d_gate")
            d = DV(vec.tensor_tensor, gate[:, :, :], lg, g1[:, :, :].to_broadcast([P, NT, NE]), ALU.subtract,
                   after=[d], sem="d_gate")
            banks.give(gi, d)
            a = AC(act.activation, gate[:, :, :], gate[:, :, :], ACTF.Exp, after=[d], sem="d_gexp")
            d = DV(vec.reduce_sum, g1[:, :, 0], gate[:, :, :], AXX, after=[a], sem="d_gate")
            d = DV(vec.reciprocal, g1[:, :, :], g1[:, :, :], after=[d], sem="d_gate")
            d = DV(vec.tensor_tensor, gate[:, :, :], gate[:, :, :], g1[:, :, :].to_broadcast([P, NT, NE]),
                   ALU.mult, after=[d], sem="d_gate")
            mine = gate[:, :, :].unsqueeze(3).to_broadcast([P, NT, NE, NE])
            other = gate[:, :, :].unsqueeze(2).to_broadcast([P, NT, NE, NE])
            d = DV(vec.tensor_tensor, cmp[:, :, :, :], other, mine, ALU.is_gt, after=[d], sem="d_rank")
            d = DV(vec.tensor_tensor, cmp2[:, :, :, :], other, mine, ALU.is_equal, after=[d], sem="d_rank")
            d = DV(vec.tensor_tensor, cmp2[:, :, :, :], cmp2[:, :, :, :],
                   lower[:, :, :].unsqueeze(1).to_broadcast([P, NT, NE, NE]), ALU.mult, after=[d, ld_const],
                   sem="d_rank")
            d = DV(vec.tensor_tensor, cmp[:, :, :, :], cmp[:, :, :, :], cmp2[:, :, :, :], ALU.add, after=[d],
                   sem="d_rank")
            d = DV(vec.reduce_sum, wsel[:, :, :], cmp[:, :, :, :], AXX, after=[d], sem="d_rank")
            d = DV(vec.tensor_scalar, wsel[:, :, :], wsel[:, :, :], float(TOPK) - 0.5, None, ALU.is_lt, after=[d],
                   sem="d_pick")
            d = DV(vec.tensor_tensor, wsel[:, :, :], wsel[:, :, :], gate[:, :, :], ALU.mult, after=[d],
                   sem="d_pick")
            d = DV(vec.reduce_sum, g1[:, :, 0], wsel[:, :, :], AXX, after=[d], sem="d_pick")
            d = DV(vec.reciprocal, g1[:, :, :], g1[:, :, :], after=[d], sem="d_pick")
            w_done = DV(vec.tensor_tensor, wsel[:, :, :], wsel[:, :, :], g1[:, :, :].to_broadcast([P, NT, NE]),
                        ALU.mult, after=[d], sem="d_pick")

            acc = dict(x_ready)

            def expert(e, n, wts):
                fi, fw, pjw, lf = wts
                hi_, hb, hfree = hid.take()
                tpc = CHUNK // P
                src = xTd[:, n * tpc:(n + 1) * tpc, :].rearrange("p a t -> p (a t)")
                for f in range(FCH):
                    i, bank, free = banks.take()
                    m = PE(mm, bank[:, :], fw[:, f * P:(f + 1) * P], src, start=True, stop=True,
                           after=[lf, xT_done[n * tpc + tpc - 1], *free], sem="d_fc")
                    a = AC(act.activation, hb[:, f, :], bank[:, :], ACTF.Gelu, after=[m, *hfree], sem="d_gelu")
                    banks.give(i, a)
                    yield
                i, bank, free = banks.take()
                for q in range(tpc):
                    for f in range(FCH):
                        m = PE(mm, bank[:, q * P:(q + 1) * P], hb[:, f, q * P:(q + 1) * P], pjw[:, f, :],
                               start=(f == 0), stop=(f == FCH - 1), after=[a, *free], sem="d_pj")
                    yield
                hid.give(hi_, m)
                if n == NT // tpc - 1:
                    fc.give(fi, m)
                    pj.give(fi, m)
                for q in range(tpc):
                    t = n * tpc + q
                    acc[t] = DV(vec.scalar_tensor_tensor, x[:, t, :], bank[:, q * P:(q + 1) * P], wsel[:, t, e:e + 1],
                                x[:, t, :], ALU.mult, ALU.add, after=[m, w_done, acc[t]], sem="d_acc")
                banks.give(i, acc[t])
                yield

            def weights(e):
                fi, fw, ffree = fc.take()
                _, pjw, pfree = pj.take()
                SP(sync.dma_start, fw[:, :], T["fc_w"][e], after=ffree, sem=f"ld_e{e}", by=16)
                lf = SP(sync.dma_start, pjw[:, :, :], T["proj_w"][e].rearrange("(f p) d -> p f d", p=P), after=pfree,
                        sem=f"ld_e{e}", by=16)
                return fi, fw, pjw, lf

            wts = {e: weights(e) for e in range(2)}
            for e in range(NE):
                if e + 2 < NE:
                    wts[e + 2] = weights(e + 2)
                weave([expert(e, n, wts[e]) for n in range(SEQ * NB // CHUNK)], 2, 5)
            for b in range(NB):
                weave([layer_norm(b, acc)], 1)
            stage_out()

        SP.wait(*done_all())
        block = ctx.enter_context(nc.Block())

        @block.sync
        def _(eng):
            SP.play(eng)

        @block.tensor
        def _(eng):
            PE.play(eng)

        @block.vector
        def _(eng):
            DV.play(eng)

        @block.scalar
        def _(eng):
            AC.play(eng)

        @block.gpsimd
        def _(eng):
            GP.play(eng)


_NAMES = {"x": "L0_attn_x", "Wq": "L0_attn_Wq", "Wk": "L0_attn_Wk", "Wv": "L0_attn_Wv", "Wout": "L0_attn_Wout",
          "wqkv": "L0_ffn_wqkv", "q_scale": "L0_ffn_q_scale", "k_scale": "L0_ffn_k_scale", "wo": "L0_ffn_wo",
          "ln_g": "L0_ffn_ln_g", "ln_b": "L0_ffn_ln_b", "w1": "L0_ffn_w1", "b1": "L0_ffn_b1", "w2": "L0_ffn_w2",
          "b2": "L0_ffn_b2", "gate_w": "L1_ffn_gate_w", "fc_w": "L1_ffn_fc_w", "proj_w": "L1_ffn_proj_w"}


def constants():
    import numpy as np
    bf16 = mybir.dt.np(BF16)
    f = np.float32
    c = {"c_ident": np.eye(P, dtype=f), "c_identb": np.eye(P).astype(bf16), "c_ones": np.ones((1, P), f),
         "c_augones": np.ones((SPLIT, H0 // 2, SEQ)).astype(bf16)}
    q, k = np.arange(P)[:, None], np.arange(KEYS)[None, :] - WIN
    seen = (k <= q) & (k >= q - WIN)
    both = np.stack([np.where(seen, 0.0, LOCAL_NEG), np.where(seen & (k >= 0), 0.0, LOCAL_NEG)], 1)
    c["c_local"] = np.repeat(both[:, :, None, :], 2, 2).astype(bf16)
    kk = np.arange(P)[None, :]
    c["c_causal"] = np.where(kk <= q, 0.0, NEG).astype(bf16)
    e = np.arange(NE)
    c["c_lower"] = np.broadcast_to((e[None, :] < e[:, None]).astype(f), (P, NE, NE)).copy()
    half = np.arange(0, DH1, 2, dtype=f)
    inv = (f(1.0) / f(10000.0) ** (half / f(DH1))).astype(f)
    t = np.arange(SEQ, dtype=f)
    fr = (t[:, None] * inv[None, :]).astype(f)
    fr = np.concatenate([fr, fr], -1)
    base = ((half + f(0.4 * DH1)) / f(1.4 * DH1)).astype(f)
    power = ((t - SEQ // 2) / f(WIN // 2)).astype(f)
    sc = (base[None, :] ** power[:, None]).astype(f)
    sc = np.concatenate([sc, sc], -1)
    cos, sin = np.cos(fr), np.sin(fr)
    sign = np.where(np.arange(DH1) < DH1 // 2, -1.0, 1.0).astype(f)
    tabs = np.stack([cos * sc, sin * sc * sign, cos / sc, sin / sc * sign])
    c["c_rot"] = np.ascontiguousarray(tabs.reshape(4, TPB, P, DH1).transpose(2, 0, 1, 3)).astype(f)
    pos = np.arange(0, HS, 2, dtype=f)
    theta = (f(10000.0) ** (f(-2.0) * pos / f(HS))).astype(f)
    an = (t[:, None] * theta[None, :]).astype(f)
    cs = np.repeat(np.cos(an), 2, 1)
    sn = np.stack([-np.sin(an), np.sin(an)], -1).reshape(SEQ, HS)
    c["c_rope"] = np.ascontiguousarray(np.stack([cs, sn]).reshape(2, TPB, P, HS).transpose(2, 0, 1, 3)).astype(f)
    return c


def lay_out(inputs):
    import numpy as np
    a = {name: np.ascontiguousarray(inputs[full]) for name, full in _NAMES.items()}
    a["Wq1T"] = np.ascontiguousarray(np.transpose(inputs["L1_attn_Wq"], (0, 2, 1)))
    for name, full in (("Wk1T", "L1_attn_Wk"), ("Wv1T", "L1_attn_Wv"), ("Wo1T", "L1_attn_Wo")):
        a[name] = np.ascontiguousarray(np.transpose(inputs[full]))
    return {**a, **constants()}


def kernel(**inputs):
    import numpy as np
    import concourse.bacc as bacc
    from concourse.bass_utils import run_bass_kernel_spmd as launch
    inputs = {k: np.asarray(v) for k, v in inputs.items()}
    arrays = {f"in_{k}": v for k, v in lay_out(inputs).items()}
    nc = bacc.Bacc("TRN2", target_bir_lowering=False, num_devices=1)
    T = {k[3:]: nc.dram_tensor(k, v.shape, mybir.dt.from_np(v.dtype), kind="ExternalInput").ap()
         for k, v in arrays.items()}
    T["out"] = nc.dram_tensor("out", (NB, SEQ, D), F32, kind="ExternalOutput").ap()
    program(nc, T)
    return launch(nc, [arrays], core_ids=[0]).results[0]["out"]
```

```python
import concourse.bass as bass
from concourse import mybir
from contextlib import ExitStack

F32 = mybir.dt.float32
BF16 = mybir.dt.bfloat16
ALU = mybir.AluOpType
ACTF = mybir.ActivationFunctionType
AXX = mybir.AxisListType.X

P = 128
D = 128
NB = 2
SEQ = 1024
TPB = SEQ // P
NT = NB * TPB
BANK = 512
NEG = -3.3895313892515355e38
LOCAL_NEG = -3e37
EPS = 1e-5

H0, DH0 = 16, 8
GH = 4
NG = H0 // GH
STRIP = 32
SPLIT = 3
QK_ROWS = SPLIT * SPLIT * DH0
AUG = QK_ROWS + SPLIT

DEPTH = 2
H1, DH1 = 8, 64
INNER = H1 * DH1
WIN = 64
HID = int(D * 4 * 2 / 3)
HCH = -(-HID // 3)
HIDC = [min(HCH, HID - c * HCH) for c in range(3)]
KEYS = WIN + P
QK_SCALE = 8.0

NKV, HS = 2, 128
NE, FF, TOPK = 8, 4 * D, 2
FCH = FF // P
CHUNK = 512


WIDTH, SKEW, OFFSET = 3, 9, 5


class Sem:

    def __init__(self, handle):
        self.handle, self.count = handle, 0


class Queue:

    def __init__(self, sems):
        self.items, self.reached, self.sems = [], {}, sems

    def __call__(self, method, *args, after=(), sem=None, by=1, **kw):
        for s, value in after:
            if value > self.reached.get(s, 0):
                self.reached[s] = value
                self.items.append((None, s, value, None))
        self.items.append((method, args, kw, (sem, by)))
        if sem is None:
            return None
        self.sems[sem].count += by
        return sem, self.sems[sem].count

    def wait(self, *after):
        for s, value in after:
            if value > self.reached.get(s, 0):
                self.reached[s] = value
                self.items.append((None, s, value, None))

    def play(self, eng):
        for method, a, kw, last in self.items:
            if method is None:
                eng.wait_ge(self.sems[a].handle, kw)
            else:
                ins = method(*a, **kw)
                if last[0] is not None:
                    ins.then_inc(self.sems[last[0]].handle, last[1])


class Ring:

    def __init__(self, bufs):
        self.bufs = bufs
        self.free = [[] for _ in bufs]
        self.order = list(range(len(bufs)))

    def take(self):
        i = self.order.pop(0)
        return i, self.bufs[i], self.free[i]

    def get(self):
        while not self.order:
            yield
        return self.take()

    def give(self, i, *after):
        self.free[i] = list(after)
        self.order.append(i)


def need(ready, key):
    while key not in ready:
        yield
    return ready[key]


def lane(gens, width, skew=1):
    gens = list(gens)
    live, turn, nxt = [], 0, 0
    while gens or live:
        if gens and len(live) < width and turn >= nxt:
            live.append(gens.pop(0))
            nxt = turn + skew
        for g in list(live):
            try:
                next(g)
            except StopIteration:
                live.remove(g)
        turn += 1
        yield


def weave(gens, width, skew=1):
    for _ in lane(gens, width, skew):
        pass


def program(nc, T):
    ctx = ExitStack()
    with ctx:
        names = {}

        def sb(name, shape, dt=F32):
            return ctx.enter_context(nc.sbuf_tensor(name, shape, dt))

        class Sems(dict):
            def __missing__(self, name):
                self[name] = Sem(ctx.enter_context(nc.semaphore(name)))
                return self[name]

        sems = Sems()
        PE, DV, AC, GP, SP = (Queue(sems) for _ in range(5))
        mm, tr = nc.tensor.matmul, nc.tensor.transpose
        vec, act, gps, sync = nc.vector, nc.scalar, nc.gpsimd, nc.sync
        banks = Ring([ctx.enter_context(nc.psum_tensor(f"bank{i}", [P, BANK], F32)) for i in range(8)])

        ident = sb("ident", [P, P])
        identb = sb("identb", [P, P], BF16)
        ones_row = sb("ones_row", [1, P])
        local_mask = sb("local_mask", [P, 2, 2, KEYS], BF16)
        causal_mask = sb("causal_mask", [P, P], BF16)
        lower = sb("lower", [P, NE, NE])

        x = sb("x", [P, NT, D])
        xin = sb("xin", [P, NT, D])

        def load(dst, src, sem):
            return SP(sync.dma_start, dst, src, sem=sem, by=16)

        ld_x = load(x[:, :, :], T["x"].rearrange("b (t p) d -> p (b t) d", p=P), "ld_x")
        ld_id = load(ident[:, :], T["c_ident"], "ld_ident")
        wqkv0 = sb("wqkv0", [P, 3, D])
        for j, n in enumerate(("Wq", "Wk", "Wv")):
            ld_w0 = load(wqkv0[:, j, :], T[n], "ld_w0")
        wout0 = sb("wout0", [P, D])
        ld_w0 = load(wout0[:, :], T["Wout"], "ld_w0")
        load(identb[:, :], T["c_identb"], "ld_const")
        load(ones_row[:, :], T["c_ones"], "ld_const")
        load(local_mask[:, :, :, :], T["c_local"], "ld_const")
        load(causal_mask[:, :], T["c_causal"], "ld_const")
        ld_const = load(lower[:, :, :], T["c_lower"], "ld_const")

        stat = Ring([sb(f"stat{i}", [P, 10]) for i in range(8)])
        minus_half = sb("minus_half", [P, 2 * H1])
        mh_ready = GP(gps.memset, minus_half[:, :], -0.5, sem="minus_half")

        x_ready = {t: ld_x for t in range(NT)}

        def transposed(t, dst, after, sem):
            i, bank, free = yield from banks.get()
            done = PE(tr, bank[:, 0:P], x[:, t, :], ident[:, :], after=[x_ready[t], ld_id, *free], sem="pe_xT")
            done = AC(act.copy, dst, bank[:, 0:P], after=[done, *after], sem=sem)
            banks.give(i, done)
            return done

        def deviation(src, after, st):
            d = DV(vec.bn_stats, st[:, 0:6], src, after=after, sem="ln_stat")
            read = d
            d = DV(vec.bn_aggr, st[:, 6:8], st[:, 0:6], after=[d], sem="ln_aggr")
            d = DV(vec.tensor_scalar, st[:, 9:10], st[:, 7:8], EPS, None, ALU.add, after=[d], sem="ln_eps")
            return read, GP(gps.tensor_tensor, st[:, 8:9], st[:, 9:10], minus_half[:, 0:1], ALU.pow,
                            after=[d, mh_ready], sem="ln_rstd")

        def layer_norm(t, done):
            si, st, free = yield from stat.get()
            _, r = deviation(x[:, t, :], [done, *free], st)
            yield
            x_ready[t] = DV(vec.tensor_scalar, x[:, t, :], x[:, t, :], st[:, 6:7], st[:, 8:9], ALU.subtract, ALU.mult,
                            after=[r], sem="ln_out")
            stat.give(si, x_ready[t])
            yield

        def stage_out():
            for b in range(NB):
                ts = slice(b * TPB, (b + 1) * TPB)
                o = SP(sync.dma_start, T["out"][b].rearrange("(t p) d -> p t d", p=P), x[:, ts, :],
                       after=[x_ready[t] for t in range(b * TPB, (b + 1) * TPB)], sem="store", by=16)
            SP.wait(o)

        def done_all():
            return [(name, s.count) for name, s in sems.items() if s.count]

        def fence(tokens):
            for q in (SP, GP, PE, DV, AC):
                q.wait(*tokens)

        region = ExitStack()
        with region:
            def rb(name, shape, dt=F32):
                return region.enter_context(nc.sbuf_tensor(name, shape, dt))

            xT = rb("a_xT", [P, SEQ])
            parts = [rb(f"a_parts{j}", [P, SPLIT, SEQ], BF16) for j in range(2)]
            rest = rb("a_rest", [P, 2, BANK])
            UH = H0 // 2
            aug = [[rb(f"a_aug{u}{j}", [AUG, UH, SEQ], BF16) for j in range(2)] for u in range(2)]
            vaug = [rb(f"a_v{b}", [P, TPB, H0, STRIP]) for b in range(NB)]
            probs = Ring([rb(f"a_p{i}", [P, BANK]) for i in range(9)])
            oT = rb("a_oT", [P, BANK])
            z = rb("a_z", [P, TPB, D])
            zT = rb("a_zT", [P, P])
            mx = [rb(f"a_mx{i}", [P, 2, GH * TPB]) for i in range(2)]
            nmax = rb("a_nmax", [P, GH * TPB])
            mrest = rb("a_mrest", [GH * TPB, P])
            mpart = rb("a_mpart", [GH * TPB, SPLIT, P], BF16)
            rden = rb("a_rden", [P, TPB // 2, GH])
            scratch = [nc.dram_tensor(f"a_scratch{j}", [NB, SPLIT, P, SEQ], BF16).ap() for j in range(2)]

            vz = [GP(gps.memset, vaug[b][:, :, :, :], 0.0, sem="vaug_zero") for b in range(NB)]
            vz = [GP(gps.memset, vaug[b][:, :, :, DH0:DH0 + 1], 1.0, after=[vz[b]], sem="vaug_one")
                  for b in range(NB)]
            for u in range(2):
                ld_ones = load(aug[u][1][QK_ROWS:AUG, :, :], T["c_augones"], "ld_augones")
            v_ready, sc_ready = {}, {}
            scratch_free = {}
            parts_free = []
            xT_free = []

            def project(b):
                nonlocal parts_free, xT_free
                ts = range(b * TPB, (b + 1) * TPB)
                for j, t in enumerate(ts):
                    xt = yield from transposed(t, xT[:, j * P:(j + 1) * P], xT_free, "a_xT")
                    yield
                last_mm = []
                for j in range(2):
                    for half in range(SEQ // BANK):
                        i, bank, free = banks.take()
                        cols = slice(half * BANK, (half + 1) * BANK)
                        m = PE(mm, bank[:, :], wqkv0[:, j, :], xT[:, cols], start=True, stop=True,
                               after=[xt, ld_w0, *free], sem="a_qk")
                        d = DV(vec.tensor_copy, parts[j][:, 0, cols], bank[:, :], after=[m, *parts_free], sem="a_split")
                        d = DV(vec.tensor_tensor, rest[:, half, :], bank[:, :], parts[j][:, 0, cols], ALU.subtract,
                               after=[d], sem="a_split")
                        banks.give(i, d)
                        d = DV(vec.tensor_copy, parts[j][:, 1, cols], rest[:, half, :], after=[d], sem="a_split")
                        d = DV(vec.tensor_tensor, parts[j][:, 2, cols], rest[:, half, :], parts[j][:, 1, cols],
                               ALU.subtract, after=[d], sem="a_split")
                        yield
                    sc_ready[b, j] = SP(sync.dma_start, scratch[j][b].rearrange("s p t -> p s t"), parts[j][:, :, :],
                                        after=[d], sem=f"scratch{b}{j}", by=16)
                parts_free = [sc_ready[b, 0], sc_ready[b, 1]]
                for j, t in enumerate(ts):
                    i, bank, free = banks.take()
                    m = PE(mm, bank[:, 0:D], xT[:, j * P:(j + 1) * P], wqkv0[:, 2, :], start=True, stop=True,
                           after=[xt, ld_w0, *free], sem="a_v")
                    v_ready[t] = AC(act.copy, vaug[b][:, j, :, 0:DH0],
                                    bank[:, 0:D].rearrange("p (h d) -> p h d", h=H0), after=[m, vz[b]], sem="a_vcopy")
                    banks.give(i, v_ready[t])
                    yield
                xT_free = [m]

            aug_ready = {}
            aug_free = {0: [], 1: []}

            def gather(b, u):
                for j in range(2):
                    for a in range(SPLIT):
                        for c in range(SPLIT):
                            row = (a * SPLIT + c) * DH0
                            src = scratch[j][b, (a, c)[j], u * UH * DH0:(u + 1) * UH * DH0, :]
                            aug_ready[b, u] = SP(sync.dma_start, aug[u][j][row:row + DH0, :, :],
                                                 src.rearrange("(h d) t -> d h t", d=DH0),
                                                 after=[sc_ready[b, j], *aug_free[u]], sem=f"gather{b}{u}", by=16)
                yield

            nmax_ready = {}
            mrow_free = []
            m_free = []

            def maxima(b, g):
                nonlocal mrow_free, m_free
                u = g // (NG // 2)
                mxb = mx[(b * NG + g) % 2]
                for hh in range(GH):
                    hu = (g * GH + hh) % UH
                    for qt in range(TPB):
                        for half in range(2):
                            i, bank, free = banks.take()
                            m = PE(mm, bank[:, :], aug[u][0][0:QK_ROWS, hu, qt * P:(qt + 1) * P],
                                   aug[u][1][0:QK_ROWS, hu, half * BANK:(half + 1) * BANK], start=True, stop=True,
                                   after=[aug_ready[b, u], *free], sem="a_smax")
                            c = hh * TPB + qt
                            d = DV(vec.reduce_max, mxb[:, half, c:c + 1], bank[:, :], AXX, after=[m], sem="a_max")
                            banks.give(i, d)
                            yield
                n = DV(vec.tensor_tensor, nmax[:, :], mxb[:, 0, :], mxb[:, 1, :], ALU.max, after=[d, *mrow_free],
                       sem="a_max2")
                i, bank, free = banks.take()
                m = PE(tr, bank[0:GH * TPB, 0:P], nmax[:, :], ident[:, :], after=[n, *free], sem="a_maxT")
                mrow_free = [m]
                d = DV(vec.tensor_scalar, mrest[:, :], bank[0:GH * TPB, 0:P], -1.0, None, ALU.mult, after=[m],
                       sem="a_mneg")
                banks.give(i, d)
                d = DV(vec.tensor_copy, mpart[:, 0, :], mrest[:, :], after=[d, *m_free], sem="a_msplit")
                d = DV(vec.tensor_tensor, mrest[:, :], mrest[:, :], mpart[:, 0, :], ALU.subtract, after=[d],
                       sem="a_msplit")
                d = DV(vec.tensor_copy, mpart[:, 1, :], mrest[:, :], after=[d], sem="a_msplit")
                d = DV(vec.tensor_tensor, mpart[:, 2, :], mrest[:, :], mpart[:, 1, :], ALU.subtract, after=[d],
                       sem="a_msplit")
                hu = (g * GH) % UH
                sem = f"mrows{b}{g}"
                for s in range(SPLIT):
                    dst = aug[u][0][QK_ROWS + s:QK_ROWS + s + 1, hu:hu + GH, :]
                    r = SP(sync.dma_start, dst.rearrange("a h (t q) -> a (h t) q", q=P), mpart[:, s, :],
                           after=[d], sem=sem, by=16)
                nmax_ready[b, g] = r
                m_free = [r]
                yield

            z_ready = {}
            oT_free, z_free, zT_free = [], [], []
            HEAD_TILES = TPB // 2

            def attend(b, g):
                nonlocal oT_free
                u = g // (NG // 2)
                scale = 1.0 / float(DH0) ** 0.5
                for half in range(2):
                    oi, obank, ofree = banks.take()
                    pend = []

                    def values(kt, tiles):
                        nonlocal ofree
                        for hh, (pi, pbuf, e) in enumerate(tiles):
                            h = g * GH + hh
                            m = PE(mm, obank[hh * STRIP:(hh + 1) * STRIP, :], vaug[b][:, kt, h, :], pbuf[:, :],
                                   start=(kt == 0), stop=(kt == TPB - 1), after=[e, v_ready[b * TPB + kt], *ofree],
                                   sem="a_pv")
                            probs.give(pi, m)
                        ofree = []
                        return m

                    for kt in range(TPB):
                        tiles = []
                        for hh in range(GH):
                            hu = (g * GH + hh) % UH
                            i, bank, free = banks.take()
                            m = PE(mm, bank[:, :], aug[u][1][:, hu, kt * P:(kt + 1) * P],
                                   aug[u][0][:, hu, half * BANK:(half + 1) * BANK], start=True, stop=True,
                                   after=[nmax_ready[b, g], ld_ones, *free], sem="a_sT")
                            pi, pbuf, pfree = probs.take()
                            e = AC(act.activation, pbuf[:, :], bank[:, :], ACTF.Exp, scale=scale, after=[m, *pfree],
                                   sem="a_exp")
                            banks.give(i, e)
                            tiles.append((pi, pbuf, e))
                            yield
                        if pend:
                            values(*pend)
                        pend = (kt, tiles)
                    m = values(*pend)
                    yield
                    e = AC(act.copy, oT[:, :], obank[:, :], after=[m, *oT_free], sem="a_oT")
                    banks.give(oi, e)
                    yield
                    i, bank, free = banks.take()
                    for q in range(HEAD_TILES):
                        m = PE(tr, bank[:, q * P:(q + 1) * P], oT[:, q * P:(q + 1) * P], ident[:, :], after=[e, *free],
                               sem="a_oTT")
                    oT_free = [m]
                    yield
                    o = bank[:, :].rearrange("p (q h c) -> p q h c", q=HEAD_TILES, h=GH)
                    d = DV(vec.reciprocal, rden[:, :, :], o[:, :, :, DH0], after=[m], sem="a_rden")
                    zz = z[:, half * HEAD_TILES:(half + 1) * HEAD_TILES, g * STRIP:(g + 1) * STRIP]
                    zz = zz.rearrange("p q (h c) -> p q h c", h=GH)
                    for q in range(HEAD_TILES):
                        d = DV(vec.tensor_tensor, zz[:, q], o[:, q, :, 0:DH0],
                               rden[:, q, :].unsqueeze(2).to_broadcast([P, GH, DH0]), ALU.mult,
                               after=[d, *z_free], sem="a_z")
                    banks.give(i, d)
                    z_ready[b] = d
                aug_free[u] = [("a_sT", sems["a_sT"].count), ("a_smax", sems["a_smax"].count)]

            def output(b):
                nonlocal z_free, zT_free
                out = {}
                for j in range(TPB):
                    t = b * TPB + j
                    i, bank, free = banks.take()
                    m = PE(tr, bank[:, 0:P], z[:, j, :], ident[:, :], after=[z_ready[b], *free], sem="a_zTT")
                    z_free = [m]
                    e = AC(act.copy, zT[:, :], bank[:, 0:P], after=[m, *zT_free], sem="a_zT")
                    m = PE(mm, bank[:, P:2 * P], zT[:, :], wout0[:, :], start=True, stop=True, after=[e], sem="a_out")
                    zT_free = [m]
                    out[t] = DV(vec.scalar_tensor_tensor, x[:, t, :], x[:, t, :], 2.0, bank[:, P:2 * P], ALU.mult,
                                ALU.add, after=[m], sem="a_res")
                    banks.give(i, out[t])
                    yield
                    yield from layer_norm(t, out[t])

            weave([project(0)], 1)
            weave([gather(0, 0)], 1)
            weave([gather(0, 1)], 1)
            groups = [(b, g) for b in range(NB) for g in range(NG)]
            weave([maxima(0, 0)], 1)
            extra = []
            for n, (b, g) in enumerate(groups):
                work = [attend(b, g)]
                if b == 0 and g == 0:
                    work.append(project(1))
                if n + 1 < len(groups):
                    nb, ng = groups[n + 1]
                    work.insert(0, maxima(nb, ng))
                weave(work, len(work), 0)
                if b + 1 < NB and g % 2 == 1:
                    weave([gather(b + 1, g // 2)], 1)
                if g == NG - 1:
                    weave([output(b)], 1)


        region = ExitStack()
        with region:
            fence(done_all())
            wqkv = [rb(f"b_wqkv{l}", [P, 3 * INNER]) for l in range(DEPTH)]
            wo = [rb(f"b_wo{l}", [P, INNER // P, D]) for l in range(DEPTH)]
            w1 = [rb(f"b_w1{l}", [P, 2 * HID]) for l in range(DEPTH)]
            w2 = [rb(f"b_w2{l}", [HCH, 3, D]) for l in range(DEPTH)]
            b1 = [rb(f"b_b1{l}", [HCH, 6]) for l in range(DEPTH)]
            ln = [rb(f"b_ln{l}", [P, 2]) for l in range(DEPTH)]
            scales = [rb(f"b_scales{l}", [P, 2, DH1]) for l in range(DEPTH)]
            ld_w = []
            for l in range(DEPTH):
                s = f"ld_layer{l}"
                load(wqkv[l][:, :], T["wqkv"][l], s)
                for j, n in enumerate(("q_scale", "k_scale")):
                    load(scales[l][:, j, :], T[n][l:l + 1, :].to_broadcast([P, DH1]), s)
                load(wo[l][:, :, :], T["wo"][l].rearrange("(c p) d -> p c d", p=P), s)
                load(w1[l][:, :], T["w1"][l], s)
                for c in range(3):
                    n = HIDC[c]
                    load(w2[l][0:n, c, :], T["w2"][l][c * HCH:c * HCH + n, :], s)
                    for j in range(2):
                        lo = j * HID + c * HCH
                        load(b1[l][0:n, 3 * j + c:3 * j + c + 1],
                             T["b1"][l:l + 1, lo:lo + n].rearrange("a n -> n a"), s)
                load(ln[l][:, 0:1], T["ln_g"][l:l + 1, :].rearrange("a n -> n a"), s)
                ld_w.append(load(ln[l][:, 1:2], T["ln_b"][l:l + 1, :].rearrange("a n -> n a"), s))

            rot = [rb(f"b_rot{l}", [P, 4, TPB, DH1]) for l in range(DEPTH)]
            b2b = [rb(f"b_b2b{l}", [P, D]) for l in range(DEPTH)]
            hTa = [rb(f"b_hTa{b}", [P, SEQ + 1]) for b in range(NB)]
            hTf = [rb(f"b_hTf{b}", [P, SEQ + 1]) for b in range(NB)]
            ring = lambda name, shape, n: Ring([rb(f"{name}{i}", shape) for i in range(n)])
            sq = ring("b_sq", [P, INNER], 2)
            t1 = ring("b_t1", [P, INNER], 2)
            t2 = ring("b_t2", [P, INNER], 2)
            ss = ring("b_ss", [P, 2 * H1], 6)
            rq = ring("b_r", [P, 2, INNER], 3)
            qT = ring("b_qT", [P, H1 // 2, P], 4)
            kT = [ring(f"b_kT{b}_", [P, H1 // 2, P], 4) for b in range(NB)]
            vv = [ring(f"b_vv{b}_", [P, H1, DH1 + 1], 5) for b in range(NB)]
            pp = ring("b_p", [P, 2, 2 * P], 6)
            pT = ring("b_pT", [P, 2, 2, P], 9)
            mxl = ring("b_mx", [P, 4], 6)
            rdl = ring("b_rd", [P, H1], 4)
            oo = ring("b_o", [P, INNER], 2)
            ooT = ring("b_oT", [P, INNER // P, P], 2)
            nn = ring("f_n", [P, D], 3)
            nT = ring("f_nT", [P, P], 3)
            gl = ring("f_g", [HCH, 3, P], 3)
            uT = ring("f_u", [HCH, 3, P], 3)
            for b in range(NB):
                GP(gps.memset, hTa[b][:, 0:1], 0.0, sem="b_zero")
                GP(gps.memset, hTf[b][:, 0:1], 0.0, sem="b_zero")
                for v in vv[b].bufs:
                    GP(gps.memset, v[:, :, DH1:DH1 + 1], 1.0, sem="b_zero")
            for p in pp.bufs:
                b_zero = GP(gps.memset, p[:, :, 0:WIN], 0.0, sem="b_zero")

            tables = []
            for l in range(DEPTH):
                tab_in = load(rot[l][:, :, :, :], T["c_rot"], f"ld_rot{l}")
                load(b2b[l][:, :], T["b2"][l:l + 1, :].to_broadcast([P, D]), f"ld_b2b{l}")
                half = DH1 // 2
                for j in range(2):
                    c, s, g = 2 * j, 2 * j + 1, scales[l][:, j, :]
                    for tab, lo, src in ((c, 0, g[:, 0:half]), (c, half, g[:, half:]), (s, 0, g[:, half:]),
                                         (s, half, g[:, 0:half])):
                        d = DV(vec.tensor_tensor, rot[l][:, tab, :, lo:lo + half], rot[l][:, tab, :, lo:lo + half],
                               src.unsqueeze(1).to_broadcast([P, TPB, half]), ALU.mult,
                               after=[tab_in, ld_w[l]], sem="b_fold")
                tables.append(d)
            ld_b2b = [(f"ld_b2b{l}", 16) for l in range(DEPTH)]

            hTa_free, hTf_free = {}, {}
            k_tile, v_tile = {}, {}

            def shifted(t, hT, free_of):
                j = t % TPB
                i, bank, free = yield from banks.get()
                m = PE(tr, bank[:, 0:P], x[:, t, :], ident[:, :], after=[x_ready[t], *free], sem="pe_xT")
                half = D // 2
                AC(act.copy, hT[0:half, j * P:(j + 1) * P], bank[0:half, 0:P], after=[m, b_zero, *free_of], sem="b_hT")
                h = AC(act.copy, hT[half:P, j * P + 1:(j + 1) * P + 1], bank[half:P, 0:P], sem="b_hT")
                banks.give(i, h)
                yield
                return h

            def local_layer(b, l, j):
                t = b * TPB + j
                done_before = (l, b, j - 1)
                nxt = min(j + 1, TPB - 1)
                h = yield from shifted(t, hTa[b], [hTa_free[b, l - 1, nxt]] if l else [])
                ri, r, rfree = yield from rq.get()
                si, sst, sfree = yield from ss.get()
                for part in range(2):
                    i, bank, free = yield from banks.get()
                    m = PE(mm, bank[:, :], hTa[b][:, j * P:(j + 1) * P], wqkv[l][:, part * INNER:(part + 1) * INNER],
                           start=True, stop=True, after=[h, ld_w[l], *free], sem="b_qkv")
                    qi, s, qfree = yield from sq.get()
                    a = AC(act.square, s[:, :], bank[:, :], after=[m, *qfree], sem="b_sq")
                    v = bank[:, :].rearrange("p (h d) -> p h d", h=H1)
                    half = DH1 // 2

                    def table(k, lo, n):
                        return rot[l][:, 2 * part + k, j, lo:lo + n].unsqueeze(1).to_broadcast([P, H1, n])
                    i1, a1, free1 = yield from t1.get()
                    i2, a2, free2 = yield from t2.get()
                    DV(vec.tensor_tensor, a1[:, :].rearrange("p (h d) -> p h d", h=H1), v, table(0, 0, DH1),
                       ALU.mult, after=[a, tables[l], *free1], sem="b_rot")
                    a2v = a2[:, :].rearrange("p (h d) -> p h d", h=H1)
                    DV(vec.tensor_tensor, a2v[:, :, 0:half], v[:, :, half:], table(1, 0, half), ALU.mult,
                       after=free2, sem="b_rot")
                    r2 = DV(vec.tensor_tensor, a2v[:, :, half:], v[:, :, 0:half], table(1, half, half), ALU.mult,
                            sem="b_rot")
                    banks.give(i, a, r2)
                    d = DV(vec.reduce_sum, sst[:, part * H1:(part + 1) * H1],
                           s[:, :].rearrange("p (h d) -> p h d", h=H1), AXX, after=[a, *sfree], sem="b_ss")
                    sq.give(qi, d)
                    g = GP(gps.tensor_tensor, r[:, part, :], a1[:, :], a2[:, :], ALU.add, after=[r2, *rfree],
                           sem="b_rotsum")
                    t1.give(i1, g)
                    t2.give(i2, g)
                    yield
                d = DV(vec.tensor_scalar, sst[:, :], sst[:, :], 1e-24, None, ALU.max, after=[d], sem="b_clip")
                d = GP(gps.tensor_tensor, sst[:, :], sst[:, :], minus_half[:, :], ALU.pow, after=[d, mh_ready],
                       sem="b_rn")
                i, bank, free = yield from banks.get()
                m = PE(mm, bank[:, :], hTa[b][:, j * P:(j + 1) * P], wqkv[l][:, 2 * INNER:], start=True, stop=True,
                       after=free, sem="b_qkv")
                hTa_free[b, l, j] = m
                vi, vb, vfree = yield from vv[b].get()
                e = AC(act.copy, vb[:, :, 0:DH1], bank[:, :].rearrange("p (h d) -> p h d", h=H1),
                       after=[m, b_zero, *vfree], sem="b_v")
                banks.give(i, e)
                v_tile[b, l, j] = (vi, vb, e)
                yield
                rv = r[:, :, :].rearrange("p a (h d) -> p (a h) d", h=H1)
                d = DV(vec.tensor_tensor, rv, rv, sst[:, :].unsqueeze(2).to_broadcast([P, 2 * H1, DH1]),
                       ALU.mult, after=[d, g], sem="b_scale")
                ss.give(si, d)
                yield
                ki, kb, kfree = yield from kT[b].get()
                qi, qb, qfree = yield from qT.get()
                for part in range(2):
                    i, bank, free = yield from banks.get()
                    for c in range(INNER // P):
                        m = PE(tr, bank[:, c * P:(c + 1) * P], r[:, part, c * P:(c + 1) * P], ident[:, :],
                               after=[d, *free], sem="b_qkT")
                    e = AC(act.copy, (qb, kb)[part][:, :, :], bank[:, :].rearrange("p (c t) -> p c t", t=P),
                           after=[m, *(qfree, kfree)[part]], sem="b_qkTc")
                    banks.give(i, e)
                    yield
                rq.give(ri, m)
                k_tile[b, l, j] = (ki, kb, e)
                if j:
                    pki, pkb, pke = yield from need(k_tile, (b, l, j - 1))
                    pvi, pvb, pve = yield from need(v_tile, (b, l, j - 1))
                pts = {}
                last = None
                for grp in range(2):
                    b0 = yield from banks.get()
                    b1_ = yield from banks.get()
                    held = (b0, b1_)
                    xi, mxb, mfree = yield from mxl.get()
                    for i, bank, free in held:
                        PE(mm, bank[:, 0:2 * KEYS], identb[:, :],
                           local_mask[:, 0 if j else 1, :, :].rearrange("p a k -> p (a k)"), start=True, stop=False,
                           after=[ld_const, *free])
                    for p2 in range(2):
                        p = 2 * grp + p2
                        if j:
                            for hp in range(2):
                                rows = slice(hp * DH1, (hp + 1) * DH1)
                                PE(mm, held[hp][1][:, p2 * KEYS:p2 * KEYS + WIN], qb[rows, p, :],
                                   pkb[rows, p, P - WIN:], start=False, stop=False, after=[e, pke])
                        for hp in range(2):
                            rows = slice(hp * DH1, (hp + 1) * DH1)
                            m = PE(mm, held[hp][1][:, p2 * KEYS + WIN:(p2 + 1) * KEYS], qb[rows, p, :], kb[rows, p, :],
                                   start=False, stop=(p2 == 1), after=[e], sem="b_s")
                            if p2:
                                d = DV(vec.reduce_max, mxb[:, 2 * hp:2 * hp + 2],
                                       held[hp][1][:, 0:2 * KEYS].rearrange("p (a k) -> p a k", a=2), AXX,
                                       after=[m, *mfree], sem="b_max")
                    d = DV(vec.tensor_scalar, mxb[:, :], mxb[:, :], -QK_SCALE, None, ALU.mult, after=[d],
                           sem="b_nmax")
                    yield
                    for p2 in range(2):
                        p = 2 * grp + p2
                        pi, pb, pfree = yield from pp.get()
                        for hp in range(2):
                            i, bank, _ = held[hp]
                            x_ = AC(act.activation, pb[:, hp, WIN:], bank[:, p2 * KEYS:(p2 + 1) * KEYS], ACTF.Exp,
                                    bias=mxb[:, 2 * hp + p2:2 * hp + p2 + 1], scale=QK_SCALE,
                                    after=[d, b_zero, *pfree], sem="b_exp")
                            if p2:
                                banks.give(i, x_)
                        if p2:
                            mxl.give(xi, x_)
                        yield
                        i, bank, free = yield from banks.get()
                        for k in range(4):
                            m = PE(tr, bank[:, k * P:(k + 1) * P], pb[:, k // 2, (k % 2) * P:(k % 2 + 1) * P],
                                   ident[:, :], after=[x_, *free], sem="b_pT")
                        pp.give(pi, m)
                        ti, pt, tfree = yield from pT.get()
                        dst = pt[:, :, :, :].rearrange("p a c q -> p (a c q)")
                        if p % 2:
                            c = AC(act.copy, dst, bank[:, :], after=[m, *tfree], sem="b_pTa")
                        else:
                            c = DV(vec.tensor_copy, dst, bank[:, :], after=[m, *tfree], sem="b_pTd")
                        banks.give(i, c)
                        pts[p] = (ti, pt, c)
                        yield
                qT.give(qi, ("b_s", sems["b_s"].count))
                if j:
                    kT[b].give(pki, ("b_s", sems["b_s"].count))
                if j == TPB - 1:
                    kT[b].give(ki, ("b_s", sems["b_s"].count))
                rdi, rd, rdfree = yield from rdl.get()
                oi, o, ofree = yield from oo.get()
                for q in range(2):
                    i, bank, free = yield from banks.get()
                    for h4 in range(4):
                        h_ = 4 * q + h4
                        ti, pt, c = pts[h_ // 2]
                        out = bank[:, h4 * (DH1 + 1):(h4 + 1) * (DH1 + 1)]
                        vi, vb, ve = v_tile[b, l, j]
                        if j:
                            PE(mm, out, pt[P - WIN:, h_ % 2, 0, :], pvb[P - WIN:, h_, :], start=True, stop=False,
                               after=[c, pve, *free])
                        m = PE(mm, out, pt[:, h_ % 2, 1, :], vb[:, h_, :], start=(j == 0), stop=True,
                               after=[c, ve, *free], sem="b_o")
                        if h_ % 2:
                            pT.give(ti, m)
                    bv = bank[:, 0:4 * (DH1 + 1)].rearrange("p (h d) -> p h d", h=4)
                    d = DV(vec.reciprocal, rd[:, 4 * q:4 * q + 4], bv[:, :, DH1], after=[m, *rdfree], sem="b_rden")
                    d = DV(vec.tensor_tensor, o[:, 4 * q * DH1:4 * (q + 1) * DH1].rearrange("p (h d) -> p h d", h=4),
                           bv[:, :, 0:DH1], rd[:, 4 * q:4 * q + 4].unsqueeze(2).to_broadcast([P, 4, DH1]), ALU.mult,
                           after=[d, *ofree], sem="b_on")
                    banks.give(i, d)
                    yield
                rdl.give(rdi, d)
                if j:
                    vv[b].give(pvi, m)
                if j == TPB - 1:
                    vv[b].give(vi, m)
                i, bank, free = yield from banks.get()
                for c in range(INNER // P):
                    m = PE(tr, bank[:, c * P:(c + 1) * P], o[:, c * P:(c + 1) * P], ident[:, :], after=[d, *free],
                           sem="b_oTT")
                oo.give(oi, m)
                ci, ot, cfree = yield from ooT.get()
                e = AC(act.copy, ot[:, :, :].rearrange("p c t -> p (c t)"), bank[:, :], after=[m, *cfree], sem="b_oT")
                banks.give(i, e)
                yield
                i, bank, free = yield from banks.get()
                for c in range(INNER // P):
                    m = PE(mm, bank[:, 0:D], ot[:, c, :], wo[l][:, c, :], start=(c == 0), stop=(c == INNER // P - 1),
                           after=[e, *free], sem="b_wo" if c == INNER // P - 1 else None)
                ooT.give(ci, m)
                x_ready[t] = DV(vec.tensor_tensor, x[:, t, :], bank[:, 0:D], x[:, t, :], ALU.add,
                                after=[m, x_free[t]], sem="b_res")
                banks.give(i, x_ready[t])
                yield
                h = yield from shifted(t, hTf[b], [hTf_free[b, l - 1, nxt]] if l else [])
                xb = GP(gps.tensor_tensor, x[:, t, :], x[:, t, :], b2b[l][:, :], ALU.add,
                        after=[("pe_xT", sems["pe_xT"].count), x_ready[t], ld_b2b[l]], sem="f_b2")
                x_ready[t] = xb
                i, bank, free = yield from banks.get()
                m = PE(tr, bank[:, 0:P], hTf[b][:, j * P:(j + 1) * P], ident[:, :], after=[h, *free], sem="f_hh")
                hTf_free[b, l, j] = m
                si, st, sfree = yield from stat.get()
                _, r_ = deviation(bank[:, 0:P], [m, *sfree], st)
                yield
                ni, nb_, nfree = yield from nn.get()
                d = DV(vec.tensor_scalar, nb_[:, :], bank[:, 0:P], st[:, 6:7], st[:, 8:9], ALU.subtract, ALU.mult,
                       after=[r_, *nfree], sem="f_n")
                banks.give(i, d)
                stat.give(si, d)
                yield
                i, bank, free = yield from banks.get()
                m = PE(tr, bank[:, 0:P], nb_[:, :], ident[:, :], after=[d, *free], sem="f_nTT")
                nn.give(ni, m)
                ni, nt, nfree = yield from nT.get()
                n_ = DV(vec.tensor_scalar, nt[:, :], bank[:, 0:P], ln[l][:, 0:1], ln[l][:, 1:2], ALU.mult, ALU.add,
                        after=[m, *nfree], sem="f_nT")
                banks.give(i, n_)
                yield
                gi, gbank, free = yield from banks.get()
                for c in range(3):
                    n = HIDC[c]
                    lo = HID + c * HCH
                    m = PE(mm, gbank[0:n, c * P:(c + 1) * P], w1[l][:, lo:lo + n], nt[:, :], start=True, stop=True,
                           after=[n_, *free], sem="f_w1")
                ai, abank, free = yield from banks.get()
                for c in range(3):
                    n = HIDC[c]
                    lo = c * HCH
                    ma = PE(mm, abank[0:n, c * P:(c + 1) * P], w1[l][:, lo:lo + n], nt[:, :], start=True, stop=True,
                            after=free, sem="f_w1")
                nT.give(ni, ma)
                ggi, gb, gfree = yield from gl.get()
                for c in range(3):
                    n = HIDC[c]
                    a = AC(act.activation, gb[0:n, c, :], gbank[0:n, c * P:(c + 1) * P], ACTF.Gelu,
                           bias=b1[l][0:n, 3 + c:4 + c], scale=1.0, after=[m, *gfree], sem="f_gelu")
                banks.give(gi, a)
                yield
                ui, u, ufree = yield from uT.get()
                for c in range(3):
                    n = HIDC[c]
                    d = DV(vec.scalar_tensor_tensor, u[0:n, c, :], abank[0:n, c * P:(c + 1) * P], b1[l][0:n, c:c + 1],
                           gb[0:n, c, :], ALU.add, ALU.mult, after=[ma, a, *ufree], sem="f_u")
                banks.give(ai, d)
                gl.give(ggi, d)
                yield
                i, bank, free = yield from banks.get()
                for c in range(3):
                    n = HIDC[c]
                    m = PE(mm, bank[:, 0:D], u[0:n, c, :], w2[l][0:n, c, :], start=(c == 0), stop=(c == 2),
                           after=[d, *free], sem="f_w2" if c == 2 else None)
                uT.give(ui, m)
                x_ready[t] = DV(vec.tensor_tensor, x[:, t, :], bank[:, 0:D], x[:, t, :], ALU.add,
                                after=[m, xb], sem="f_res")
                banks.give(i, x_ready[t])
                yield
                if l == DEPTH - 1:
                    d = DV(vec.tensor_tensor, x[:, t, :], x[:, t, :], xin[:, t, :], ALU.add, after=[x_ready[t], kept],
                           sem="b_add")
                    yield from layer_norm(t, d)

            for t in range(NT):
                done = GP(gps.tensor_copy, xin[:, t, :], x[:, t, :], after=[x_ready[t]], sem="b_keep")
            kept = done
            x_free = {t: kept for t in range(NT)}
            weave([lane([local_layer(b, l, j) for l in range(DEPTH) for j in range(TPB)], WIDTH, SKEW)
                   for b in range(NB)], NB, OFFSET)

        region = ExitStack()
        with region:
            fence(done_all())
            wq1 = rb("c_wqkv", [P, 4, HS])
            wo1 = rb("c_wo", [P, NKV, D])
            for j in range(NKV):
                load(wq1[:, j, :], T["Wq1T"][j], "ld_c")
                load(wo1[:, j, :], T["Wo1T"][j * P:(j + 1) * P, :], "ld_c")
            load(wq1[:, 2, :], T["Wk1T"], "ld_c")
            ld_c = load(wq1[:, 3, :], T["Wv1T"], "ld_c")
            rope_tab = rb("c_rope", [P, 2, TPB, HS])
            ld_rope = load(rope_tab[:, :, :, :], T["c_rope"], "ld_rope")
            xTc = Ring([rb(f"c_xT{i}", [P, P]) for i in range(2)])
            r1 = Ring([rb(f"c_r1{i}", [P, 3, HS]) for i in range(2)])
            r2 = Ring([rb(f"c_r2{i}", [P, 3, HS]) for i in range(2)])
            qkT = [rb(f"c_qkT{b}", [P, 3, SEQ]) for b in range(NB)]
            vc = [rb(f"c_v{b}", [P, TPB, HS + 1]) for b in range(NB)]
            pc = Ring([rb(f"c_p{i}", [P, SEQ]) for i in range(3)])
            pcT = Ring([rb(f"c_pT{i}", [P, SEQ]) for i in range(3)])
            mc = Ring([rb(f"c_m{i}", [P, 4]) for i in range(4)])
            oc = Ring([rb(f"c_o{i}", [P, NKV, HS]) for i in range(2)])
            ocT = Ring([rb(f"c_oT{i}", [P, NKV, P]) for i in range(2)])
            for b in range(NB):
                c_one = GP(gps.memset, vc[b][:, :, HS:HS + 1], 1.0, sem="c_one")
            qk_done, vc_done, res = {}, {}, {}

            def rope(b, j):
                t = b * TPB + j
                xi, xt, xfree = yield from xTc.get()
                e = yield from transposed(t, xt[:, :], xfree, "c_xT")
                yield
                i, bank, free = yield from banks.get()
                m = PE(mm, bank[:, :], xt[:, :], wq1[:, :, :].rearrange("p a k -> p (a k)"), start=True, stop=True,
                       after=[e, ld_c, *free], sem="c_qkv")
                xTc.give(xi, m)
                v = bank[:, 0:3 * HS].rearrange("p (a k) -> p a k", a=3)
                vc_done[t] = AC(act.copy, vc[b][:, j, 0:HS], bank[:, 3 * HS:], after=[m, c_one], sem="c_v")
                i1, a1, f1 = yield from r1.get()
                i2, a2, f2 = yield from r2.get()
                d = DV(vec.tensor_tensor, a1[:, :, :], v, rope_tab[:, 0, j, :].unsqueeze(1).to_broadcast([P, 3, HS]),
                       ALU.mult, after=[m, vc_done[t], ld_rope, *f1], sem="c_rot")
                for k in range(2):
                    d = DV(vec.tensor_tensor, a2[:, :, k::2], v[:, :, 1 - k::2],
                           rope_tab[:, 1, j, k::2].unsqueeze(1).to_broadcast([P, 3, HS // 2]), ALU.mult,
                           after=f2, sem="c_rot")
                banks.give(i, vc_done[t], d)
                g = GP(gps.tensor_tensor, a1[:, :, :], a1[:, :, :], a2[:, :, :], ALU.add, after=[d], sem="c_rotsum")
                r2.give(i2, g)
                yield
                i, bank, free = yield from banks.get()
                for a in range(3):
                    m = PE(tr, bank[:, a * P:(a + 1) * P], a1[:, a, :], ident[:, :], after=[g, *free], sem="c_rT")
                r1.give(i1, m)
                qk_done[t] = AC(act.copy, qkT[b][:, :, j * P:(j + 1) * P],
                                bank[:, 0:3 * P].rearrange("p (a t) -> p a t", a=3), after=[m], sem="c_qkT")
                banks.give(i, qk_done[t])
                yield

            def causal(b, j):
                t = b * TPB + j
                oi, o, ofree = yield from oc.get()
                nk = j + 1
                halves = [(lo, min(lo + 4, nk)) for lo in range(0, nk, 4)]
                for h in range(NKV):
                    mi, mb, mfree = yield from mc.get()
                    sbk = []
                    for n, (lo, hi) in enumerate(halves):
                        i, bank, free = yield from banks.get()
                        last = hi == nk
                        w = (hi - lo) * P
                        m = PE(mm, bank[:, 0:w], qkT[b][:, h, j * P:(j + 1) * P], qkT[b][:, 2, lo * P:hi * P],
                               start=True, stop=not last, after=[qk_done[t], *free], sem="c_s")
                        if last:
                            m = PE(mm, bank[:, w - P:w], identb[:, :], causal_mask[:, :], start=False, stop=True,
                                   after=[ld_const], sem="c_s")
                        d = DV(vec.reduce_max, mb[:, n:n + 1], bank[:, 0:w], AXX, after=[m, *mfree], sem="c_max")
                        sbk.append((i, bank, lo, w))
                    if len(halves) == 2:
                        d = DV(vec.tensor_tensor, mb[:, 0:1], mb[:, 0:1], mb[:, 1:2], ALU.max, after=[d], sem="c_max2")
                    d = DV(vec.tensor_scalar, mb[:, 2:3], mb[:, 0:1], -float(HS) ** -0.5, None, ALU.mult, after=[d],
                           sem="c_nmax")
                    pi, pb, pfree = yield from pc.get()
                    for i, bank, lo, w in sbk:
                        e = AC(act.activation, pb[:, lo * P:lo * P + w], bank[:, 0:w], ACTF.Exp, bias=mb[:, 2:3],
                               scale=float(HS) ** -0.5, after=[d, *pfree], sem="c_exp")
                        banks.give(i, e)
                    mc.give(mi, e)
                    yield
                    ti, pt, tfree = yield from pcT.get()
                    for n, (lo, hi) in enumerate(halves):
                        i, bank, free = yield from banks.get()
                        for k in range(lo, hi):
                            m = PE(tr, bank[:, (k - lo) * P:(k - lo + 1) * P], pb[:, k * P:(k + 1) * P], ident[:, :],
                                   after=[e, *free], sem="c_pTT")
                        c = DV(vec.tensor_copy, pt[:, lo * P:hi * P], bank[:, 0:(hi - lo) * P], after=[m, *tfree],
                               sem="c_pT")
                        banks.give(i, c)
                    pc.give(pi, m)
                    yield
                    i, bank, free = yield from banks.get()
                    for k in range(nk):
                        m = PE(mm, bank[:, 0:HS + 1], pt[:, k * P:(k + 1) * P], vc[b][:, k, :], start=(k == 0),
                               stop=(k == nk - 1), after=[c, vc_done[b * TPB + k], *free], sem="c_o")
                    pcT.give(ti, m)
                    mi, mb, mfree = yield from mc.get()
                    d = DV(vec.reciprocal, mb[:, 3:4], bank[:, HS:HS + 1], after=[m, *mfree], sem="c_rden")
                    d = DV(vec.tensor_scalar, o[:, h, :], bank[:, 0:HS], mb[:, 3:4], None, ALU.mult,
                           after=[d, *ofree], sem="c_on")
                    mc.give(mi, d)
                    banks.give(i, d)
                    yield
                i, bank, free = yield from banks.get()
                for h in range(NKV):
                    m = PE(tr, bank[:, h * P:(h + 1) * P], o[:, h, :], ident[:, :], after=[d, *free], sem="c_oTT")
                oc.give(oi, m)
                ci, ot, cfree = yield from ocT.get()
                e = AC(act.copy, ot[:, :, :], bank[:, 0:NKV * P].rearrange("p (a t) -> p a t", a=NKV),
                       after=[m, *cfree], sem="c_oT")
                for h in range(NKV):
                    m = PE(mm, bank[:, 3 * P:4 * P], ot[:, h, :], wo1[:, h, :], start=(h == 0), stop=(h == NKV - 1),
                           after=[e], sem="c_wo")
                ocT.give(ci, m)
                res[t] = DV(vec.tensor_tensor, x[:, t, :], bank[:, 3 * P:4 * P], x[:, t, :], ALU.add,
                            after=[m, x_ready[t]], sem="c_res")
                banks.give(i, res[t])
                yield
                yield from layer_norm(t, res[t])

            def causal_stream(b):
                yield from lane([rope(b, j) for j in range(TPB)], 2, 2)
                yield from lane([causal(b, j) for j in range(TPB)], 2, 5)

            weave([causal_stream(b) for b in range(NB)], NB, 3)

        region = ExitStack()
        with region:
            fence(done_all())
            fc = Ring([rb(f"d_fc{i}", [P, FF]) for i in range(3)])
            pj = Ring([rb(f"d_pj{i}", [P, FCH, D]) for i in range(3)])
            gate_w = rb("d_gate", [P, NE])
            ld_g = load(gate_w[:, :], T["gate_w"], "ld_gate")
            xTd = rb("d_xT", [P, NT, P])
            y = xin
            gate = rb("d_gates", [P, NT, NE])
            g1 = rb("d_g1", [P, NT, 1])
            cmp = rb("d_cmp", [P, NT, NE, NE])
            cmp2 = rb("d_cmp2", [P, NT, NE, NE])
            wsel = rb("d_w", [P, NT, NE])
            hid = Ring([rb(f"d_h{i}", [P, FCH, CHUNK]) for i in range(2)])

            xT_done = {}

            def logits(t):
                xT_done[t] = yield from transposed(t, xTd[:, t, :], [], "d_xT")
                yield
                PE(mm, gbank[:, t * NE:(t + 1) * NE], xTd[:, t, :], gate_w[:, :], start=True, stop=True,
                   after=[xT_done[t], ld_g, *gfree], sem="d_logit")
                yield

            gi, gbank, gfree = banks.take()
            weave([logits(t) for t in range(NT)], 2, 1)
            lg = gbank[:, 0:NT * NE].rearrange("p (t e) -> p t e", e=NE)
            m = ("d_logit", sems["d_logit"].count)
            d = DV(vec.reduce_max, g1[:, :, 0], lg, AXX, after=[m], sem="d_gate")
            d = DV(vec.tensor_tensor, gate[:, :, :], lg, g1[:, :, :].to_broadcast([P, NT, NE]), ALU.subtract,
                   after=[d], sem="d_gate")
            banks.give(gi, d)
            a = AC(act.activation, gate[:, :, :], gate[:, :, :], ACTF.Exp, after=[d], sem="d_gexp")
            d = DV(vec.reduce_sum, g1[:, :, 0], gate[:, :, :], AXX, after=[a], sem="d_gate")
            d = DV(vec.reciprocal, g1[:, :, :], g1[:, :, :], after=[d], sem="d_gate")
            d = DV(vec.tensor_tensor, gate[:, :, :], gate[:, :, :], g1[:, :, :].to_broadcast([P, NT, NE]),
                   ALU.mult, after=[d], sem="d_gate")
            mine = gate[:, :, :].unsqueeze(3).to_broadcast([P, NT, NE, NE])
            other = gate[:, :, :].unsqueeze(2).to_broadcast([P, NT, NE, NE])
            d = DV(vec.tensor_tensor, cmp[:, :, :, :], other, mine, ALU.is_gt, after=[d], sem="d_rank")
            d = DV(vec.tensor_tensor, cmp2[:, :, :, :], other, mine, ALU.is_equal, after=[d], sem="d_rank")
            d = DV(vec.tensor_tensor, cmp2[:, :, :, :], cmp2[:, :, :, :],
                   lower[:, :, :].unsqueeze(1).to_broadcast([P, NT, NE, NE]), ALU.mult, after=[d, ld_const],
                   sem="d_rank")
            d = DV(vec.tensor_tensor, cmp[:, :, :, :], cmp[:, :, :, :], cmp2[:, :, :, :], ALU.add, after=[d],
                   sem="d_rank")
            d = DV(vec.reduce_sum, wsel[:, :, :], cmp[:, :, :, :], AXX, after=[d], sem="d_rank")
            d = DV(vec.tensor_scalar, wsel[:, :, :], wsel[:, :, :], float(TOPK) - 0.5, None, ALU.is_lt, after=[d],
                   sem="d_pick")
            d = DV(vec.tensor_tensor, wsel[:, :, :], wsel[:, :, :], gate[:, :, :], ALU.mult, after=[d],
                   sem="d_pick")
            d = DV(vec.reduce_sum, g1[:, :, 0], wsel[:, :, :], AXX, after=[d], sem="d_pick")
            d = DV(vec.reciprocal, g1[:, :, :], g1[:, :, :], after=[d], sem="d_pick")
            w_done = DV(vec.tensor_tensor, wsel[:, :, :], wsel[:, :, :], g1[:, :, :].to_broadcast([P, NT, NE]),
                        ALU.mult, after=[d], sem="d_pick")

            acc = dict(x_ready)

            def expert(e, n, wts):
                fi, fw, pjw, lf = wts
                hi_, hb, hfree = hid.take()
                tpc = CHUNK // P
                src = xTd[:, n * tpc:(n + 1) * tpc, :].rearrange("p a t -> p (a t)")
                for f in range(FCH):
                    i, bank, free = banks.take()
                    m = PE(mm, bank[:, :], fw[:, f * P:(f + 1) * P], src, start=True, stop=True,
                           after=[lf, xT_done[n * tpc + tpc - 1], *free], sem="d_fc")
                    a = AC(act.activation, hb[:, f, :], bank[:, :], ACTF.Gelu, after=[m, *hfree], sem="d_gelu")
                    banks.give(i, a)
                    yield
                i, bank, free = banks.take()
                for q in range(tpc):
                    for f in range(FCH):
                        m = PE(mm, bank[:, q * P:(q + 1) * P], hb[:, f, q * P:(q + 1) * P], pjw[:, f, :],
                               start=(f == 0), stop=(f == FCH - 1), after=[a, *free], sem="d_pj")
                    yield
                hid.give(hi_, m)
                if n == NT // tpc - 1:
                    fc.give(fi, m)
                    pj.give(fi, m)
                for q in range(tpc):
                    t = n * tpc + q
                    acc[t] = DV(vec.scalar_tensor_tensor, x[:, t, :], bank[:, q * P:(q + 1) * P], wsel[:, t, e:e + 1],
                                x[:, t, :], ALU.mult, ALU.add, after=[m, w_done, acc[t]], sem="d_acc")
                banks.give(i, acc[t])
                yield

            def weights(e):
                fi, fw, ffree = fc.take()
                _, pjw, pfree = pj.take()
                SP(sync.dma_start, fw[:, :], T["fc_w"][e], after=ffree, sem=f"ld_e{e}", by=16)
                lf = SP(sync.dma_start, pjw[:, :, :], T["proj_w"][e].rearrange("(f p) d -> p f d", p=P), after=pfree,
                        sem=f"ld_e{e}", by=16)
                return fi, fw, pjw, lf

            wts = {e: weights(e) for e in range(2)}
            for e in range(NE):
                if e + 2 < NE:
                    wts[e + 2] = weights(e + 2)
                weave([expert(e, n, wts[e]) for n in range(SEQ * NB // CHUNK)], 2, 5)
            weave([layer_norm(t, acc[t]) for t in range(NT)], 4, 1)
            stage_out()

        SP.wait(*done_all())
        block = ctx.enter_context(nc.Block())

        @block.sync
        def _(eng):
            SP.play(eng)

        @block.tensor
        def _(eng):
            PE.play(eng)

        @block.vector
        def _(eng):
            DV.play(eng)

        @block.scalar
        def _(eng):
            AC.play(eng)

        @block.gpsimd
        def _(eng):
            GP.play(eng)


_NAMES = {"x": "L0_attn_x", "Wq": "L0_attn_Wq", "Wk": "L0_attn_Wk", "Wv": "L0_attn_Wv", "Wout": "L0_attn_Wout",
          "wqkv": "L0_ffn_wqkv", "q_scale": "L0_ffn_q_scale", "k_scale": "L0_ffn_k_scale", "wo": "L0_ffn_wo",
          "ln_g": "L0_ffn_ln_g", "ln_b": "L0_ffn_ln_b", "w1": "L0_ffn_w1", "b1": "L0_ffn_b1", "w2": "L0_ffn_w2",
          "b2": "L0_ffn_b2", "gate_w": "L1_ffn_gate_w", "fc_w": "L1_ffn_fc_w", "proj_w": "L1_ffn_proj_w"}


def constants():
    import numpy as np
    bf16 = mybir.dt.np(BF16)
    f = np.float32
    c = {"c_ident": np.eye(P, dtype=f), "c_identb": np.eye(P).astype(bf16), "c_ones": np.ones((1, P), f),
         "c_augones": np.ones((SPLIT, H0 // 2, SEQ)).astype(bf16)}
    q, k = np.arange(P)[:, None], np.arange(KEYS)[None, :] - WIN
    seen = (k <= q) & (k >= q - WIN)
    both = np.stack([np.where(seen, 0.0, LOCAL_NEG), np.where(seen & (k >= 0), 0.0, LOCAL_NEG)], 1)
    c["c_local"] = np.repeat(both[:, :, None, :], 2, 2).astype(bf16)
    kk = np.arange(P)[None, :]
    c["c_causal"] = np.where(kk <= q, 0.0, NEG).astype(bf16)
    e = np.arange(NE)
    c["c_lower"] = np.broadcast_to((e[None, :] < e[:, None]).astype(f), (P, NE, NE)).copy()
    half = np.arange(0, DH1, 2, dtype=f)
    inv = (f(1.0) / f(10000.0) ** (half / f(DH1))).astype(f)
    t = np.arange(SEQ, dtype=f)
    fr = (t[:, None] * inv[None, :]).astype(f)
    fr = np.concatenate([fr, fr], -1)
    base = ((half + f(0.4 * DH1)) / f(1.4 * DH1)).astype(f)
    power = ((t - SEQ // 2) / f(WIN // 2)).astype(f)
    sc = (base[None, :] ** power[:, None]).astype(f)
    sc = np.concatenate([sc, sc], -1)
    cos, sin = np.cos(fr), np.sin(fr)
    sign = np.where(np.arange(DH1) < DH1 // 2, -1.0, 1.0).astype(f)
    tabs = np.stack([cos * sc, sin * sc * sign, cos / sc, sin / sc * sign])
    c["c_rot"] = np.ascontiguousarray(tabs.reshape(4, TPB, P, DH1).transpose(2, 0, 1, 3)).astype(f)
    pos = np.arange(0, HS, 2, dtype=f)
    theta = (f(10000.0) ** (f(-2.0) * pos / f(HS))).astype(f)
    an = (t[:, None] * theta[None, :]).astype(f)
    cs = np.repeat(np.cos(an), 2, 1)
    sn = np.stack([-np.sin(an), np.sin(an)], -1).reshape(SEQ, HS)
    c["c_rope"] = np.ascontiguousarray(np.stack([cs, sn]).reshape(2, TPB, P, HS).transpose(2, 0, 1, 3)).astype(f)
    return c


def lay_out(inputs):
    import numpy as np
    a = {name: np.ascontiguousarray(inputs[full]) for name, full in _NAMES.items()}
    a["Wq1T"] = np.ascontiguousarray(np.transpose(inputs["L1_attn_Wq"], (0, 2, 1)))
    for name, full in (("Wk1T", "L1_attn_Wk"), ("Wv1T", "L1_attn_Wv"), ("Wo1T", "L1_attn_Wo")):
        a[name] = np.ascontiguousarray(np.transpose(inputs[full]))
    return {**a, **constants()}


def kernel(**inputs):
    import numpy as np
    import concourse.bacc as bacc
    from concourse.bass_utils import run_bass_kernel_spmd as launch
    inputs = {k: np.asarray(v) for k, v in inputs.items()}
    arrays = {f"in_{k}": v for k, v in lay_out(inputs).items()}
    nc = bacc.Bacc("TRN2", target_bir_lowering=False, num_devices=1)
    T = {k[3:]: nc.dram_tensor(k, v.shape, mybir.dt.from_np(v.dtype), kind="ExternalInput").ap()
         for k, v in arrays.items()}
    T["out"] = nc.dram_tensor("out", (NB, SEQ, D), F32, kind="ExternalOutput").ap()
    program(nc, T)
    return launch(nc, [arrays], core_ids=[0]).results[0]["out"]
```

```python
import concourse.bass as bass
from concourse import mybir
from contextlib import ExitStack

F32 = mybir.dt.float32
F32R = mybir.dt.float32r
BF16 = mybir.dt.bfloat16
ALU = mybir.AluOpType
ACTF = mybir.ActivationFunctionType
AXX = mybir.AxisListType.X

P = 128
D = 128
NB = 2
SEQ = 1024
TPB = SEQ // P
NT = NB * TPB
BANK = 512
NEG = -3.3895313892515355e38
LOCAL_NEG = -3e37
EPS = 1e-5

H0, DH0 = 16, 8
GH = 4
NG = H0 // GH
STRIP = 32
SPLIT = 3
QK_ROWS = SPLIT * SPLIT * DH0
PAD_ROWS = -(-QK_ROWS // STRIP) * STRIP
AUG = PAD_ROWS + SPLIT
LEAD = 37

DEPTH = 2
H1, DH1 = 8, 64
INNER = H1 * DH1
WIN = 64
HID = int(D * 4 * 2 / 3)
HCH = -(-HID // 3)
HIDC = [min(HCH, HID - c * HCH) for c in range(3)]
BLK = WIN
SPAN = WIN + BLK
KEYS = WIN + P
QK_SCALE = 8.0

NKV, HS = 2, 128
NE, FF, TOPK = 8, 4 * D, 2
FCH = FF // P
CHUNK = 512


WIDTH, ROPE_WIDTH, CAUSAL_WIDTH = 4, 3, 4
AGE = 100.0


class Sem:

    def __init__(self, handle):
        self.handle, self.count = handle, 0


class Queue:

    when = {}
    latest = pe = 0.0

    def __init__(self, sems, cost):
        self.items, self.reached, self.sems, self.cost, self.clock = [], {}, sems, cost, 0.0

    def __call__(self, method, *args, after=(), sem=None, by=1, **kw):
        self.wait(*after)
        start = max([self.clock, *[Queue.when.get(r, 0.0) for r in after]])
        busy, tail = self.cost(method, args)
        self.clock = start + busy
        if self.cost is pe_cost:
            Queue.pe = self.clock
        Queue.latest = self.clock + tail
        self.items.append((method, args, kw, (sem, by)))
        if sem is None:
            return None
        self.sems[sem].count += by
        Queue.when[sem, self.sems[sem].count] = Queue.latest
        return sem, self.sems[sem].count

    def wait(self, *after):
        for s, value in after:
            if value > self.reached.get(s, 0):
                self.reached[s] = value
                self.items.append((None, s, value, None))

    def play(self, eng):
        for method, a, kw, last in self.items:
            if method is None:
                eng.wait_ge(self.sems[a].handle, kw)
            else:
                ins = method(*a, **kw)
                if last[0] is not None:
                    ins.then_inc(self.sems[last[0]].handle, last[1])


def columns(ap):
    n = 1
    for k in ap.shape[1:]:
        n *= k
    return n


def pe_cost(method, args):
    out, stationary = args[0], args[1]
    n = columns(out)
    if method.__name__ == "transpose":
        return n / 1.2, 230.0
    if stationary.dtype in (BF16, F32R):
        return n / 2.4 + 3, 230.0
    if out.shape[0] <= STRIP:
        return n / 0.6 / 3.6, 230.0
    if out.shape[0] == BLK:
        return (134.0 if n == SPAN else 77.0), 230.0
    return max(n, 128) / 0.6 + 3, 230.0


def dve_cost(method, args):
    return 1.04 * max(columns(a) for a in args[:2] if hasattr(a, "shape")) + 70, 100.0


def act_cost(method, args):
    global act_table
    switch = 0.0
    if args[-1] in (ACTF.Exp, ACTF.Gelu):
        switch = 0.0 if args[-1] == act_table else 1300.0
        act_table = args[-1]
    return 0.84 * columns(args[0]) + 60 + switch, 100.0


act_table = None


def pool_cost(method, args):
    return (2900.0 if ALU.pow in args else 2.1 * columns(args[0]) + 60), 100.0


def dma_cost(method, args):
    return 60.0, 2500.0


class Ring:

    def __init__(self, bufs):
        self.bufs = bufs
        self.free = [[] for _ in bufs]
        self.order = list(range(len(bufs)))

    def due(self, i):
        return max([0.0, *[Queue.when[r] for r in self.free[i]]])

    def take(self):
        i = min(self.order, key=self.due)
        self.order.remove(i)
        return i, self.bufs[i], self.free[i]

    def get(self):
        while not self.order:
            yield
        return self.take()

    def give(self, i, *after):
        self.free[i] = list(after)
        self.order.append(i)


def need(ready, key):
    while key not in ready:
        yield
    return ready[key]


def interleave(lanes):
    state = [dict(todo=list(pieces), width=width, live=[]) for pieces, width in lanes]
    now, order = 0.0, 0
    stuck = set()
    while True:
        for st in state:
            while st["todo"] and len(st["live"]) < st["width"]:
                order += 1
                st["live"].append([now, order, st["todo"].pop(0)])
        live = [(p, st) for st in state for p in st["live"]]
        if not live:
            return
        free = [(p, st) for p, st in live if p[1] not in stuck]
        assert free, "nothing can go on"
        piece, st = min(free, key=lambda ps: (max(ps[0][0], Queue.pe) + AGE * st_index(ps), ps[0][0], ps[0][1]))
        now = max(now, piece[0])
        Queue.latest = -1.0
        try:
            ready = next(piece[2])
        except StopIteration:
            st["live"].remove(piece)
            stuck.clear()
            continue
        if Queue.latest < 0 and ready is None:
            stuck.add(piece[1])
        else:
            stuck.clear()
            piece[0] = max(piece[0], Queue.latest if ready is None else ready)


def st_index(ps):
    return ps[1]["live"].index(ps[0])


def weave(gens, width):
    interleave([(gens, width)])


def program(nc, T):
    ctx = ExitStack()
    with ctx:
        names = {}

        def sb(name, shape, dt=F32):
            return ctx.enter_context(nc.sbuf_tensor(name, shape, dt))

        class Sems(dict):
            def __missing__(self, name):
                self[name] = Sem(ctx.enter_context(nc.semaphore(name)))
                return self[name]

        sems = Sems()
        PE, DV, AC, GP, SP = (Queue(sems, cost) for cost in (pe_cost, dve_cost, act_cost, pool_cost, dma_cost))
        mm, tr = nc.tensor.matmul, nc.tensor.transpose
        vec, act, gps, sync = nc.vector, nc.scalar, nc.gpsimd, nc.sync
        banks = Ring([ctx.enter_context(nc.psum_tensor(f"bank{i}", [P, BANK], F32)) for i in range(8)])

        ident = sb("ident", [P, P])
        identb = sb("identb", [P, P], BF16)
        local_mask = sb("local_mask", [P, 2, H1 // 2, SPAN], BF16)
        causal_mask = sb("causal_mask", [P, P], BF16)
        lower = sb("lower", [P, NE, NE])

        x = sb("x", [P, NT, D])
        xin = sb("xin", [P, NT, D])

        def load(dst, src, sem):
            return SP(sync.dma_start, dst, src, sem=sem, by=16)

        ld_id = load(ident[:, :], T["c_ident"], "ld_ident")
        ld_x = [load(x[:, b * TPB:(b + 1) * TPB, :], T["x"][b].rearrange("(t p) d -> p t d", p=P), f"ld_x{b}")
                for b in range(NB)]
        w0 = sb("w0", [P, 4, D])
        wqkv0, wout0 = w0[:, 0:3, :], w0[:, 3, :]
        for j, n in enumerate(("Wq", "Wk", "Wv")):
            ld_w0 = load(wqkv0[:, j, :], T[n], "ld_w0")
        ld_w0 = load(wout0, T["Wout"], "ld_w0")
        load(identb[:, :], T["c_identb"], "ld_const")
        load(local_mask[:, :, :, :], T["c_local"], "ld_const")
        load(causal_mask[:, :], T["c_causal"], "ld_const")
        ld_const = load(lower[:, :, :], T["c_lower"], "ld_const")

        stat = Ring([sb(f"stat{i}", [P, 10]) for i in range(8)])
        minus_half = sb("minus_half", [P, 2 * H1])
        mh_ready = GP(gps.memset, minus_half[:, :], -0.5, sem="minus_half")

        x_ready = {t: ld_x[t // TPB] for t in range(NT)}

        def transposed(t, dst, after, sem):
            i, bank, free = yield from banks.get()
            done = PE(tr, bank[:, 0:P], x[:, t, :], ident[:, :], after=[x_ready[t], ld_id, *free], sem="pe_xT")
            done = AC(act.copy, dst, bank[:, 0:P], after=[done, *after], sem=sem)
            banks.give(i, done)
            return done

        def deviation(src, after, st):
            d = DV(vec.bn_stats, st[:, 0:6], src, after=after, sem="ln_stat")
            read = d
            d = DV(vec.bn_aggr, st[:, 6:8], st[:, 0:6], after=[d], sem="ln_aggr")
            d = DV(vec.tensor_scalar, st[:, 9:10], st[:, 7:8], EPS, None, ALU.add, after=[d], sem="ln_eps")
            return read, GP(gps.tensor_tensor, st[:, 8:9], st[:, 9:10], minus_half[:, 0:1], ALU.pow,
                            after=[d, mh_ready], sem="ln_rstd")

        def layer_norm(t, done):
            si, st, free = yield from stat.get()
            _, r = deviation(x[:, t, :], [done, *free], st)
            yield
            x_ready[t] = DV(vec.tensor_scalar, x[:, t, :], x[:, t, :], st[:, 6:7], st[:, 8:9], ALU.subtract, ALU.mult,
                            after=[r], sem="ln_out")
            stat.give(si, x_ready[t])
            yield

        def stage_out():
            for b in range(NB):
                ts = slice(b * TPB, (b + 1) * TPB)
                o = SP(sync.dma_start, T["out"][b].rearrange("(t p) d -> p t d", p=P), x[:, ts, :],
                       after=[x_ready[t] for t in range(b * TPB, (b + 1) * TPB)], sem="store", by=16)
            SP.wait(o)

        def done_all():
            return [(name, s.count) for name, s in sems.items() if s.count]

        def fence(tokens):
            for q in (SP, GP, PE, DV, AC):
                q.wait(*tokens)

        z = xin
        zT = Ring([sb(f"a_zT{i}", [P, P]) for i in range(2)])
        nmax_ready = {}
        z_ready, tile_done = {}, {}

        def output_tile(t):
            b, j = divmod(t, TPB)
            i, bank, free = yield from banks.get()
            m = PE(tr, bank[:, 0:P], z[:, t, :], ident[:, :], after=[z_ready[b], *free], sem="a_zTT")
            zi, zt, zfree = yield from zT.get()
            e = AC(act.copy, zt[:, :], bank[:, 0:P], after=[m, *zfree], sem="a_zT")
            yield
            m = PE(mm, bank[:, P:2 * P], zt[:, :], wout0, start=True, stop=True, after=[e], sem="a_out")
            zT.give(zi, m)
            d = DV(vec.scalar_tensor_tensor, x[:, t, :], x[:, t, :], 2.0, bank[:, P:2 * P], ALU.mult,
                   ALU.add, after=[m], sem="a_res")
            banks.give(i, d)
            yield
            yield from layer_norm(t, d)
            tile_done[-1, t] = True

        rot0 = sb("b_rot0", [P, 4, TPB, DH1])
        local_weights = ExitStack()

        def lw(name, shape, dt=F32):
            return local_weights.enter_context(nc.sbuf_tensor(name, shape, dt))

        wqkv = [lw(f"b_wqkv{l}", [P, 3 * INNER]) for l in range(DEPTH)]
        wo = [lw(f"b_wo{l}", [P, INNER // P, D]) for l in range(DEPTH)]
        w1 = [lw(f"b_w1{l}", [P, 2 * HID]) for l in range(DEPTH)]
        w2 = [lw(f"b_w2{l}", [HCH, 3, D]) for l in range(DEPTH)]
        b1 = [lw(f"b_b1{l}", [HCH, 6]) for l in range(DEPTH)]
        ln = [lw(f"b_ln{l}", [P, 2]) for l in range(DEPTH)]
        scales = [lw(f"b_scales{l}", [P, 2, DH1]) for l in range(DEPTH)]
        rot = [rot0] + [lw(f"b_rot{l}", [P, 4, TPB, DH1]) for l in range(1, DEPTH)]
        b2b = [lw(f"b_b2b{l}", [P, D]) for l in range(DEPTH)]
        ld_w, tables = [], []

        def load_layers():
            yield from need(nmax_ready, (0, 0, 0))
            for l in range(DEPTH):
                s = f"ld_layer{l}"
                load(wqkv[l][:, :], T["wqkv"][l], s)
                for j, n in enumerate(("q_scale", "k_scale")):
                    load(scales[l][:, j, :], T[n][l:l + 1, :].to_broadcast([P, DH1]), s)
                load(wo[l][:, :, :], T["wo"][l].rearrange("(c p) d -> p c d", p=P), s)
                load(w1[l][:, :], T["w1"][l], s)
                for c in range(3):
                    n = HIDC[c]
                    load(w2[l][0:n, c, :], T["w2"][l][c * HCH:c * HCH + n, :], s)
                    for j in range(2):
                        lo = j * HID + c * HCH
                        load(b1[l][0:n, 3 * j + c:3 * j + c + 1],
                             T["b1"][l:l + 1, lo:lo + n].rearrange("a n -> n a"), s)
                load(ln[l][:, 0:1], T["ln_g"][l:l + 1, :].rearrange("a n -> n a"), s)
                ld_w.append(load(ln[l][:, 1:2], T["ln_b"][l:l + 1, :].rearrange("a n -> n a"), s))
            for l in range(DEPTH):
                tab_in = load(rot[l][:, :, :, :], T["c_rot"], f"ld_rot{l}")
                load(b2b[l][:, :], T["b2"][l:l + 1, :].to_broadcast([P, D]), f"ld_b2b{l}")
                half = DH1 // 2
                for j in range(2):
                    c, s, g = 2 * j, 2 * j + 1, scales[l][:, j, :]
                    for tab, lo, src in ((c, 0, g[:, 0:half]), (c, half, g[:, half:]), (s, 0, g[:, half:]),
                                         (s, half, g[:, 0:half])):
                        d = GP(gps.tensor_tensor, rot[l][:, tab, :, lo:lo + half], rot[l][:, tab, :, lo:lo + half],
                               src.unsqueeze(1).to_broadcast([P, TPB, half]), ALU.mult,
                               after=[tab_in, ld_w[l]], sem="b_fold")
                tables.append(d)
                yield

        ld_b2b = [(f"ld_b2b{l}", 16) for l in range(DEPTH)]

        region = ExitStack()
        with region:
            def rb(name, shape, dt=F32):
                return region.enter_context(nc.sbuf_tensor(name, shape, dt))

            xT = rb("a_xT", [P, SEQ])
            parts = [rb(f"a_parts{j}", [P, SPLIT, SEQ], BF16) for j in range(2)]
            rest = rb("a_rest", [P, 2, BANK])
            UH = H0 // 2
            HALVES = SEQ // BANK
            augq = [rb(f"a_augq{u}", [AUG, HALVES, UH, BANK], BF16) for u in range(2)]
            augk = [rb(f"a_augk{u}", [AUG, UH, SEQ], BF16) for u in range(2)]
            vaug = [rb(f"a_v{b}", [P, TPB, H0, STRIP]) for b in range(NB)]
            probs = Ring([rb(f"a_p{i}", [P, BANK]) for i in range(9)])
            oT = rb("a_oT", [P, BANK])
            QT = BANK // P
            mx = [rb(f"a_mx{i}", [P, 2, GH * QT]) for i in range(2)]
            nmax = rb("a_nmax", [P, GH * QT])
            mrest = rb("a_mrest", [GH * QT, P])
            mpart = rb("a_mpart", [GH * QT, SPLIT, P], BF16)
            rden = rb("a_rden", [P, QT, GH])
            scratch = [nc.dram_tensor(f"a_scratch{j}", [NB, P, SPLIT, SEQ], BF16).ap() for j in range(2)]

            strip = slice(PAD_ROWS - STRIP, PAD_ROWS)
            vz, pad_zero, ones = [], [], []
            last = mh_ready

            def zeros(u, keys):
                nonlocal last
                vz.append(GP(gps.memset, vaug[u][:, :, :, :], 0.0, after=[last], sem="vaug_zero"))
                vz[u] = GP(gps.memset, vaug[u][:, :, :, DH0:DH0 + 1], 1.0, after=[vz[u]], sem="vaug_one")
                q0 = GP(gps.memset, augq[u][strip, :, :, :], 0.0, after=[vz[u]], sem="pad_zero_q")
                engine, name, after = (GP, gps, [q0]) if keys == "pool" else (DV, vec, [])
                k0 = engine(name.memset, augk[u][strip, :, :], 0.0, after=after, sem=f"pad_zero_k{u}")
                pad_zero.append([q0, k0])
                last = k0 if keys == "pool" else q0

            def one_rows():
                nonlocal last
                for u in range(2):
                    last = GP(gps.memset, augk[u][PAD_ROWS:AUG, :, :], 1.0, after=[last], sem="pad_zero_q")
                    ones.append(last)

            zeros(0, "vector")
            v_ready, sc_ready = {}, {}
            scratch_free = {}
            parts_free = []
            xT_free = []

            def project(b):
                nonlocal parts_free, xT_free
                ts = range(b * TPB, (b + 1) * TPB)
                for j, t in enumerate(ts):
                    xt = yield from transposed(t, xT[:, j * P:(j + 1) * P], xT_free, "a_xT")
                    yield
                last_mm = []
                for j in range(2):
                    for half in range(SEQ // BANK):
                        i, bank, free = (yield from banks.get())
                        cols = slice(half * BANK, (half + 1) * BANK)
                        m = PE(mm, bank[:, :], wqkv0[:, j, :], xT[:, cols], start=True, stop=True,
                               after=[xt, ld_w0, *free], sem="a_qk")
                        d = DV(vec.tensor_copy, parts[j][:, 0, cols], bank[:, :], after=[m, *parts_free], sem="a_split")
                        d = DV(vec.tensor_tensor, rest[:, half, :], bank[:, :], parts[j][:, 0, cols], ALU.subtract,
                               after=[d], sem="a_split")
                        banks.give(i, d)
                        d = DV(vec.tensor_copy, parts[j][:, 1, cols], rest[:, half, :], after=[d], sem="a_split")
                        d = DV(vec.tensor_tensor, parts[j][:, 2, cols], rest[:, half, :], parts[j][:, 1, cols],
                               ALU.subtract, after=[d], sem="a_split")
                        yield
                    sc_ready[b, j] = SP(sync.dma_start, scratch[j][b], parts[j][:, :, :],
                                        after=[d], sem=f"scratch{b}{j}", by=16)
                parts_free = [sc_ready[b, 0], sc_ready[b, 1]]
                for j, t in enumerate(ts):
                    i, bank, free = (yield from banks.get())
                    m = PE(mm, bank[:, 0:D], xT[:, j * P:(j + 1) * P], wqkv0[:, 2, :], start=True, stop=True,
                           after=[xt, ld_w0, *free], sem="a_v")
                    v_ready[t] = AC(act.copy, vaug[b][:, j, :, 0:DH0],
                                    bank[:, 0:D].rearrange("p (h d) -> p h d", h=H0), after=[m, vz[b]], sem="a_vcopy")
                    banks.give(i, v_ready[t])
                    yield
                xT_free = [m]

            aug_ready, gathered = {}, {}
            aug_free = {}

            def gather(b, u):
                rows = SPLIT * DH0
                free = [*pad_zero[u], *aug_free.get((b - 1, u), [])]
                heads = slice(u * UH * DH0, (u + 1) * UH * DH0)
                src_q = scratch[0][b, heads].rearrange("(h d) s t -> (d s) h t", d=DH0)
                src_k = scratch[1][b, heads].rearrange("(h d) s t -> (d s) h t", d=DH0)
                for i in range(SPLIT):
                    for half in range(HALVES):
                        SP(sync.dma_start, augq[u][i * rows:(i + 1) * rows, half, :, :],
                           src_q[:, :, half * BANK:(half + 1) * BANK], after=[sc_ready[b, 0], *free],
                           sem=f"gather{b}{u}", by=16)
                for i in range(SPLIT):
                    if i == 0:
                        moves = [(slice(0, rows), slice(0, rows))]
                    else:
                        moves = [(slice(i * rows + s, (i + 1) * rows, SPLIT), slice((s + i) % SPLIT, rows, SPLIT))
                                 for s in range(SPLIT)]
                    for dst, src in moves:
                        aug_ready[b, u] = SP(sync.dma_start, augk[u][dst, :, :], src_k[src, :, :],
                                             after=[sc_ready[b, 1], *free], sem=f"gather{b}{u}", by=16)
                gathered[b, u] = True
                yield

            mrow_free = []
            m_free = []

            def maxima(b, g, part):
                nonlocal mrow_free, m_free
                u = g // (NG // 2)
                mxb = mx[part]
                yield from need(gathered, (b, u))
                hu = (g * GH) % UH
                for hh in range(GH):
                    for qt in range(QT):
                        for half in range(HALVES):
                            i, bank, free = yield from banks.get()
                            m = PE(mm, bank[:, :], augq[u][0:PAD_ROWS, part, hu + hh, qt * P:(qt + 1) * P],
                                   augk[u][0:PAD_ROWS, hu + hh, half * BANK:(half + 1) * BANK], start=True, stop=True,
                                   after=[aug_ready[b, u], *free], sem="a_smax")
                            c = hh * QT + qt
                            d = DV(vec.reduce_max, mxb[:, half, c:c + 1], bank[:, :], AXX, after=[m], sem="a_max")
                            banks.give(i, d)
                            yield PE.clock
                n = DV(vec.tensor_tensor, nmax[:, :], mxb[:, 0, :], mxb[:, 1, :], ALU.max, after=[d, *mrow_free],
                       sem="a_max2")
                yield PE.clock
                i, bank, free = yield from banks.get()
                m = PE(tr, bank[0:GH * QT, 0:P], nmax[:, :], ident[:, :], after=[n, *free], sem="a_maxT")
                mrow_free = [m]
                d = DV(vec.tensor_scalar, mrest[:, :], bank[0:GH * QT, 0:P], -1.0, None, ALU.mult, after=[m],
                       sem="a_mneg")
                banks.give(i, d)
                d = DV(vec.tensor_copy, mpart[:, 0, :], mrest[:, :], after=[d, *m_free], sem="a_msplit")
                d = DV(vec.tensor_tensor, mrest[:, :], mrest[:, :], mpart[:, 0, :], ALU.subtract, after=[d],
                       sem="a_msplit")
                d = DV(vec.tensor_copy, mpart[:, 1, :], mrest[:, :], after=[d], sem="a_msplit")
                d = DV(vec.tensor_tensor, mpart[:, 2, :], mrest[:, :], mpart[:, 1, :], ALU.subtract, after=[d],
                       sem="a_msplit")
                for s in range(SPLIT):
                    dst = augq[u][PAD_ROWS + s:PAD_ROWS + s + 1, part, hu:hu + GH, :]
                    r = SP(sync.dma_start, dst.rearrange("a h (t q) -> a (h t) q", q=P), mpart[:, s, :],
                           after=[d], sem=f"mrows{b}{g}{part}", by=16)
                nmax_ready[b, g, part] = r
                m_free = [r]
                yield

            oT_free = []
            def attend(b, g, half):
                nonlocal oT_free
                u = g // (NG // 2)
                scale = 1.0 / float(DH0) ** 0.5
                oi, obank, ofree = yield from banks.get()
                pend = []

                yield from need(nmax_ready, (b, g, half))

                def values(kt, tiles):
                    nonlocal ofree
                    for hh, (pi, pbuf, e) in enumerate(tiles):
                        h = g * GH + hh
                        m = PE(mm, obank[hh * STRIP:(hh + 1) * STRIP, :], vaug[b][:, kt, h, :], pbuf[:, :],
                               start=(kt == 0), stop=(kt == TPB - 1), after=[e, v_ready[b * TPB + kt], *ofree],
                               sem="a_pv")
                        probs.give(pi, m)
                    ofree = []
                    return m

                for kt in range(TPB):
                    tiles = []
                    for hh in range(GH):
                        hu = (g * GH + hh) % UH
                        i, bank, free = yield from banks.get()
                        m = PE(mm, bank[:, :], augk[u][:, hu, kt * P:(kt + 1) * P],
                               augq[u][:, half, hu, :], start=True, stop=True,
                               after=[nmax_ready[b, g, half], ones[u], *free], sem="a_sT")
                        pi, pbuf, pfree = yield from probs.get()
                        e = AC(act.activation, pbuf[:, :], bank[:, :], ACTF.Exp, scale=scale, after=[m, *pfree],
                               sem="a_exp")
                        banks.give(i, e)
                        tiles.append((pi, pbuf, e))
                        yield PE.clock
                    if pend:
                        values(*pend)
                    pend = (kt, tiles)
                m = values(*pend)
                yield
                e = AC(act.copy, oT[:, :], obank[:, :], after=[m, *oT_free], sem="a_oT")
                banks.give(oi, e)
                yield
                i, bank, free = yield from banks.get()
                for q in range(QT):
                    m = PE(tr, bank[:, q * P:(q + 1) * P], oT[:, q * P:(q + 1) * P], ident[:, :], after=[e, *free],
                           sem="a_oTT")
                oT_free = [m]
                yield
                o = bank[:, :].rearrange("p (q h c) -> p q h c", q=QT, h=GH)
                d = DV(vec.reciprocal, rden[:, :, :], o[:, :, :, DH0], after=[m], sem="a_rden")
                zz = z[:, b * TPB + half * QT:b * TPB + (half + 1) * QT, g * STRIP:(g + 1) * STRIP]
                zz = zz.rearrange("p q (h c) -> p q h c", h=GH)
                for q in range(QT):
                    d = DV(vec.tensor_tensor, zz[:, q], o[:, q, :, 0:DH0],
                           rden[:, q, :].unsqueeze(2).to_broadcast([P, GH, DH0]), ALU.mult,
                           after=[d], sem="a_z")
                banks.give(i, d)
                if (g, half) == (NG - 1, 1):
                    z_ready[b] = d
                if g % (NG // 2) == NG // 2 - 1 and half == 1:
                    aug_free[b, u] = [("a_sT", sems["a_sT"].count), ("a_smax", sems["a_smax"].count)]

            units = [(b, g, half) for b in range(NB) for g in range(NG) for half in range(2)]

            def prepare(b):
                yield from project(b)
                for u in range(2):
                    if (b, u) == (0, 1):
                        one_rows()
                        zeros(1, "pool")
                    if b:
                        yield from need(aug_free, (b - 1, u))
                    yield from gather(b, u)

            def outputs(b, j):
                yield from need(z_ready, b)
                yield from output_tile(b * TPB + j)

            def units_in_step():
                done = [0, 0]
                todo = [(p for u in units for p in maxima(*u)), (p for u in units for p in attend(*u))]
                live = [True, True]
                while any(live):
                    lane = 0 if live[0] and (done[0] <= done[1] + LEAD or not live[1]) else 1
                    ready = next(todo[lane], "end")
                    if ready == "end":
                        live[lane] = False
                        continue
                    done[lane] += Queue.latest >= 0
                    yield ready

            interleave([([prepare(b) for b in range(NB)], 1), ([units_in_step()], 1), ([load_layers()], 1),
                        ([outputs(0, j) for j in range(TPB)], 2)])
            fence(done_all())

        region = ExitStack()
        with region:
            hTa = [rb(f"b_hTa{b}", [P, SEQ + 1]) for b in range(NB)]
            hTf = [rb(f"b_hTf{b}", [P, SEQ + 1]) for b in range(NB)]
            ring = lambda name, shape, n: Ring([rb(f"{name}{i}", shape) for i in range(n)])
            sq = ring("b_sq", [P, INNER], 2)
            t1 = ring("b_t1", [P, INNER], 2)
            t2 = ring("b_t2", [P, INNER], 2)
            ss = ring("b_ss", [P, 2 * H1], 6)
            rq = ring("b_r", [P, 2, INNER], 3)
            qT = ring("b_qT", [P, H1 // 2, P], 4)
            kT = [ring(f"b_kT{b}_", [P, H1 // 2, KEYS], 4) for b in range(NB)]
            vv = ring("b_vv", [P, H1, DH1 + 1], 5)
            va = [ring(f"b_va{b}_", [P, H1, DH1 + 1], 4) for b in range(NB)]
            pp = ring("b_p", [P, H1 // 2, SPAN], 6)
            pT = ring("b_pT", [P, H1 // 2, P], 5)
            mxl = ring("b_mx", [P, H1], 6)
            rdl = ring("b_rd", [P, H1], 4)
            oo = ring("b_o", [P, INNER], 2)
            ooT = ring("b_oT", [P, INNER // P, P], 2)
            nn = ring("f_n", [P, D], 3)
            nT = ring("f_nT", [P, P], 3)
            gl = ring("f_g", [HCH, 3, P], 3)
            uT = ring("f_u", [HCH, 3, P], 3)
            for b in range(NB):
                GP(gps.memset, hTa[b][:, 0:1], 0.0, sem="b_zero")
                GP(gps.memset, hTf[b][:, 0:1], 0.0, sem="b_zero")
                for v in va[b].bufs:
                    win_zero = DV(vec.memset, v[0:WIN, :, 0:DH1], 0.0, sem="b_win_zero")
                    GP(gps.memset, v[:, :, DH1:DH1 + 1], 1.0, sem="b_zero")
                for k in kT[b].bufs:
                    GP(gps.memset, k[:, :, 0:WIN], 0.0, sem="b_zero")
            for v in vv.bufs:
                b_zero = GP(gps.memset, v[:, :, DH1:DH1 + 1], 1.0, sem="b_zero")

            hTa_free, hTf_free, hTa_done, hTf_done, kept = {}, {}, {}, {}, {}
            k_tile, v_tile = {}, {}

            def shifted(t, hT, free_of):
                j = t % TPB
                i, bank, free = yield from banks.get()
                m = PE(tr, bank[:, 0:P], x[:, t, :], ident[:, :], after=[x_ready[t], *free], sem="pe_xT")
                half = D // 2
                AC(act.copy, hT[0:half, j * P:(j + 1) * P], bank[0:half, 0:P], after=[m, b_zero, *free_of], sem="b_hT")
                h = AC(act.copy, hT[half:P, j * P + 1:(j + 1) * P + 1], bank[half:P, 0:P], sem="b_hT")
                banks.give(i, h)
                yield
                return h

            rot_read, causal_ready = {}, {}

            def load_causal():
                yield from need(tile_done, (-1, NT - 1))
                free = [("a_out", sems["a_out"].count)]
                for j in range(NKV):
                    SP(sync.dma_start, w0[:, j, :], T["Wq1T"][j], after=free, sem="ld_c", by=16)
                SP(sync.dma_start, w0[:, 2, :], T["Wk1T"], sem="ld_c", by=16)
                causal_ready["w"] = SP(sync.dma_start, w0[:, 3, :], T["Wv1T"], sem="ld_c", by=16)
                reads = []
                for key in [(b, 0, j, part) for b in range(NB) for j in range(TPB) for part in range(2)]:
                    reads.append((yield from need(rot_read, key)))
                causal_ready["rope"] = SP(sync.dma_start, rot[0][:, :, :, :].rearrange("p a t d -> p (a t d)"),
                                          T["c_rope"].rearrange("p a t d -> p (a t d)"),
                                          after=reads, sem="ld_rope", by=16)
                yield

            def local_layer(b, l, j):
                t = b * TPB + j
                yield from need(tile_done, (l - 1, t))
                if l == 0:
                    kept[t] = GP(gps.tensor_copy, xin[:, t, :], x[:, t, :], after=[x_ready[t]], sem="b_keep")
                nxt = min(j + 1, TPB - 1)
                if l:
                    yield from need(hTa_free, (b, l - 1, nxt))
                if j:
                    yield from need(hTa_done, (b, l, j - 1))
                h = yield from shifted(t, hTa[b], [hTa_free[b, l - 1, nxt]] if l else [])
                hTa_done[b, l, j] = h
                ri, r, rfree = yield from rq.get()
                si, sst, sfree = yield from ss.get()
                for part in range(2):
                    i, bank, free = yield from banks.get()
                    m = PE(mm, bank[:, :], hTa[b][:, j * P:(j + 1) * P], wqkv[l][:, part * INNER:(part + 1) * INNER],
                           start=True, stop=True, after=[h, ld_w[l], *free], sem="b_qkv")
                    qi, s, qfree = yield from sq.get()
                    a = AC(act.square, s[:, :], bank[:, :], after=[m, *qfree], sem="b_sq")
                    v = bank[:, :].rearrange("p (h d) -> p h d", h=H1)
                    half = DH1 // 2

                    def table(k, lo, n):
                        return rot[l][:, 2 * part + k, j, lo:lo + n].unsqueeze(1).to_broadcast([P, H1, n])
                    i1, a1, free1 = yield from t1.get()
                    i2, a2, free2 = yield from t2.get()
                    DV(vec.tensor_tensor, a1[:, :].rearrange("p (h d) -> p h d", h=H1), v, table(0, 0, DH1),
                       ALU.mult, after=[a, tables[l], *free1], sem="b_rot")
                    a2v = a2[:, :].rearrange("p (h d) -> p h d", h=H1)
                    DV(vec.tensor_tensor, a2v[:, :, 0:half], v[:, :, half:], table(1, 0, half), ALU.mult,
                       after=free2, sem="b_rot")
                    r2 = DV(vec.tensor_tensor, a2v[:, :, half:], v[:, :, 0:half], table(1, half, half), ALU.mult,
                            sem="b_rot")
                    banks.give(i, a, r2)
                    rot_read[b, l, j, part] = r2
                    d = DV(vec.reduce_sum, sst[:, part * H1:(part + 1) * H1],
                           s[:, :].rearrange("p (h d) -> p h d", h=H1), AXX, after=[a, *sfree], sem="b_ss")
                    sq.give(qi, d)
                    g = GP(gps.tensor_tensor, r[:, part, :], a1[:, :], a2[:, :], ALU.add, after=[r2, *rfree],
                           sem="b_rotsum")
                    t1.give(i1, g)
                    t2.give(i2, g)
                    yield
                d = DV(vec.tensor_scalar, sst[:, :], sst[:, :], 1e-24, None, ALU.max, after=[d], sem="b_clip")
                d = GP(gps.tensor_tensor, sst[:, :], sst[:, :], minus_half[:, :], ALU.pow, after=[d, mh_ready],
                       sem="b_rn")
                i, bank, free = yield from banks.get()
                m = PE(mm, bank[:, :], hTa[b][:, j * P:(j + 1) * P], wqkv[l][:, 2 * INNER:], start=True, stop=True,
                       after=free, sem="b_qkv")
                hTa_free[b, l, j] = m
                vi, vb, vfree = yield from vv.get()
                v_done = AC(act.copy, vb[:, :, 0:DH1], bank[:, :].rearrange("p (h d) -> p h d", h=H1),
                            after=[m, b_zero, *vfree], sem="b_v")
                banks.give(i, v_done)
                yield
                if j == 0:
                    v_tile[b, l, j] = (yield from va[b].get())
                    k_tile[b, l, j] = (yield from kT[b].get())
                vai, vab, vafree = yield from need(v_tile, (b, l, j))
                va_done = DV(vec.tensor_copy, vab[P - BLK:, :, 0:DH1], vb[0:BLK, :, 0:DH1],
                             after=[v_done, b_zero, win_zero, *vafree], sem="b_va")
                if j < TPB - 1:
                    n_, nb_, nfree = yield from va[b].get()
                    nd = DV(vec.tensor_copy, nb_[0:WIN, :, 0:DH1], vb[P - WIN:, :, 0:DH1],
                            after=[v_done, b_zero, win_zero, *nfree], sem="b_va")
                    v_tile[b, l, j + 1] = (n_, nb_, [*nfree, nd])
                rv = r[:, :, :].rearrange("p a (h d) -> p (a h) d", h=H1)
                d = DV(vec.tensor_tensor, rv, rv, sst[:, :].unsqueeze(2).to_broadcast([P, 2 * H1, DH1]),
                       ALU.mult, after=[d, g], sem="b_scale")
                ss.give(si, d)
                yield
                ki, kb, kfree = yield from need(k_tile, (b, l, j))
                qi, qb, qfree = yield from qT.get()
                if j < TPB - 1:
                    nki, nkb, nkfree = yield from kT[b].get()
                for part in range(2):
                    i, bank, free = yield from banks.get()
                    for c in range(INNER // P):
                        m = PE(tr, bank[:, c * P:(c + 1) * P], r[:, part, c * P:(c + 1) * P], ident[:, :],
                               after=[d, *free], sem="b_qkT")
                    turned = bank[:, :].rearrange("p (c t) -> p c t", t=P)
                    e = AC(act.copy, (qb[:, :, :], kb[:, :, WIN:])[part], turned,
                           after=[m, b_zero, *(qfree, kfree)[part]], sem="b_qkTc")
                    if part and j < TPB - 1:
                        e2 = AC(act.copy, nkb[:, :, 0:WIN], turned[:, :, P - WIN:], after=[b_zero, *nkfree],
                                sem="b_qkTc")
                        k_tile[b, l, j + 1] = (nki, nkb, [*nkfree, e2])
                        banks.give(i, e2)
                    else:
                        banks.give(i, e)
                    yield
                rq.give(ri, m)
                held = []
                for hp in range(2):
                    held.append((yield from banks.get()))
                xi, mxb, mfree = yield from mxl.get()
                for i, bank, free in held:
                    PE(mm, bank[:, :], identb[:, :],
                       local_mask[:, 0 if j else 1, :, :].rearrange("p a k -> p (a k)"), start=True, stop=False,
                       after=[ld_const, *free])
                for p in range(H1 // 2):
                    for hp in range(2):
                        rows = slice(hp * DH1, (hp + 1) * DH1)
                        for n in range(P // BLK):
                            m = PE(mm, held[hp][1][n * BLK:(n + 1) * BLK, p * SPAN:(p + 1) * SPAN],
                                   qb[rows, p, n * BLK:(n + 1) * BLK], kb[rows, p, n * BLK:n * BLK + SPAN],
                                   start=False, stop=(p == H1 // 2 - 1), after=[e, *kfree], sem="b_s")
                qT.give(qi, m)
                kT[b].give(ki, m)
                yield
                for hp in range(2):
                    d = DV(vec.reduce_max, mxb[:, hp * 4:(hp + 1) * 4],
                           held[hp][1][:, :].rearrange("p (a k) -> p a k", k=SPAN), AXX, after=[m, *mfree],
                           sem="b_max")
                d = DV(vec.tensor_scalar, mxb[:, :], mxb[:, :], -QK_SCALE, None, ALU.mult, after=[d],
                       sem="b_nmax")
                yield
                pbs = []
                for hp in range(2):
                    pi, pb, pfree = yield from pp.get()
                    i, bank, _ = held[hp]
                    for p in range(H1 // 2):
                        x_ = AC(act.activation, pb[:, p, :], bank[:, p * SPAN:(p + 1) * SPAN], ACTF.Exp,
                                bias=mxb[:, 4 * hp + p:4 * hp + p + 1], scale=QK_SCALE, after=[d, *pfree],
                                sem="b_exp")
                    banks.give(i, x_)
                    pbs.append((pi, pb, x_))
                    yield
                mxl.give(xi, x_)
                pts = []
                for hp, (pi, pb, x_) in enumerate(pbs):
                    i, bank, free = yield from banks.get()
                    for p in range(H1 // 2):
                        m = PE(tr, bank[:, p * P:(p + 1) * P], pb[:, p, :], ident[:, :], after=[x_, *free],
                               sem="b_pT")
                    pp.give(pi, m)
                    yield
                    ti, pt, tfree = yield from pT.get()
                    dst = pt[:, :, :].rearrange("p a q -> p (a q)")
                    if hp:
                        c = AC(act.copy, dst, bank[:, :], after=[m, *tfree], sem="b_pTa")
                    else:
                        c = DV(vec.tensor_copy, dst, bank[:, :], after=[m, *tfree], sem="b_pTd")
                    banks.give(i, c)
                    pts.append((ti, pt, c))
                    yield
                rdi, rd, rdfree = yield from rdl.get()
                oi, o, ofree = yield from oo.get()
                for hp, (ti, pt, c) in enumerate(pts):
                    i, bank, free = yield from banks.get()
                    for p in range(H1 // 2):
                        for n, v in enumerate((vab, vb)):
                            m = PE(mm, bank[n * BLK:(n + 1) * BLK, p * (DH1 + 1):(p + 1) * (DH1 + 1)],
                                   pt[:, p, n * BLK:(n + 1) * BLK], v[:, 2 * p + hp, :], start=True, stop=True,
                                   after=[c, v_done, va_done, *vafree, *free], sem="b_o")
                    pT.give(ti, m)
                    yield
                    bv = bank[:, 0:4 * (DH1 + 1)].rearrange("p (h d) -> p h d", h=4)
                    d = DV(vec.reciprocal, rd[:, 4 * hp:4 * hp + 4], bv[:, :, DH1], after=[m, *rdfree], sem="b_rden")
                    d = DV(vec.tensor_tensor, o[:, :].rearrange("p (a b d) -> p a b d", b=2, d=DH1)[:, :, hp, :],
                           bv[:, :, 0:DH1], rd[:, 4 * hp:4 * hp + 4].unsqueeze(2).to_broadcast([P, 4, DH1]), ALU.mult,
                           after=[d, *ofree], sem="b_on")
                    banks.give(i, d)
                    yield
                rdl.give(rdi, d)
                vv.give(vi, m)
                va[b].give(vai, m)
                i, bank, free = yield from banks.get()
                for c in range(INNER // P):
                    m = PE(tr, bank[:, c * P:(c + 1) * P], o[:, c * P:(c + 1) * P], ident[:, :], after=[d, *free],
                           sem="b_oTT")
                oo.give(oi, m)
                ci, ot, cfree = yield from ooT.get()
                e = AC(act.copy, ot[:, :, :].rearrange("p c t -> p (c t)"), bank[:, :], after=[m, *cfree], sem="b_oT")
                banks.give(i, e)
                yield
                i, bank, free = yield from banks.get()
                for c in range(INNER // P):
                    m = PE(mm, bank[:, 0:D], ot[:, c, :], wo[l][:, c, :], start=(c == 0), stop=(c == INNER // P - 1),
                           after=[e, *free], sem="b_wo" if c == INNER // P - 1 else None)
                ooT.give(ci, m)
                x_ready[t] = DV(vec.tensor_tensor, x[:, t, :], bank[:, 0:D], x[:, t, :], ALU.add,
                                after=[m, kept[t]], sem="b_res")
                banks.give(i, x_ready[t])
                yield
                if l:
                    yield from need(hTf_free, (b, l - 1, nxt))
                if j:
                    yield from need(hTf_done, (b, l, j - 1))
                h = yield from shifted(t, hTf[b], [hTf_free[b, l - 1, nxt]] if l else [])
                hTf_done[b, l, j] = h
                xb = GP(gps.tensor_tensor, x[:, t, :], x[:, t, :], b2b[l][:, :], ALU.add,
                        after=[("pe_xT", sems["pe_xT"].count), x_ready[t], ld_b2b[l]], sem="f_b2")
                x_ready[t] = xb
                i, bank, free = yield from banks.get()
                m = PE(tr, bank[:, 0:P], hTf[b][:, j * P:(j + 1) * P], ident[:, :], after=[h, *free], sem="f_hh")
                hTf_free[b, l, j] = m
                si, st, sfree = yield from stat.get()
                _, r_ = deviation(bank[:, 0:P], [m, *sfree], st)
                yield
                ni, nb_, nfree = yield from nn.get()
                d = DV(vec.tensor_scalar, nb_[:, :], bank[:, 0:P], st[:, 6:7], st[:, 8:9], ALU.subtract, ALU.mult,
                       after=[r_, *nfree], sem="f_n")
                banks.give(i, d)
                stat.give(si, d)
                yield
                i, bank, free = yield from banks.get()
                m = PE(tr, bank[:, 0:P], nb_[:, :], ident[:, :], after=[d, *free], sem="f_nTT")
                nn.give(ni, m)
                ni, nt, nfree = yield from nT.get()
                n_ = DV(vec.tensor_scalar, nt[:, :], bank[:, 0:P], ln[l][:, 0:1], ln[l][:, 1:2], ALU.mult, ALU.add,
                        after=[m, *nfree], sem="f_nT")
                banks.give(i, n_)
                yield
                gi, gbank, free = yield from banks.get()
                for c in range(3):
                    n = HIDC[c]
                    lo = HID + c * HCH
                    m = PE(mm, gbank[0:n, c * P:(c + 1) * P], w1[l][:, lo:lo + n], nt[:, :], start=True, stop=True,
                           after=[n_, *free], sem="f_w1")
                ai, abank, free = yield from banks.get()
                for c in range(3):
                    n = HIDC[c]
                    lo = c * HCH
                    ma = PE(mm, abank[0:n, c * P:(c + 1) * P], w1[l][:, lo:lo + n], nt[:, :], start=True, stop=True,
                            after=free, sem="f_w1")
                nT.give(ni, ma)
                ggi, gb, gfree = yield from gl.get()
                for c in range(3):
                    n = HIDC[c]
                    a = AC(act.activation, gb[0:n, c, :], gbank[0:n, c * P:(c + 1) * P], ACTF.Gelu,
                           bias=b1[l][0:n, 3 + c:4 + c], scale=1.0, after=[m, *gfree], sem="f_gelu")
                banks.give(gi, a)
                yield
                ui, u, ufree = yield from uT.get()
                for c in range(3):
                    n = HIDC[c]
                    d = DV(vec.scalar_tensor_tensor, u[0:n, c, :], abank[0:n, c * P:(c + 1) * P], b1[l][0:n, c:c + 1],
                           gb[0:n, c, :], ALU.add, ALU.mult, after=[ma, a, *ufree], sem="f_u")
                banks.give(ai, d)
                gl.give(ggi, d)
                yield
                i, bank, free = yield from banks.get()
                for c in range(3):
                    n = HIDC[c]
                    m = PE(mm, bank[:, 0:D], u[0:n, c, :], w2[l][0:n, c, :], start=(c == 0), stop=(c == 2),
                           after=[d, *free], sem="f_w2" if c == 2 else None)
                uT.give(ui, m)
                x_ready[t] = DV(vec.tensor_tensor, x[:, t, :], bank[:, 0:D], x[:, t, :], ALU.add,
                                after=[m, xb], sem="f_res")
                banks.give(i, x_ready[t])
                yield
                if l == DEPTH - 1:
                    d = DV(vec.tensor_tensor, x[:, t, :], x[:, t, :], xin[:, t, :], ALU.add, after=[x_ready[t], kept[t]],
                           sem="b_add")
                    yield from layer_norm(t, d)
                tile_done[l, t] = True

            interleave([([outputs(NB - 1, j) for j in range(TPB)], 3)] +
                       [([local_layer(b, l, j) for l in range(DEPTH) for j in range(TPB)], WIDTH)
                        for b in range(NB)] + [([load_causal()], 1)])

        local_weights.close()

        region = ExitStack()
        with region:
            fence(done_all())
            wo1 = rb("c_wo", [P, NKV, D])
            for j in range(NKV):
                ld_wo1 = load(wo1[:, j, :], T["Wo1T"][j * P:(j + 1) * P, :], "ld_c_wo")
            ld_c, ld_rope = causal_ready["w"], causal_ready["rope"]
            rope_tab = rot[0][:, :, :, :].rearrange("p (a c) t d -> p a (c t d)", a=2)
            rope_tab = rope_tab.rearrange("p a (t d) -> p a t d", d=HS)
            xTc = Ring([rb(f"c_xT{i}", [P, P]) for i in range(2)])
            r1 = Ring([rb(f"c_r1{i}", [P, 3, HS]) for i in range(2)])
            r2 = Ring([rb(f"c_r2{i}", [P, 3, HS]) for i in range(2)])
            qkT = [rb(f"c_qkT{b}", [P, 3, SEQ]) for b in range(NB)]
            vc = [rb(f"c_v{b}", [P, TPB, HS + 1]) for b in range(NB)]
            pc = Ring([rb(f"c_p{i}", [P, SEQ]) for i in range(3)])
            pcT = Ring([rb(f"c_pT{i}", [P, SEQ]) for i in range(3)])
            mc = Ring([rb(f"c_m{i}", [P, 4]) for i in range(4)])
            oc = Ring([rb(f"c_o{i}", [P, NKV, HS]) for i in range(2)])
            ocT = Ring([rb(f"c_oT{i}", [P, NKV, P]) for i in range(2)])
            for b in range(NB):
                c_one = GP(gps.memset, vc[b][:, :, HS:HS + 1], 1.0, sem="c_one")
            qk_done, vc_done, res = {}, {}, {}

            def rope(b, j):
                t = b * TPB + j
                xi, xt, xfree = yield from xTc.get()
                e = yield from transposed(t, xt[:, :], xfree, "c_xT")
                yield
                i, bank, free = yield from banks.get()
                m = PE(mm, bank[:, :], xt[:, :], w0[:, :, :].rearrange("p a k -> p (a k)"), start=True, stop=True,
                       after=[e, ld_c, *free], sem="c_qkv")
                xTc.give(xi, m)
                v = bank[:, 0:3 * HS].rearrange("p (a k) -> p a k", a=3)
                vc_done[t] = AC(act.copy, vc[b][:, j, 0:HS], bank[:, 3 * HS:], after=[m, c_one], sem="c_v")
                i1, a1, f1 = yield from r1.get()
                i2, a2, f2 = yield from r2.get()
                d = DV(vec.tensor_tensor, a1[:, :, :], v, rope_tab[:, 0, j, :].unsqueeze(1).to_broadcast([P, 3, HS]),
                       ALU.mult, after=[m, vc_done[t], ld_rope, *f1], sem="c_rot")
                for k in range(2):
                    d = DV(vec.tensor_tensor, a2[:, :, k::2], v[:, :, 1 - k::2],
                           rope_tab[:, 1, j, k::2].unsqueeze(1).to_broadcast([P, 3, HS // 2]), ALU.mult,
                           after=f2, sem="c_rot")
                banks.give(i, vc_done[t], d)
                g = GP(gps.tensor_tensor, a1[:, :, :], a1[:, :, :], a2[:, :, :], ALU.add, after=[d], sem="c_rotsum")
                r2.give(i2, g)
                yield
                i, bank, free = yield from banks.get()
                for a in range(3):
                    m = PE(tr, bank[:, a * P:(a + 1) * P], a1[:, a, :], ident[:, :], after=[g, *free], sem="c_rT")
                r1.give(i1, m)
                qk_done[t] = AC(act.copy, qkT[b][:, :, j * P:(j + 1) * P],
                                bank[:, 0:3 * P].rearrange("p (a t) -> p a t", a=3), after=[m], sem="c_qkT")
                banks.give(i, qk_done[t])
                yield

            def causal(b, j):
                t = b * TPB + j
                yield from need(qk_done, t)
                oi, o, ofree = yield from oc.get()
                nk = j + 1
                halves = [(lo, min(lo + 4, nk)) for lo in range(0, nk, 4)]
                for h in range(NKV):
                    mi, mb, mfree = yield from mc.get()
                    sbk = []
                    for n, (lo, hi) in enumerate(halves):
                        i, bank, free = yield from banks.get()
                        last = hi == nk
                        w = (hi - lo) * P
                        m = PE(mm, bank[:, 0:w], qkT[b][:, h, j * P:(j + 1) * P], qkT[b][:, 2, lo * P:hi * P],
                               start=True, stop=not last, after=[qk_done[t], *free], sem="c_s")
                        if last:
                            m = PE(mm, bank[:, w - P:w], identb[:, :], causal_mask[:, :], start=False, stop=True,
                                   after=[ld_const], sem="c_s")
                        d = DV(vec.reduce_max, mb[:, n:n + 1], bank[:, 0:w], AXX, after=[m, *mfree], sem="c_max")
                        sbk.append((i, bank, lo, w))
                    if len(halves) == 2:
                        d = DV(vec.tensor_tensor, mb[:, 0:1], mb[:, 0:1], mb[:, 1:2], ALU.max, after=[d], sem="c_max2")
                    d = DV(vec.tensor_scalar, mb[:, 2:3], mb[:, 0:1], -float(HS) ** -0.5, None, ALU.mult, after=[d],
                           sem="c_nmax")
                    pi, pb, pfree = yield from pc.get()
                    for i, bank, lo, w in sbk:
                        e = AC(act.activation, pb[:, lo * P:lo * P + w], bank[:, 0:w], ACTF.Exp, bias=mb[:, 2:3],
                               scale=float(HS) ** -0.5, after=[d, *pfree], sem="c_exp")
                        banks.give(i, e)
                    mc.give(mi, e)
                    yield
                    ti, pt, tfree = yield from pcT.get()
                    for n, (lo, hi) in enumerate(halves):
                        i, bank, free = yield from banks.get()
                        for k in range(lo, hi):
                            m = PE(tr, bank[:, (k - lo) * P:(k - lo + 1) * P], pb[:, k * P:(k + 1) * P], ident[:, :],
                                   after=[e, *free], sem="c_pTT")
                        c = DV(vec.tensor_copy, pt[:, lo * P:hi * P], bank[:, 0:(hi - lo) * P], after=[m, *tfree],
                               sem="c_pT")
                        banks.give(i, c)
                        yield
                    pc.give(pi, m)
                    i, bank, free = yield from banks.get()
                    for k in range(nk):
                        m = PE(mm, bank[:, 0:HS + 1], pt[:, k * P:(k + 1) * P], vc[b][:, k, :], start=(k == 0),
                               stop=(k == nk - 1), after=[c, vc_done[b * TPB + k], *free], sem="c_o")
                    pcT.give(ti, m)
                    mi, mb, mfree = yield from mc.get()
                    d = DV(vec.reciprocal, mb[:, 3:4], bank[:, HS:HS + 1], after=[m, *mfree], sem="c_rden")
                    d = DV(vec.tensor_scalar, o[:, h, :], bank[:, 0:HS], mb[:, 3:4], None, ALU.mult,
                           after=[d, *ofree], sem="c_on")
                    mc.give(mi, d)
                    banks.give(i, d)
                    yield
                i, bank, free = yield from banks.get()
                for h in range(NKV):
                    m = PE(tr, bank[:, h * P:(h + 1) * P], o[:, h, :], ident[:, :], after=[d, *free], sem="c_oTT")
                oc.give(oi, m)
                ci, ot, cfree = yield from ocT.get()
                e = AC(act.copy, ot[:, :, :], bank[:, 0:NKV * P].rearrange("p (a t) -> p a t", a=NKV),
                       after=[m, *cfree], sem="c_oT")
                yield
                for h in range(NKV):
                    m = PE(mm, bank[:, 3 * P:4 * P], ot[:, h, :], wo1[:, h, :], start=(h == 0), stop=(h == NKV - 1),
                           after=[e, ld_wo1], sem="c_wo")
                ocT.give(ci, m)
                res[t] = DV(vec.tensor_tensor, x[:, t, :], bank[:, 3 * P:4 * P], x[:, t, :], ALU.add,
                            after=[m, x_ready[t]], sem="c_res")
                banks.give(i, res[t])
                yield
                yield from layer_norm(t, res[t])
                tile_done[DEPTH, t] = True
                yield from logits(t)

            fc_in = Ring([rb(f"d_fc_in{i}", [P, FF]) for i in range(3)])
            fc_hi, fc_lo = rb("d_fc_hi", [P, NE, FF], F32R), rb("d_fc_lo", [P, NE, FF], F32R)
            x_hi, x_lo = rb("d_x_hi", [P, NT, P], F32R), rb("d_x_lo", [P, NT, P], F32R)
            pj = rb("d_pj", [P, NE, FCH, D])
            gate_w = rb("d_gate", [P, NE])
            ld_g = load(gate_w[:, :], T["gate_w"], "ld_gate")
            for e in range(NE):
                ld_pj = load(pj[:, e, :, :], T["proj_w"][e].rearrange("(f p) d -> p f d", p=P), "ld_pj")
            fc_done = {}

            def expert_weights(e):
                fi, fw, ffree = yield from fc_in.get()
                r = SP(sync.dma_start, fw[:, :], T["fc_w"][e], after=ffree, sem=f"ld_fc{fi}", by=16)
                yield
                h = AC(act.copy, fc_hi[:, e, :], fw[:, :], after=[r], sem="d_fc_hi")
                fc_done[e] = GP(gps.tensor_tensor, fc_lo[:, e, :], fw[:, :], fc_hi[:, e, :].bitcast(F32),
                                ALU.subtract, after=[h], sem="d_fc_lo")
                fc_in.give(fi, fc_done[e])
                yield
            xTd = rb("d_xT", [P, NT, P])
            gate = rb("d_gates", [P, NT, NE])
            g1 = rb("d_g1", [P, NT, 1])
            cmps = [[rb(f"d_cmp{b}{i}", [P, TPB, NE, NE]) for i in range(2)] for b in range(NB)]
            wsel = rb("d_w", [P, NT, NE])
            hid = Ring([rb(f"d_h{i}", [P, FCH, CHUNK]) for i in range(2)])
            xT_done, split_done, lg_done, acc = {}, {}, {}, {}

            def logits(t):
                xT_done[t] = yield from transposed(t, xTd[:, t, :], [], "d_xT")
                yield
                h = AC(act.copy, x_hi[:, t, :], xTd[:, t, :], after=[xT_done[t]], sem="d_x_hi")
                split_done[t] = DV(vec.tensor_tensor, x_lo[:, t, :], xTd[:, t, :], x_hi[:, t, :].bitcast(F32),
                                   ALU.subtract, after=[h], sem="d_x_lo")
                i, bank, free = yield from banks.get()
                m = PE(mm, bank[:, 0:NE], xTd[:, t, :], gate_w[:, :], start=True, stop=True,
                       after=[xT_done[t], ld_g, *free], sem="d_logit")
                lg_done[t] = DV(vec.tensor_copy, gate[:, t, :], bank[:, 0:NE], after=[m], sem="d_lg")
                banks.give(i, lg_done[t])
                yield

            def gating(b):
                for t in range(b * TPB, (b + 1) * TPB):
                    yield from need(lg_done, t)
                ts = slice(b * TPB, (b + 1) * TPB)
                gt, g, w = gate[:, ts, :], g1[:, ts, :], wsel[:, ts, :]
                wide = [P, TPB, NE]
                d = DV(vec.reduce_max, g[:, :, 0], gt, AXX, after=[lg_done[t] for t in range(b * TPB, (b + 1) * TPB)],
                       sem="d_gate")
                d = DV(vec.tensor_tensor, gt, gt, g.to_broadcast(wide), ALU.subtract, after=[d], sem="d_gate")
                a = AC(act.activation, gt, gt, ACTF.Exp, after=[d], sem="d_gexp")
                yield
                d = DV(vec.reduce_sum, g[:, :, 0], gt, AXX, after=[a], sem="d_gate")
                d = DV(vec.reciprocal, g, g, after=[d], sem="d_gate")
                d = DV(vec.tensor_tensor, gt, gt, g.to_broadcast(wide), ALU.mult, after=[d], sem="d_gate")
                cube = [P, TPB, NE, NE]
                c1, c2 = cmps[b]
                mine, other = gt.unsqueeze(3).to_broadcast(cube), gt.unsqueeze(2).to_broadcast(cube)
                d = DV(vec.tensor_tensor, c1[:, :, :, :], other, mine, ALU.is_gt, after=[d], sem="d_rank")
                d = DV(vec.tensor_tensor, c2[:, :, :, :], other, mine, ALU.is_equal, after=[d], sem="d_rank")
                yield
                d = DV(vec.tensor_tensor, c2[:, :, :, :], c2[:, :, :, :],
                       lower[:, :, :].unsqueeze(1).to_broadcast(cube), ALU.mult, after=[d, ld_const], sem="d_rank")
                d = DV(vec.tensor_tensor, c1[:, :, :, :], c1[:, :, :, :], c2[:, :, :, :], ALU.add, after=[d],
                       sem="d_rank")
                yield
                d = DV(vec.reduce_sum, w, c1[:, :, :, :], AXX, after=[d], sem="d_rank")
                d = DV(vec.tensor_scalar, w, w, float(TOPK) - 0.5, None, ALU.is_lt, after=[d], sem="d_pick")
                d = DV(vec.tensor_tensor, w, w, gt, ALU.mult, after=[d], sem="d_pick")
                yield
                d = DV(vec.reduce_sum, g[:, :, 0], w, AXX, after=[d], sem="d_pick")
                d = DV(vec.reciprocal, g, g, after=[d], sem="d_pick")
                w_done[b] = DV(vec.tensor_tensor, w, w, g.to_broadcast(wide), ALU.mult, after=[d], sem="d_pick")
                yield

            w_done, added = {}, {}
            tpc = CHUNK // P

            def expert(e, n):
                yield from need(fc_done, e)
                for t in range(n * tpc, (n + 1) * tpc):
                    yield from need(split_done, t)
                hi_, hb, hfree = yield from hid.get()
                src_hi, src_lo = (s[:, n * tpc:(n + 1) * tpc, :].rearrange("p a t -> p (a t)") for s in (x_hi, x_lo))
                for f in range(FCH):
                    i, bank, free = yield from banks.get()
                    fs = slice(f * P, (f + 1) * P)
                    after = [fc_done[e], *[split_done[t] for t in range(n * tpc, (n + 1) * tpc)], *free]
                    PE(mm, bank[:, :], fc_lo[:, e, fs], src_hi, start=True, stop=False, after=after)
                    PE(mm, bank[:, :], fc_hi[:, e, fs], src_lo, start=False, stop=False)
                    m = PE(mm, bank[:, :], fc_hi[:, e, fs], src_hi, start=False, stop=True, sem="d_fc")
                    a = AC(act.activation, hb[:, f, :], bank[:, :], ACTF.Gelu, after=[m, *hfree], sem="d_gelu")
                    banks.give(i, a)
                    yield
                i, bank, free = yield from banks.get()
                for q in range(tpc):
                    for f in range(FCH):
                        m = PE(mm, bank[:, q * P:(q + 1) * P], hb[:, f, q * P:(q + 1) * P], pj[:, e, f, :],
                               start=(f == 0), stop=(f == FCH - 1), after=[a, ld_pj, *free], sem="d_pj")
                    yield
                hid.give(hi_, m)
                yield from need(w_done, n * tpc // TPB)
                if e:
                    yield from need(added, (e - 1, n))
                for q in range(tpc):
                    t = n * tpc + q
                    acc[t] = DV(vec.scalar_tensor_tensor, x[:, t, :], bank[:, q * P:(q + 1) * P], wsel[:, t, e:e + 1],
                                x[:, t, :], ALU.mult, ALU.add,
                                after=[m, w_done[t // TPB], acc.get(t, xT_done[t])], sem="d_acc")
                banks.give(i, acc[t])
                added[e, n] = True
                if e == NE - 1:
                    for q in range(tpc):
                        yield from layer_norm(n * tpc + q, acc[n * tpc + q])

            chunks = [range(b * TPB // tpc, (b + 1) * TPB // tpc) for b in range(NB)]
            tiles = [(b, j) for b in range(NB) for j in range(TPB)]
            interleave([([rope(b, j) for b, j in tiles], ROPE_WIDTH), ([causal(b, j) for b, j in tiles], CAUSAL_WIDTH)] +
                       [([expert_weights(e) for e in range(NE)], 1)] +
                       [([gating(b) for b in range(NB)], 1)] +
                       [([expert(e, n) for b in range(NB) for e in range(NE) for n in chunks[b]], 2)])
            stage_out()

        SP.wait(*done_all())
        block = ctx.enter_context(nc.Block())

        @block.sync
        def _(eng):
            SP.play(eng)

        @block.tensor
        def _(eng):
            PE.play(eng)

        @block.vector
        def _(eng):
            DV.play(eng)

        @block.scalar
        def _(eng):
            AC.play(eng)

        @block.gpsimd
        def _(eng):
            GP.play(eng)


_NAMES = {"x": "L0_attn_x", "Wq": "L0_attn_Wq", "Wk": "L0_attn_Wk", "Wv": "L0_attn_Wv", "Wout": "L0_attn_Wout",
          "wqkv": "L0_ffn_wqkv", "q_scale": "L0_ffn_q_scale", "k_scale": "L0_ffn_k_scale", "wo": "L0_ffn_wo",
          "ln_g": "L0_ffn_ln_g", "ln_b": "L0_ffn_ln_b", "w1": "L0_ffn_w1", "b1": "L0_ffn_b1", "w2": "L0_ffn_w2",
          "b2": "L0_ffn_b2", "gate_w": "L1_ffn_gate_w", "fc_w": "L1_ffn_fc_w", "proj_w": "L1_ffn_proj_w"}


def constants():
    import numpy as np
    bf16 = mybir.dt.np(BF16)
    f = np.float32
    c = {"c_ident": np.eye(P, dtype=f), "c_identb": np.eye(P).astype(bf16)}
    q, k = np.arange(P)[:, None], np.arange(SPAN)[None, :] + np.arange(P)[:, None] // BLK * BLK - WIN
    seen = (k <= q) & (k >= q - WIN)
    both = np.stack([np.where(seen, 0.0, LOCAL_NEG), np.where(seen & (k >= 0), 0.0, LOCAL_NEG)], 1)
    c["c_local"] = np.repeat(both[:, :, None, :], H1 // 2, 2).astype(bf16)
    kk = np.arange(P)[None, :]
    c["c_causal"] = np.where(kk <= q, 0.0, NEG).astype(bf16)
    e = np.arange(NE)
    c["c_lower"] = np.broadcast_to((e[None, :] < e[:, None]).astype(f), (P, NE, NE)).copy()
    half = np.arange(0, DH1, 2, dtype=f)
    inv = (f(1.0) / f(10000.0) ** (half / f(DH1))).astype(f)
    t = np.arange(SEQ, dtype=f)
    fr = (t[:, None] * inv[None, :]).astype(f)
    fr = np.concatenate([fr, fr], -1)
    base = ((half + f(0.4 * DH1)) / f(1.4 * DH1)).astype(f)
    power = ((t - SEQ // 2) / f(WIN // 2)).astype(f)
    sc = (base[None, :] ** power[:, None]).astype(f)
    sc = np.concatenate([sc, sc], -1)
    cos, sin = np.cos(fr), np.sin(fr)
    sign = np.where(np.arange(DH1) < DH1 // 2, -1.0, 1.0).astype(f)
    tabs = np.stack([cos * sc, sin * sc * sign, cos / sc, sin / sc * sign])
    c["c_rot"] = np.ascontiguousarray(tabs.reshape(4, TPB, P, DH1).transpose(2, 0, 1, 3)).astype(f)
    pos = np.arange(0, HS, 2, dtype=f)
    theta = (f(10000.0) ** (f(-2.0) * pos / f(HS))).astype(f)
    an = (t[:, None] * theta[None, :]).astype(f)
    cs = np.repeat(np.cos(an), 2, 1)
    sn = np.stack([-np.sin(an), np.sin(an)], -1).reshape(SEQ, HS)
    c["c_rope"] = np.ascontiguousarray(np.stack([cs, sn]).reshape(2, TPB, P, HS).transpose(2, 0, 1, 3)).astype(f)
    return c


def lay_out(inputs):
    import numpy as np
    a = {name: np.ascontiguousarray(inputs[full]) for name, full in _NAMES.items()}
    a["Wq1T"] = np.ascontiguousarray(np.transpose(inputs["L1_attn_Wq"], (0, 2, 1)))
    for name, full in (("Wk1T", "L1_attn_Wk"), ("Wv1T", "L1_attn_Wv"), ("Wo1T", "L1_attn_Wo")):
        a[name] = np.ascontiguousarray(np.transpose(inputs[full]))
    return {**a, **constants()}


def kernel(**inputs):
    import numpy as np
    import concourse.bacc as bacc
    from concourse.bass_utils import run_bass_kernel_spmd as launch
    inputs = {k: np.asarray(v) for k, v in inputs.items()}
    arrays = {f"in_{k}": v for k, v in lay_out(inputs).items()}
    nc = bacc.Bacc("TRN2", target_bir_lowering=False, num_devices=1)
    T = {k[3:]: nc.dram_tensor(k, v.shape, mybir.dt.from_np(v.dtype), kind="ExternalInput").ap()
         for k, v in arrays.items()}
    T["out"] = nc.dram_tensor("out", (NB, SEQ, D), F32, kind="ExternalOutput").ap()
    program(nc, T)
    return launch(nc, [arrays], core_ids=[0]).results[0]["out"]
```
